# Optimizing a Trainium2 kernel written in Bass

```python
import numpy as np
import jax
import jax.numpy as jnp

def _softmax(x, axis=-1):
    return jax.nn.softmax(x, axis=axis)

def _gelu(x):
    return jax.nn.gelu(x, approximate=True)

def _silu(x):
    return jax.nn.silu(x)

def _sigmoid(x):
    return jax.nn.sigmoid(x)

def _layernorm(x, axis=-1, eps=1e-05):
    m = jnp.mean(x, axis=axis, keepdims=True)
    v = jnp.var(x, axis=axis, keepdims=True)
    return (x - m) / jnp.sqrt(v + eps)

def _scatter_add(tgt, idx, src, axis=0):
    return tgt.at[idx].add(src)

def _segment_sum(src, seg, n):
    return jax.ops.segment_sum(src, seg, n)
kernel_name = 'mk_seq_postln_d2_jaxref_r8_83b263'

def setup_inputs(seed: int=0):
    np.random.seed(seed)
    _w = jnp.asarray

    def _L0_attn_setup():
        import math
        import jax, jax.numpy as jnp
        import numpy as np
        N_HEADS = 16
        D_EMBED = 128
        key = jax.random.key(seed)
        ks = jax.random.split(key, 5)
        b, l, d = (2, 256, D_EMBED)
        return {'x': jax.random.normal(ks[0], (b, l, d), dtype=jnp.float32), 'w_in': jax.random.normal(ks[1], (3 * d, d), dtype=jnp.float32) * 0.02, 'b_in': jax.random.normal(ks[2], (3 * d,), dtype=jnp.float32) * 0.02, 'w_out': jax.random.normal(ks[3], (d, d), dtype=jnp.float32) * 0.02, 'b_out': jax.random.normal(ks[4], (d,), dtype=jnp.float32) * 0.02}
    _L0_attn_in = _L0_attn_setup()

    def _L0_ffn_setup():
        import jax, jax.numpy as jnp
        import numpy as np
        D = 128
        H = 16
        HD = D // H
        E = 32
        ES = 128
        K = 4
        B, S = (2, 128)
        ROPE_BASE = 10000.0

        def _layernorm(x, g, b):
            m = x.mean(-1, keepdims=True)
            v = ((x - m) ** 2).mean(-1, keepdims=True)
            return (x - m) * jax.lax.rsqrt(v + 1e-05) * g + b

        def _forward(src, wq, wk, wv, wp, wo, ln1_g, ln1_b, ln2_g, ln2_b, sel_w, keys, values):
            Bs, Ss, Ds = src.shape
            scale = 1.0 / jnp.sqrt(jnp.array(HD, dtype=src.dtype))
            x = _layernorm(src, ln1_g, ln1_b)
            q = (x @ wq).reshape(Bs, Ss, H, HD)
            k = (x @ wk).reshape(Bs, Ss, H, HD)
            v = (x @ wv).reshape(Bs, Ss, H, HD)
            pos = jnp.arange(Ss - 1, -Ss, -1, dtype=src.dtype)
            inv_freq = 1.0 / ROPE_BASE ** (jnp.arange(0, Ds, 2, dtype=src.dtype) / Ds)
            ang = pos[:, None] * inv_freq[None, :]
            pe = jnp.concatenate([jnp.sin(ang), jnp.cos(ang)], axis=-1)
            p = (pe @ wp).reshape(2 * Ss - 1, H, HD)
            ac = jnp.einsum('bihd,bjhd->bhij', q, k)
            bd_full = jnp.einsum('bihd,phd->bhip', q, p)
            rel = jnp.arange(Ss)[:, None] - jnp.arange(Ss)[None, :] + (Ss - 1)
            bd = bd_full[:, :, jnp.arange(Ss)[:, None], rel]
            att = jax.nn.softmax((ac + bd) * scale, axis=-1)
            attn_out = jnp.einsum('bhij,bjhd->bihd', att, v).reshape(Bs, Ss, Ds) @ wo
            src = src + attn_out
            x2 = _layernorm(src, ln2_g, ln2_b)
            sel = jax.nn.sigmoid(x2 @ sel_w)
            scores, idx = jax.lax.top_k(sel, K)
            gate = (jax.nn.one_hot(idx, E, dtype=sel.dtype) * scores[..., None]).sum(-2)
            h = jax.nn.relu(jnp.einsum('bsd,edh->bseh', x2, keys))
            moe_out = jnp.einsum('bseh,ehd,bse->bsd', h, values, gate)
            return src + moe_out
        key = jax.random.key(seed)
        ks = jax.random.split(key, 10)
        std_scale = np.sqrt(2.0 / 18)
        w_std = std_scale / np.sqrt(D)
        return {'src': jax.random.normal(ks[0], (B, S, D), jnp.float32), 'wq': jax.random.normal(ks[1], (D, H * HD), jnp.float32) * w_std, 'wk': jax.random.normal(ks[2], (D, H * HD), jnp.float32) * w_std, 'wv': jax.random.normal(ks[3], (D, H * HD), jnp.float32) * w_std, 'wp': jax.random.normal(ks[4], (D, H * HD), jnp.float32) * w_std, 'wo': jax.random.normal(ks[5], (H * HD, D), jnp.float32) * w_std, 'ln1_g': jnp.ones((D,), jnp.float32), 'ln1_b': jnp.zeros((D,), jnp.float32), 'ln2_g': jnp.ones((D,), jnp.float32), 'ln2_b': jnp.zeros((D,), jnp.float32), 'sel_w': jax.random.normal(ks[6], (D, E), jnp.float32) / np.sqrt(D), 'keys': jax.random.normal(ks[7], (E, D, ES), jnp.float32) * w_std, 'values': jax.random.normal(ks[8], (E, ES, D), jnp.float32) * (std_scale / np.sqrt(ES))}
    _L0_ffn_in = _L0_ffn_setup()

    def _L1_attn_setup():
        import jax, jax.numpy as jnp
        import numpy as np
        from jax import lax
        D_MODEL = 128
        D_STATE = 64
        EXPAND = 2
        HEADDIM = 64
        D_INNER = EXPAND * D_MODEL
        NH = D_INNER // HEADDIM
        N_ANG = D_STATE // 2
        A_FLOOR = 0.0001
        BATCH, SEQ = (2, 64)
        D_IN_PROJ = D_INNER + D_INNER + D_STATE + D_STATE + NH + NH + NH + N_ANG

        def _layernorm(x, g, b, eps=1e-05):
            m = x.mean(-1, keepdims=True)
            v = ((x - m) ** 2).mean(-1, keepdims=True)
            return (x - m) / jnp.sqrt(v + eps) * g + b

        def _rope_pairs(v, ang):
            ve, vo = (v[..., 0::2], v[..., 1::2])
            c, s = (jnp.cos(ang), jnp.sin(ang))
            re = ve * c - vo * s
            ro = ve * s + vo * c
            return jnp.stack([re, ro], axis=-1).reshape(v.shape)
        key = jax.random.key(seed)
        ks = jax.random.split(key, 9)
        u = jax.random.normal(ks[0], (BATCH, SEQ, D_MODEL), jnp.float32)
        W_in = jax.random.normal(ks[1], (D_MODEL, D_IN_PROJ), jnp.float32) * 0.02
        W_out = jax.random.normal(ks[2], (D_INNER, D_MODEL), jnp.float32) * 0.02
        dt_bias = jax.random.normal(ks[3], (NH,), jnp.float32) * 0.1
        D_param = jnp.ones((NH,), jnp.float32)
        Bn_g = 1.0 + 0.1 * jax.random.normal(ks[4], (D_STATE,), jnp.float32)
        Bn_b = 0.1 * jax.random.normal(ks[5], (D_STATE,), jnp.float32)
        Cn_g = 1.0 + 0.1 * jax.random.normal(ks[6], (D_STATE,), jnp.float32)
        Cn_b = 0.1 * jax.random.normal(ks[7], (D_STATE,), jnp.float32)
        return {'u': u, 'W_in': W_in, 'W_out': W_out, 'dt_bias': dt_bias, 'D_param': D_param, 'Bn_g': Bn_g, 'Bn_b': Bn_b, 'Cn_g': Cn_g, 'Cn_b': Cn_b}
    _L1_attn_in = _L1_attn_setup()

    def _L1_ffn_setup():
        import jax, jax.numpy as jnp
        import numpy as np
        DIM = 128
        DEPTH = 2
        HEADS = 8
        DIM_HEAD = 64
        WINDOW = 64
        INNER = HEADS * DIM_HEAD
        HID = int(DIM * 4 * 2 / 3)
        B, N = (2, 1024)
        QK_SCALE = 8.0

        def shift_token(t):
            t1, t2 = jnp.split(t, 2, axis=-1)
            t2 = jnp.pad(t2, ((0, 0), (1, 0), (0, 0)))[:, :-1]
            return jnp.concatenate([t1, t2], axis=-1)

        def l2norm(t):
            return t / jnp.clip(jnp.linalg.norm(t, axis=-1, keepdims=True), 1e-12)

        def rotate_half(x):
            x1, x2 = jnp.split(x, 2, axis=-1)
            return jnp.concatenate([-x2, x1], axis=-1)

        def rotary_xpos(q, k):
            n = q.shape[-2]
            half_idx = jnp.arange(0, DIM_HEAD, 2, dtype=jnp.float32)
            inv_freq = 1.0 / 10000.0 ** (half_idx / DIM_HEAD)
            t = jnp.arange(n, dtype=jnp.float32)
            freqs = t[:, None] * inv_freq[None, :]
            freqs = jnp.concatenate([freqs, freqs], axis=-1)
            base = (half_idx + 0.4 * DIM_HEAD) / (1.4 * DIM_HEAD)
            power = (t - n // 2) / float(WINDOW // 2)
            scale = base[None, :] ** power[:, None]
            scale = jnp.concatenate([scale, scale], axis=-1)
            cos, sin = (jnp.cos(freqs), jnp.sin(freqs))
            q = q * cos * scale + rotate_half(q) * sin * scale
            k = k * cos / scale + rotate_half(k) * sin / scale
            return (q, k)

        def local_attention(q, k, v):
            b, h, n, d = q.shape
            w = n // WINDOW
            bq = q.reshape(b, h, w, WINDOW, d) * QK_SCALE
            bk = k.reshape(b, h, w, WINDOW, d)
            bv = v.reshape(b, h, w, WINDOW, d)

            def look_around(t):
                p = jnp.pad(t, ((0, 0), (0, 0), (1, 0), (0, 0), (0, 0)))
                return jnp.concatenate([p[:, :, :w], p[:, :, 1:]], axis=3)
            bk, bv = (look_around(bk), look_around(bv))
            bt = jnp.arange(n).reshape(w, WINDOW)
            btp = jnp.pad(bt, ((1, 0), (0, 0)), constant_values=-1)
            btk = jnp.concatenate([btp[:w], btp[1:]], axis=1)
            sim = jnp.einsum('bhwid,bhwjd->bhwij', bq, bk)
            i = bt[:, :, None]
            j = btk[:, None, :]
            mask = (i < j) | (i > j + WINDOW) | (j == -1)
            sim = jnp.where(mask, -jnp.finfo(sim.dtype).max, sim)
            attn = jax.nn.softmax(sim, axis=-1)
            out = jnp.einsum('bhwij,bhwjd->bhwid', attn, bv)
            return out.reshape(b, h, n, d)

        def _layer(x, wqkv, qs, ksc, wo, lg, lb, w1, b1, w2, b2):
            b, n, _ = x.shape
            h = shift_token(x)
            qkv = h @ wqkv
            q, k, v = jnp.split(qkv, 3, axis=-1)
            to_heads = lambda t: t.reshape(b, n, HEADS, DIM_HEAD).transpose(0, 2, 1, 3)
            q, k, v = (to_heads(q), to_heads(k), to_heads(v))
            q = l2norm(q) * qs
            k = l2norm(k) * ksc
            q, k = rotary_xpos(q, k)
            o = local_attention(q, k, v)
            o = o.transpose(0, 2, 1, 3).reshape(b, n, INNER)
            x = x + o @ wo
            h = shift_token(x)
            mu = h.mean(-1, keepdims=True)
            var = h.var(-1, keepdims=True)
            h = (h - mu) / jnp.sqrt(var + 1e-05) * lg + lb
            h = h @ w1 + b1
            a, g = jnp.split(h, 2, axis=-1)
            h = a * jax.nn.gelu(g, approximate=False)
            x = x + h @ w2 + b2
            return x
        key = jax.random.key(seed)
        ks = jax.random.split(key, 6)
        return {'x': jax.random.normal(ks[0], (B, N, DIM), jnp.float32), 'wqkv': jax.random.normal(ks[1], (DEPTH, DIM, 3 * INNER), jnp.float32) * 0.02, 'q_scale': jnp.ones((DEPTH, DIM_HEAD), jnp.float32), 'k_scale': jnp.ones((DEPTH, DIM_HEAD), jnp.float32), 'wo': jax.random.normal(ks[2], (DEPTH, INNER, DIM), jnp.float32) * 0.02, 'ln_g': jnp.ones((DEPTH, DIM), jnp.float32), 'ln_b': jnp.zeros((DEPTH, DIM), jnp.float32), 'w1': jax.random.normal(ks[3], (DEPTH, DIM, 2 * HID), jnp.float32) * 0.02, 'b1': jnp.zeros((DEPTH, 2 * HID), jnp.float32), 'w2': jax.random.normal(ks[4], (DEPTH, HID, DIM), jnp.float32) * 0.02, 'b2': jnp.zeros((DEPTH, DIM), jnp.float32)}
    _L1_ffn_in = _L1_ffn_setup()
    _d = {'L0_attn_x': _L0_attn_in['x'], 'L0_attn_w_in': _L0_attn_in['w_in'], 'L0_attn_b_in': _L0_attn_in['b_in'], 'L0_attn_w_out': _L0_attn_in['w_out'], 'L0_attn_b_out': _L0_attn_in['b_out'], 'L0_ffn_wq': _L0_ffn_in['wq'], 'L0_ffn_wk': _L0_ffn_in['wk'], 'L0_ffn_wv': _L0_ffn_in['wv'], 'L0_ffn_wp': _L0_ffn_in['wp'], 'L0_ffn_wo': _L0_ffn_in['wo'], 'L0_ffn_ln1_g': _L0_ffn_in['ln1_g'], 'L0_ffn_ln1_b': _L0_ffn_in['ln1_b'], 'L0_ffn_ln2_g': _L0_ffn_in['ln2_g'], 'L0_ffn_ln2_b': _L0_ffn_in['ln2_b'], 'L0_ffn_sel_w': _L0_ffn_in['sel_w'], 'L0_ffn_keys': _L0_ffn_in['keys'], 'L0_ffn_values': _L0_ffn_in['values'], 'L1_attn_W_in': _L1_attn_in['W_in'], 'L1_attn_W_out': _L1_attn_in['W_out'], 'L1_attn_dt_bias': _L1_attn_in['dt_bias'], 'L1_attn_D_param': _L1_attn_in['D_param'], 'L1_attn_Bn_g': _L1_attn_in['Bn_g'], 'L1_attn_Bn_b': _L1_attn_in['Bn_b'], 'L1_attn_Cn_g': _L1_attn_in['Cn_g'], 'L1_attn_Cn_b': _L1_attn_in['Cn_b'], 'L1_ffn_wqkv': _L1_ffn_in['wqkv'], 'L1_ffn_q_scale': _L1_ffn_in['q_scale'], 'L1_ffn_k_scale': _L1_ffn_in['k_scale'], 'L1_ffn_wo': _L1_ffn_in['wo'], 'L1_ffn_ln_g': _L1_ffn_in['ln_g'], 'L1_ffn_ln_b': _L1_ffn_in['ln_b'], 'L1_ffn_w1': _L1_ffn_in['w1'], 'L1_ffn_b1': _L1_ffn_in['b1'], 'L1_ffn_w2': _L1_ffn_in['w2'], 'L1_ffn_b2': _L1_ffn_in['b2']}
    _x0 = _d['L0_attn_x']
    _d['L0_attn_x'] = jax.random.normal(jax.random.fold_in(jax.random.key(seed), 1), (8, 512, 128), dtype=_x0.dtype)
    del _x0
    return _d

def reference(L0_attn_x, L0_attn_w_in, L0_attn_b_in, L0_attn_w_out, L0_attn_b_out, L0_ffn_wq, L0_ffn_wk, L0_ffn_wv, L0_ffn_wp, L0_ffn_wo, L0_ffn_ln1_g, L0_ffn_ln1_b, L0_ffn_ln2_g, L0_ffn_ln2_b, L0_ffn_sel_w, L0_ffn_keys, L0_ffn_values, L1_attn_W_in, L1_attn_W_out, L1_attn_dt_bias, L1_attn_D_param, L1_attn_Bn_g, L1_attn_Bn_b, L1_attn_Cn_g, L1_attn_Cn_b, L1_ffn_wqkv, L1_ffn_q_scale, L1_ffn_k_scale, L1_ffn_wo, L1_ffn_ln_g, L1_ffn_ln_b, L1_ffn_w1, L1_ffn_b1, L1_ffn_w2, L1_ffn_b2):

    def _L0_attn_ref(x, w_in, b_in, w_out, b_out):
        import math
        import jax, jax.numpy as jnp
        import numpy as np
        N_HEADS = 16
        D_EMBED = 128
        b, l, d = x.shape
        h = N_HEADS
        scale = 1.0 / math.sqrt(d // h)
        x_proj = (x @ w_in.T + b_in).reshape(b, l, h, -1)
        q, k, v = jnp.split(x_proj, 3, axis=-1)
        att = jnp.einsum('blhd,bmhd->blmh', q, k) * scale
        att = jax.nn.softmax(att, axis=2)
        opt = jnp.einsum('blmh,blhd->blhd', att, v).reshape(b, l, d)
        return opt @ w_out.T + b_out

    def _L0_ffn_ref(src, wq, wk, wv, wp, wo, ln1_g, ln1_b, ln2_g, ln2_b, sel_w, keys, values):
        import jax, jax.numpy as jnp
        import numpy as np
        D = 128
        H = 16
        HD = D // H
        E = 32
        ES = 128
        K = 4
        B, S = (2, 128)
        ROPE_BASE = 10000.0

        def _layernorm(x, g, b):
            m = x.mean(-1, keepdims=True)
            v = ((x - m) ** 2).mean(-1, keepdims=True)
            return (x - m) * jax.lax.rsqrt(v + 1e-05) * g + b

        def _forward(src, wq, wk, wv, wp, wo, ln1_g, ln1_b, ln2_g, ln2_b, sel_w, keys, values):
            Bs, Ss, Ds = src.shape
            scale = 1.0 / jnp.sqrt(jnp.array(HD, dtype=src.dtype))
            x = _layernorm(src, ln1_g, ln1_b)
            q = (x @ wq).reshape(Bs, Ss, H, HD)
            k = (x @ wk).reshape(Bs, Ss, H, HD)
            v = (x @ wv).reshape(Bs, Ss, H, HD)
            pos = jnp.arange(Ss - 1, -Ss, -1, dtype=src.dtype)
            inv_freq = 1.0 / ROPE_BASE ** (jnp.arange(0, Ds, 2, dtype=src.dtype) / Ds)
            ang = pos[:, None] * inv_freq[None, :]
            pe = jnp.concatenate([jnp.sin(ang), jnp.cos(ang)], axis=-1)
            p = (pe @ wp).reshape(2 * Ss - 1, H, HD)
            ac = jnp.einsum('bihd,bjhd->bhij', q, k)
            bd_full = jnp.einsum('bihd,phd->bhip', q, p)
            rel = jnp.arange(Ss)[:, None] - jnp.arange(Ss)[None, :] + (Ss - 1)
            bd = bd_full[:, :, jnp.arange(Ss)[:, None], rel]
            att = jax.nn.softmax((ac + bd) * scale, axis=-1)
            attn_out = jnp.einsum('bhij,bjhd->bihd', att, v).reshape(Bs, Ss, Ds) @ wo
            src = src + attn_out
            x2 = _layernorm(src, ln2_g, ln2_b)
            sel = jax.nn.sigmoid(x2 @ sel_w)
            scores, idx = jax.lax.top_k(sel, K)
            gate = (jax.nn.one_hot(idx, E, dtype=sel.dtype) * scores[..., None]).sum(-2)
            h = jax.nn.relu(jnp.einsum('bsd,edh->bseh', x2, keys))
            moe_out = jnp.einsum('bseh,ehd,bse->bsd', h, values, gate)
            return src + moe_out
        return _forward(src, wq, wk, wv, wp, wo, ln1_g, ln1_b, ln2_g, ln2_b, sel_w, keys, values)

    def _L1_attn_ref(u, W_in, W_out, dt_bias, D_param, Bn_g, Bn_b, Cn_g, Cn_b):
        import jax, jax.numpy as jnp
        import numpy as np
        from jax import lax
        D_MODEL = 128
        D_STATE = 64
        EXPAND = 2
        HEADDIM = 64
        D_INNER = EXPAND * D_MODEL
        NH = D_INNER // HEADDIM
        N_ANG = D_STATE // 2
        A_FLOOR = 0.0001
        BATCH, SEQ = (2, 64)
        D_IN_PROJ = D_INNER + D_INNER + D_STATE + D_STATE + NH + NH + NH + N_ANG

        def _layernorm(x, g, b, eps=1e-05):
            m = x.mean(-1, keepdims=True)
            v = ((x - m) ** 2).mean(-1, keepdims=True)
            return (x - m) / jnp.sqrt(v + eps) * g + b

        def _rope_pairs(v, ang):
            ve, vo = (v[..., 0::2], v[..., 1::2])
            c, s = (jnp.cos(ang), jnp.sin(ang))
            re = ve * c - vo * s
            ro = ve * s + vo * c
            return jnp.stack([re, ro], axis=-1).reshape(v.shape)
        B_, L, _ = u.shape
        proj = u @ W_in
        idx = np.cumsum([D_INNER, D_INNER, D_STATE, D_STATE, NH, NH, NH])
        z, x, Bp, Cp, dd_dt, dd_A, trap_raw, angles = jnp.split(proj, idx, axis=-1)
        x4 = x.reshape(B_, L, NH, HEADDIM)
        z4 = z.reshape(B_, L, NH, HEADDIM)
        Bp = _layernorm(Bp, Bn_g, Bn_b)
        Cp = _layernorm(Cp, Cn_g, Cn_b)
        DT = jax.nn.softplus(dd_dt + dt_bias)
        DT_mean = DT.mean(axis=-1, keepdims=True)
        phase = jnp.cumsum(angles * DT_mean, axis=1)
        Bp_rot = _rope_pairs(Bp, phase)
        Cp_rot = _rope_pairs(Cp, phase)
        A = jnp.minimum(-jax.nn.softplus(dd_A), -A_FLOOR)
        decay = jnp.exp(A * DT)
        trap = jax.nn.sigmoid(trap_raw)
        Bx = jnp.einsum('blhp,bln->blhpn', x4, Bp_rot)
        Bx_prev = jnp.pad(Bx[:, :-1], ((0, 0), (1, 0), (0, 0), (0, 0), (0, 0)))
        te = trap[..., None, None]
        inp = (te * Bx + (1.0 - te) * Bx_prev) * DT[..., None, None]
        decay_t = jnp.moveaxis(decay, 1, 0)
        inp_t = jnp.moveaxis(inp, 1, 0)
        C_t = jnp.moveaxis(Cp_rot, 1, 0)

        def step(h, xs):
            d, ip, c = xs
            h = d[:, :, None, None] * h + ip
            y = jnp.einsum('bhpn,bn->bhp', h, c)
            return (h, y)
        h0 = jnp.zeros((B_, NH, HEADDIM, D_STATE), u.dtype)
        _, ys = lax.scan(step, h0, (decay_t, inp_t, C_t))
        y = jnp.moveaxis(ys, 0, 1)
        y = (y + D_param[None, None, :, None] * x4) * jax.nn.silu(z4)
        out = y.reshape(B_, L, D_INNER) @ W_out
        return out

    def _L1_ffn_ref(x, wqkv, q_scale, k_scale, wo, ln_g, ln_b, w1, b1, w2, b2):
        import jax, jax.numpy as jnp
        import numpy as np
        DIM = 128
        DEPTH = 2
        HEADS = 8
        DIM_HEAD = 64
        WINDOW = 64
        INNER = HEADS * DIM_HEAD
        HID = int(DIM * 4 * 2 / 3)
        B, N = (2, 1024)
        QK_SCALE = 8.0

        def shift_token(t):
            t1, t2 = jnp.split(t, 2, axis=-1)
            t2 = jnp.pad(t2, ((0, 0), (1, 0), (0, 0)))[:, :-1]
            return jnp.concatenate([t1, t2], axis=-1)

        def l2norm(t):
            return t / jnp.clip(jnp.linalg.norm(t, axis=-1, keepdims=True), 1e-12)

        def rotate_half(x):
            x1, x2 = jnp.split(x, 2, axis=-1)
            return jnp.concatenate([-x2, x1], axis=-1)

        def rotary_xpos(q, k):
            n = q.shape[-2]
            half_idx = jnp.arange(0, DIM_HEAD, 2, dtype=jnp.float32)
            inv_freq = 1.0 / 10000.0 ** (half_idx / DIM_HEAD)
            t = jnp.arange(n, dtype=jnp.float32)
            freqs = t[:, None] * inv_freq[None, :]
            freqs = jnp.concatenate([freqs, freqs], axis=-1)
            base = (half_idx + 0.4 * DIM_HEAD) / (1.4 * DIM_HEAD)
            power = (t - n // 2) / float(WINDOW // 2)
            scale = base[None, :] ** power[:, None]
            scale = jnp.concatenate([scale, scale], axis=-1)
            cos, sin = (jnp.cos(freqs), jnp.sin(freqs))
            q = q * cos * scale + rotate_half(q) * sin * scale
            k = k * cos / scale + rotate_half(k) * sin / scale
            return (q, k)

        def local_attention(q, k, v):
            b, h, n, d = q.shape
            w = n // WINDOW
            bq = q.reshape(b, h, w, WINDOW, d) * QK_SCALE
            bk = k.reshape(b, h, w, WINDOW, d)
            bv = v.reshape(b, h, w, WINDOW, d)

            def look_around(t):
                p = jnp.pad(t, ((0, 0), (0, 0), (1, 0), (0, 0), (0, 0)))
                return jnp.concatenate([p[:, :, :w], p[:, :, 1:]], axis=3)
            bk, bv = (look_around(bk), look_around(bv))
            bt = jnp.arange(n).reshape(w, WINDOW)
            btp = jnp.pad(bt, ((1, 0), (0, 0)), constant_values=-1)
            btk = jnp.concatenate([btp[:w], btp[1:]], axis=1)
            sim = jnp.einsum('bhwid,bhwjd->bhwij', bq, bk)
            i = bt[:, :, None]
            j = btk[:, None, :]
            mask = (i < j) | (i > j + WINDOW) | (j == -1)
            sim = jnp.where(mask, -jnp.finfo(sim.dtype).max, sim)
            attn = jax.nn.softmax(sim, axis=-1)
            out = jnp.einsum('bhwij,bhwjd->bhwid', attn, bv)
            return out.reshape(b, h, n, d)

        def _layer(x, wqkv, qs, ksc, wo, lg, lb, w1, b1, w2, b2):
            b, n, _ = x.shape
            h = shift_token(x)
            qkv = h @ wqkv
            q, k, v = jnp.split(qkv, 3, axis=-1)
            to_heads = lambda t: t.reshape(b, n, HEADS, DIM_HEAD).transpose(0, 2, 1, 3)
            q, k, v = (to_heads(q), to_heads(k), to_heads(v))
            q = l2norm(q) * qs
            k = l2norm(k) * ksc
            q, k = rotary_xpos(q, k)
            o = local_attention(q, k, v)
            o = o.transpose(0, 2, 1, 3).reshape(b, n, INNER)
            x = x + o @ wo
            h = shift_token(x)
            mu = h.mean(-1, keepdims=True)
            var = h.var(-1, keepdims=True)
            h = (h - mu) / jnp.sqrt(var + 1e-05) * lg + lb
            h = h @ w1 + b1
            a, g = jnp.split(h, 2, axis=-1)
            h = a * jax.nn.gelu(g, approximate=False)
            x = x + h @ w2 + b2
            return x
        for l in range(DEPTH):
            x = _layer(x, wqkv[l], q_scale[l], k_scale[l], wo[l], ln_g[l], ln_b[l], w1[l], b1[l], w2[l], b2[l])
        return x
    x = L0_attn_x
    x = _layernorm(x + _L0_attn_ref(x, L0_attn_w_in, L0_attn_b_in, L0_attn_w_out, L0_attn_b_out), axis=-1)
    x = _layernorm(x + _L0_ffn_ref(x, L0_ffn_wq, L0_ffn_wk, L0_ffn_wv, L0_ffn_wp, L0_ffn_wo, L0_ffn_ln1_g, L0_ffn_ln1_b, L0_ffn_ln2_g, L0_ffn_ln2_b, L0_ffn_sel_w, L0_ffn_keys, L0_ffn_values), axis=-1)
    x = _layernorm(x + _L1_attn_ref(x, L1_attn_W_in, L1_attn_W_out, L1_attn_dt_bias, L1_attn_D_param, L1_attn_Bn_g, L1_attn_Bn_b, L1_attn_Cn_g, L1_attn_Cn_b), axis=-1)
    x = _layernorm(x + _L1_ffn_ref(x, L1_ffn_wqkv, L1_ffn_q_scale, L1_ffn_k_scale, L1_ffn_wo, L1_ffn_ln_g, L1_ffn_ln_b, L1_ffn_w1, L1_ffn_b1, L1_ffn_w2, L1_ffn_b2), axis=-1)
    return x

_drawn_inputs = setup_inputs


def setup_inputs(seed=0):
    import zlib

    import numpy as np

    out = dict(_drawn_inputs(seed))
    spreads = {'L0_ffn_ln1_g': (1.0, 0.6),
     'L0_ffn_ln1_b': (0.0, 0.716),
     'L0_ffn_ln2_g': (1.0, 0.2),
     'L0_ffn_ln2_b': (0.0, 0.321),
     'L1_attn_D_param': (1.0, 0.6),
     'L1_ffn_q_scale': (1.0, 0.6),
     'L1_ffn_k_scale': (1.0, 0.6),
     'L1_ffn_ln_g': (1.0, 0.6),
     'L1_ffn_ln_b': (0.0, 0.8),
     'L1_ffn_b1': (0.0, 0.8),
     'L1_ffn_b2': (0.0, 0.532)}
    factors = {'L0_attn_b_in': 8.0,
     'L0_ffn_wq': 8.0,
     'L0_ffn_wk': 8.0,
     'L0_ffn_wv': 5.374,
     'L0_ffn_wp': 8.0,
     'L0_ffn_wo': 5.537,
     'L1_attn_dt_bias': 8.0,
     'L1_attn_Bn_g': 8.0,
     'L1_attn_Bn_b': 8.0,
     'L1_attn_Cn_g': 8.0,
     'L1_attn_Cn_b': 8.0,
     'L1_ffn_wqkv': 3.655,
     'L1_ffn_wo': 3.698,
     'L1_ffn_w1': 6.61,
     'L1_ffn_w2': 6.474}
    for name, (base, spread) in spreads.items():
        noise = np.random.default_rng([zlib.crc32(name.encode()), seed]).standard_normal(out[name].shape)
        drawn = base * np.exp(spread * noise) if base else spread * noise
        out[name] = jnp.asarray(drawn.astype(out[name].dtype))
    for name, factor in factors.items():
        out[name] = (out[name] * factor).astype(out[name].dtype)
    return out
```

```python
from contextlib import ExitStack

import numpy as np

import concourse.bass as bass
from concourse import mybir

ALU = mybir.AluOpType
ACT = mybir.ActivationFunctionType
F32 = mybir.dt.float32
BF16 = mybir.dt.bfloat16
LN_EXP = "natural_log_exp_and_others"
AX_X = mybir.AxisListType.X

P = 128
NB = 8
T = 512
NT = T // P
EPS = 1e-5


class NormSems:
    def __init__(self, sem, name):
        self.y = sem(f"{name}_y_ready")
        self.mean = sem(f"{name}_mean_ready")
        self.cent = sem(f"{name}_centred")
        self.sq = sem(f"{name}_squared")
        self.var = sem(f"{name}_var_ready")
        self.log = sem(f"{name}_log_var")
        self.rstd = sem(f"{name}_rstd")
        self.out = sem(f"{name}_out")


def norm_pe(nc, pe, s, n, ones, y, sq, mean_ps, var_ps):
    pe.wait_ge(s.y, n)
    nc.tensor.matmul(mean_ps, ones, y, start=True, stop=True).then_inc(s.mean, 1)
    pe.wait_ge(s.sq, n)
    nc.tensor.matmul(var_ps, ones, sq, start=True, stop=True).then_inc(s.var, 1)


def norm_act(nc, act, s, n, cent, sq, var_ps, eps):
    act.wait_ge(s.cent, n)
    nc.scalar.activation(sq, cent, ACT.Square).then_inc(s.sq, 1)
    act.wait_ge(s.var, n)
    nc.scalar.activation(var_ps, var_ps, ACT.Ln, bias=eps).then_inc(s.log, 1)
    act.wait_ge(s.log, n)
    nc.scalar.activation(var_ps, var_ps, ACT.Exp, scale=-0.5).then_inc(s.rstd, 1)


def norm_dve(nc, dve, s, n, y, cent, mean_ps, var_ps, out):
    dve.wait_ge(s.mean, n)
    nc.vector.tensor_tensor(cent, y, mean_ps, ALU.subtract).then_inc(s.cent, 1)
    dve.wait_ge(s.rstd, n)
    nc.vector.tensor_tensor(out, cent, var_ps, ALU.mult).then_inc(s.out, 1)


class Core:

    def __init__(self, nc, ctx):
        self.nc = nc
        self.ctx = ctx
        self.bank = [ctx.enter_context(nc.psum_tensor(f"bank{i}", [P, 512], F32)) for i in range(8)]
        self.resid = self.sb("resid", [P, NB, T])
        self.normed = self.sb("normed", [P, NB, T])
        self.outer = self.sb("outer", [P, NB, T])
        self.ones = self.sb("ones_mean", [P, P])
        self.eps = self.sb("eps", [P, 1])
        self.ident = self.sb("ident", [P, P])

    def sb(self, name, shape, dt=F32):
        return self.ctx.enter_context(self.nc.sbuf_tensor(name, shape, dt))


class Phase:

    def __init__(self, core, ctx):
        self.nc, self.ctx, self.sems = core.nc, ctx, []
        ctx.callback(self.clear)

    def sb(self, name, shape, dt=F32):
        return self.ctx.enter_context(self.nc.sbuf_tensor(name, shape, dt))

    def sem(self, name):
        s = self.nc.alloc_semaphore(name)
        self.sems.append(s)
        return s

    def clear(self):
        nums = sorted(s.num for s in self.sems)
        with self.nc.Block() as block:
            @block.sync
            def _(sp):
                at = 0
                while at < len(nums):
                    end = at
                    while end + 1 < len(nums) and nums[end + 1] == nums[end] + 1:
                        end += 1
                    sp.sem_clear(range(nums[at], nums[end] + 1))
                    at = end + 1
        for s in self.sems:
            self.nc.release_semaphore(s)


def phase_first_attention(c, d):
    nc = c.nc
    with ExitStack() as ctx:
        ph = Phase(c, ctx)
        wv = ph.sb("wv0", [P, P])
        wo = ph.sb("wo0", [P, P])
        vec = ph.sb("vec0", [P, 4])
        v_sb = ph.sb("v0_sb", [P, T])
        y = ph.sb("y0", [P, T])
        cent = ph.sb("cent0", [P, T])
        sq = ph.sb("sq0", [P, T])
        bias_v, bias_o, gain, shift = (vec[:, i:i + 1] for i in range(4))
        loaded = ph.sem("p1_loaded")
        ones_set = ph.sem("p1_ones_set")
        v_ready, v_biased, o_ready = ph.sem("p1_v"), ph.sem("p1_v_biased"), ph.sem("p1_o")
        na, nb_ = NormSems(ph.sem, "p1a"), NormSems(ph.sem, "p1b")
        affine = ph.sem("p1_affine")
        v_ps, o_ps, mean_ps, var_ps = (c.bank[i] for i in range(4))
        N_LOADS = 8

        with nc.Block() as block:
            @block.sync
            def _(sp):
                sp.dma_start(c.resid[:], d["x"].rearrange("b p t -> p b t")).then_inc(loaded, 16)
                sp.dma_start(wv[:], d["wv0"]).then_inc(loaded, 16)
                sp.dma_start(wo[:], d["wo0"]).then_inc(loaded, 16)
                sp.dma_start(vec[:, 0:1], d["bv0"]).then_inc(loaded, 16)
                sp.dma_start(vec[:, 1:2], d["bo0"]).then_inc(loaded, 16)
                sp.dma_start(vec[:, 2:3], d["ln1_g"]).then_inc(loaded, 16)
                sp.dma_start(vec[:, 3:4], d["ln1_b"]).then_inc(loaded, 16)
                sp.dma_start(c.ident[:], d["ident"]).then_inc(loaded, 16)

            @block.gpsimd
            def _(pool):
                nc.gpsimd.memset(c.ones[:], 1.0 / P).then_inc(ones_set, 1)
                nc.gpsimd.memset(c.eps[:], EPS).then_inc(ones_set, 1)

            @block.tensor
            def _(pe):
                pe.wait_ge(loaded, 16 * N_LOADS)
                pe.wait_ge(ones_set, 2)
                with pe.Fori(0, NB) as b:
                    nc.tensor.matmul(v_ps[:], wv[:], c.resid[:, b], start=True, stop=True).then_inc(v_ready, 1)
                    pe.wait_ge(v_biased, b + 1)
                    nc.tensor.matmul(o_ps[:], wo[:], v_sb[:], start=True, stop=True).then_inc(o_ready, 1)
                    norm_pe(nc, pe, na, b + 1, c.ones[:], y[:], sq[:], mean_ps[:], var_ps[:])
                    norm_pe(nc, pe, nb_, b + 1, c.ones[:], y[:], sq[:], mean_ps[:], var_ps[:])

            @block.scalar
            def _(act):
                nc.scalar.preload_act_table_set(LN_EXP)
                act.wait_ge(loaded, 16 * N_LOADS)
                act.wait_ge(ones_set, 2)
                with act.Fori(0, NB) as b:
                    act.wait_ge(v_ready, b + 1)
                    nc.scalar.activation(v_sb[:], v_ps[:], ACT.Identity, bias=bias_v).then_inc(v_biased, 1)
                    norm_act(nc, act, na, b + 1, cent[:], sq[:], var_ps[:], c.eps[:])
                    norm_act(nc, act, nb_, b + 1, cent[:], sq[:], var_ps[:], c.eps[:])

            @block.vector
            def _(dve):
                dve.wait_ge(loaded, 16 * N_LOADS)
                with dve.Fori(0, NB) as b:
                    dve.wait_ge(o_ready, b + 1)
                    nc.vector.scalar_tensor_tensor(out=y[:], in0=o_ps[:], scalar=bias_o, in1=c.resid[:, b],
                                                   op0=ALU.add, op1=ALU.add).then_inc(na.y, 1)
                    norm_dve(nc, dve, na, b + 1, y[:], cent[:], mean_ps[:], var_ps[:], y[:])
                    dve.wait_ge(na.out, b + 1)
                    nc.vector.tensor_scalar(c.outer[:, b], y[:], 1.0, None, ALU.mult)
                    nc.vector.tensor_scalar(c.resid[:, b], y[:], 1.0, None, ALU.mult).then_inc(nb_.y, 1)
                    norm_dve(nc, dve, nb_, b + 1, y[:], cent[:], mean_ps[:], var_ps[:], cent[:])
                    dve.wait_ge(nb_.out, b + 1)
                    nc.vector.tensor_scalar(c.normed[:, b], cent[:], gain, shift, ALU.mult, ALU.add).then_inc(affine, 1)


HG = 4
TURNS = NB * 4
W_Q, W_K, W_A, W_B = 0, P, 2 * P, 3 * P
W_V = 4 * P
W_COLS = 4 * P + 32


def phase_relative_attention(c, d):
    nc = c.nc
    SCALE = 8.0 ** -0.5
    with ExitStack() as ctx:
        ph = Phase(c, ctx)
        cos_q = ph.sb("cos_q", [P, T])
        sin_q = ph.sb("sin_q", [P, T])
        angle_k = ph.sb("angle_k", [P, T])
        angle_kb = ph.sb("angle_kb", [P, T], BF16)
        k_ones = ph.sb("k_ones", [P, 1])
        pick_sum = ph.sb("pick_sum", [P, P])
        w = [ph.sb(f"w_group{p}", [P, W_COLS]) for p in range(2)]
        wo = [ph.sb(f"wo_group{p}", [P, P]) for p in range(2)]
        xs = [ph.sb(f"x_staged{p}", [P, T]) for p in range(2)]
        q32 = [ph.sb(f"q32_{p}", [P, T]) for p in range(2)]
        k32 = [ph.sb(f"k32_{p}", [P, T]) for p in range(2)]
        qb = ph.sb("q_bf", [P, T], BF16)
        kb = ph.sb("k_bf", [P, T], BF16)
        vaug = [ph.sb(f"v_aug{p}", [P, NT, HG, 32]) for p in range(2)]
        half = ph.sb("turned_halves", [P, 2, 2, T])
        rot = [ph.sb(f"rot{p}", [P, HG, T]) for p in range(2)]
        rotb = ph.sb("rot_bf", [P, HG, T], BF16)
        maxima = ph.sb("maxima", [P, NT, P])
        probs = ph.sb("probs", [P, 2, NT, T])
        av = ph.sb("av", [P, T])
        rden = ph.sb("rden", [P, T])
        avn = ph.sb("av_normed", [P, T])

        score_ps = c.bank[0:2]
        av_ps, a_ps, b_ps, misc_ps = c.bank[2], c.bank[3], c.bank[4], c.bank[5]

        tables = ph.sem("p2_tables")
        set_up = ph.sem("p2_set_up")
        w_here = [ph.sem(f"p2_w_here{p}") for p in range(2)]
        wo_here = [ph.sem(f"p2_wo_here{p}") for p in range(2)]
        q_ready, k_ready, v_ready = ph.sem("p2_q"), ph.sem("p2_k"), ph.sem("p2_v")
        q_copied, k_copied, v_copied = ph.sem("p2_q_copied"), ph.sem("p2_k_copied"), ph.sem("p2_v_copied")
        turned = ph.sem("p2_turned")
        halves = ph.sem("p2_halves")
        rot_ready = ph.sem("p2_rot")
        rotb_ready = ph.sem("p2_rotb")
        rough = ph.sem("p2_rough")
        maxed = ph.sem("p2_maxed")
        max_turned = ph.sem("p2_max_turned")
        q_final = ph.sem("p2_q_final")
        scored = ph.sem("p2_scored")
        exped = ph.sem("p2_exped")
        av_ready, av_copied = ph.sem("p2_av"), ph.sem("p2_av_copied")
        den_ready, den_inv = ph.sem("p2_den"), ph.sem("p2_den_inv")
        avn_ready, o_ready = ph.sem("p2_avn"), ph.sem("p2_o")
        added = ph.sem("p2_added")
        N_TABLES = 7

        with nc.Block() as block:
            @block.sync
            def _(sp):
                sp.dma_start(cos_q[:], d["rel_cos"]).then_inc(tables, 16)
                sp.dma_start(sin_q[:], d["rel_sin"]).then_inc(tables, 16)
                sp.dma_start(angle_k[:], d["rel_angle"]).then_inc(tables, 16)
                sp.dma_start(k_ones[:], d["rel_k_ones"]).then_inc(tables, 16)
                sp.dma_start(pick_sum[:], d["rel_pick_sum"]).then_inc(tables, 16)
                sp.dma_start(vaug[0][:], d["rel_v_aug"]).then_inc(tables, 16)
                sp.dma_start(vaug[1][:], d["rel_v_aug"]).then_inc(tables, 16)

                def load_w(u, p):
                    sp.dma_start(w[p][:], d["rel_w"][u % 4]).then_inc(w_here[p], 16)
                    sp.dma_start(xs[p][:], c.normed[:, (u // 4) % NB]).then_inc(w_here[p], 16)

                def load_wo(t, p):
                    sp.dma_start(wo[p][:], d["rel_wo"][t % 4]).then_inc(wo_here[p], 16)

                for p in range(2):
                    load_w(p, p)
                    load_wo(p, p)
                with sp.Fori(0, TURNS // 2 - 1) as i:
                    for p in range(2):
                        t = 2 * i + p
                        sp.wait_ge(turned, HG * (t + 1))
                        load_w(t + 2, p)
                        sp.wait_ge(o_ready, t + 1)
                        load_wo(t + 2, p)
                sp.wait_ge(turned, HG * (TURNS - 1))
                load_w(TURNS, 0)

            @block.gpsimd
            def _(pool):
                nc.gpsimd.memset(maxima[:], 0.0).then_inc(set_up, 1)

                def prepare(u, p):
                    for r in range(HG):
                        pool.wait_ge(halves, HG * u + r + 1)
                        nc.gpsimd.tensor_tensor(rot[p][:, r], half[:, r % 2, 0], half[:, r % 2, 1],
                                                ALU.add).then_inc(rot_ready, 1)

                prepare(0, 0)
                with pool.Fori(0, TURNS // 2) as i:
                    prepare(2 * i + 1, 1)
                    prepare(2 * i + 2, 0)

            @block.tensor
            def _(pe):
                pe.wait_ge(tables, 16 * N_TABLES)
                pe.wait_ge(set_up, 2)

                def project(u, i, p):
                    pe.wait_ge(w_here[p], 32 * (i + 1))
                    wp = w[p]
                    nc.tensor.matmul(a_ps[:], wp[:, W_Q:W_Q + P], xs[p][:], start=True, stop=True).then_inc(q_ready, 1)
                    nc.tensor.matmul(b_ps[:], wp[:, W_K:W_K + P], xs[p][:], start=True, stop=True).then_inc(k_ready, 1)
                    if not isinstance(u, int):
                        pe.wait_ge(q_final, u)
                    for j in range(NT):
                        last = nc.tensor.matmul(misc_ps[:, 32 * j:32 * j + 32], xs[p][:, P * j:P * j + P],
                                                wp[:, W_V:W_V + 32], start=True, stop=True)
                    last.then_inc(v_ready, 1)

                def turn(u, p, r):
                    rows = slice(32 * r, 32 * r + 32)
                    if r == 0:
                        pe.wait_ge(q_copied, 2 * u + 2)
                        pe.wait_ge(k_copied, 2 * u + 2)
                    else:
                        pe.wait_ge(halves, HG * u + r)
                    nc.tensor.matmul(a_ps[:], w[p][rows, W_A:W_A + P], q32[p][rows, :], start=True, stop=True)
                    nc.tensor.matmul(b_ps[:], w[p][rows, W_B:W_B + P], q32[p][rows, :], start=True, stop=True).then_inc(turned, 1)

                def rough_scores(u, r, h):
                    rows = slice(32 * r, 32 * r + 32)
                    pe.wait_ge(rotb_ready, HG * u + r + 1)
                    pe.wait_ge(maxed, 8 * u + 2 * r + h + 1)
                    for k in range(2):
                        q_tile = slice(P * (2 * h + k), P * (2 * h + k) + P)
                        bank = c.bank[6 + k]
                        nc.tensor.matmul(bank[:], rotb[:, r, q_tile], angle_kb[:], start=True, stop=False)
                        last = nc.tensor.matmul(bank[:], qb[rows, q_tile], kb[rows, :], start=False, stop=True)
                    last.then_inc(rough, 1)

                def turn_maxima(u):
                    pe.wait_ge(maxed, 8 * u + 9)
                    pe.wait_ge(v_copied, u + 1)
                    for k in range(NT):
                        last = nc.tensor.transpose(misc_ps[:, P * k:P * k + P], maxima[:, k], c.ident[:])
                    last.then_inc(max_turned, 1)

                def scores(t, p, r):
                    rows = slice(32 * r, 32 * r + 32)
                    if r == 0:
                        pe.wait_ge(q_final, t + 1)
                        pe.wait_ge(rot_ready, HG * (t + 1))
                    for j in range(NT):
                        keys = slice(P * j, P * j + P)
                        pe.wait_ge(exped, 16 * t + 4 * r + j + 1)
                        bank = score_ps[j % 2]
                        nc.tensor.matmul(bank[:], angle_k[:, keys], rot[p][:, r], start=True, stop=False)
                        nc.tensor.matmul(bank[:], k32[p][rows, keys], q32[p][rows, :], start=False, stop=True).then_inc(scored, 1)

                def weigh_v(t, p, r):
                    if r == 0:
                        pe.wait_ge(added, t + 1)
                    pe.wait_ge(exped, 16 * t + 4 * r + 4 + 2)
                    for j in range(NT):
                        last = nc.tensor.matmul(av_ps[32 * r:32 * r + 32, :], vaug[p][:, j, r], probs[:, r % 2, j],
                                                start=(j == 0), stop=(j == NT - 1))
                    if r == HG - 1:
                        last.then_inc(av_ready, 1)

                def denominators(t):
                    pe.wait_ge(av_copied, t + 1)
                    nc.tensor.matmul(av_ps[:], pick_sum[:], av[:], start=True, stop=True).then_inc(den_ready, 1)

                def project_out(t, i, p):
                    pe.wait_ge(wo_here[p], 16 * (i + 1))
                    pe.wait_ge(avn_ready, t + 1)
                    nc.tensor.matmul(av_ps[:], wo[p][:], avn[:], start=True, stop=True).then_inc(o_ready, 1)

                def step(t, i, p, i_next):
                    u, n = t + 1, 1 - p
                    project(u, i_next, n)
                    scores(t, p, 0)
                    turn(u, n, 0)
                    scores(t, p, 1)
                    weigh_v(t, p, 0)
                    turn(u, n, 1)
                    rough_scores(u, 0, 0)
                    scores(t, p, 2)
                    rough_scores(u, 0, 1)
                    weigh_v(t, p, 1)
                    turn(u, n, 2)
                    rough_scores(u, 1, 0)
                    scores(t, p, 3)
                    rough_scores(u, 1, 1)
                    weigh_v(t, p, 2)
                    turn(u, n, 3)
                    rough_scores(u, 2, 0)
                    weigh_v(t, p, 3)
                    rough_scores(u, 2, 1)
                    denominators(t)
                    rough_scores(u, 3, 0)
                    project_out(t, i, p)
                    rough_scores(u, 3, 1)
                    turn_maxima(u)

                project(0, 0, 0)
                for r in range(HG):
                    turn(0, 0, r)
                    rough_scores(0, r, 0)
                    rough_scores(0, r, 1)
                turn_maxima(0)
                with pe.Fori(0, TURNS // 2) as i:
                    step(2 * i, i, 0, i)
                    step(2 * i + 1, i, 1, i + 1)

            @block.scalar
            def _(act):
                act.wait_ge(tables, 16 * N_TABLES)
                nc.scalar.activation(angle_kb[:], angle_k[:], ACT.Copy).then_inc(set_up, 1)
                act.sem_inc(exped, 2)

                def copy_qk(u, p):
                    act.wait_ge(q_ready, u + 1)
                    nc.scalar.activation(q32[p][:], a_ps[:], ACT.Copy).then_inc(q_copied, 1)
                    nc.scalar.activation(qb[:], a_ps[:], ACT.Copy).then_inc(q_copied, 1)
                    act.wait_ge(k_ready, u + 1)
                    nc.scalar.activation(k32[p][:], b_ps[:], ACT.Identity, bias=k_ones[:]).then_inc(k_copied, 1)
                    nc.scalar.activation(kb[:], b_ps[:], ACT.Copy).then_inc(k_copied, 1)

                def narrow(u, p, r):
                    act.wait_ge(rot_ready, HG * u + r + 1)
                    nc.scalar.activation(rotb[:, r], rot[p][:, r], ACT.Copy).then_inc(rotb_ready, 1)

                def exps(t, r):
                    for j in range(NT):
                        act.wait_ge(scored, 16 * t + 4 * r + j + 1)
                        nc.scalar.activation(probs[:, r % 2, j], score_ps[j % 2][:], ACT.Exp, scale=SCALE).then_inc(exped, 1)

                def step(t, p):
                    u, n = t + 1, 1 - p
                    copy_qk(u, n)
                    for r in range(HG):
                        exps(t, r)
                        narrow(u, n, r)
                    act.wait_ge(av_ready, t + 1)
                    nc.scalar.activation(av[:], av_ps[:], ACT.Copy).then_inc(av_copied, 1)

                copy_qk(0, 0)
                for r in range(HG):
                    narrow(0, 0, r)
                with act.Fori(0, TURNS // 2) as i:
                    step(2 * i, 0)
                    step(2 * i + 1, 1)

            @block.vector
            def _(dve):
                dve.wait_ge(tables, 16 * N_TABLES)
                dve.wait_ge(set_up, 2)
                dve.sem_inc(maxed, 1)
                dve.sem_inc(added, 1)

                def copy_v(u, p):
                    dve.wait_ge(v_ready, u + 1)
                    nc.vector.tensor_scalar(vaug[p][:, :, :, 0:8],
                                            misc_ps[:, 0:P].rearrange("p (j r e) -> p j r e", j=NT, r=HG),
                                            1.0, None, ALU.mult).then_inc(v_copied, 1)

                def turn(u, r):
                    dve.wait_ge(turned, HG * u + r + 1)
                    if r >= 2:
                        dve.wait_ge(rot_ready, HG * u + r - 1)
                    nc.vector.tensor_tensor(half[:, r % 2, 0], a_ps[:], cos_q[:], ALU.mult)
                    nc.vector.tensor_tensor(half[:, r % 2, 1], b_ps[:], sin_q[:], ALU.mult).then_inc(halves, 1)

                def maximum(u, r, h):
                    dve.wait_ge(rough, 8 * u + 2 * r + h + 1)
                    for k in range(2):
                        last = nc.vector.tensor_reduce(maxima[:, 2 * h + k, 32 * r:32 * r + 1], c.bank[6 + k][:], AX_X, ALU.max)
                    last.then_inc(maxed, 1)

                def finish_q(u, p):
                    dve.wait_ge(max_turned, u + 1)
                    nc.vector.tensor_tensor(q32[p][:], q32[p][:], misc_ps[:], ALU.subtract).then_inc(q_final, 1)

                def normalise(t):
                    dve.wait_ge(den_ready, t + 1)
                    nc.vector.reciprocal(rden[:], av_ps[:]).then_inc(den_inv, 1)
                    dve.wait_ge(den_inv, t + 1)
                    nc.vector.tensor_tensor(avn[:], av[:], rden[:], ALU.mult).then_inc(avn_ready, 1)

                def add(t, b):
                    dve.wait_ge(o_ready, t + 1)
                    nc.vector.tensor_tensor(c.resid[:, b], c.resid[:, b], av_ps[:], ALU.add).then_inc(added, 1)

                def step(t, b, p):
                    u, n = t + 1, 1 - p
                    copy_v(u, n)
                    turn(u, 0)
                    turn(u, 1)
                    for r in range(2):
                        maximum(u, r, 0)
                        maximum(u, r, 1)
                        turn(u, r + 2)
                    maximum(u, 2, 0)
                    maximum(u, 2, 1)
                    normalise(t)
                    maximum(u, 3, 0)
                    add(t, b)
                    maximum(u, 3, 1)
                    finish_q(u, n)

                copy_v(0, 0)
                for r in range(HG):
                    turn(0, r)
                    maximum(0, r, 0)
                    maximum(0, r, 1)
                finish_q(0, 0)
                with dve.Fori(0, TURNS // 2) as i:
                    step(2 * i, i // 2, 0)
                    step(2 * i + 1, i // 2, 1)


def phase_norm(c, name):
    nc = c.nc
    with ExitStack() as ctx:
        ph = Phase(c, ctx)
        cent = [ph.sb(f"{name}_cent{p}", [P, T]) for p in range(2)]
        sq = [ph.sb(f"{name}_sq{p}", [P, T]) for p in range(2)]
        s = [NormSems(ph.sem, f"{name}{p}") for p in range(2)]

        with nc.Block() as block:
            @block.tensor
            def _(pe):
                with pe.Fori(0, NB // 2) as i:
                    for p in range(2):
                        pe.wait_ge(s[p].y, i + 1)
                        nc.tensor.matmul(c.bank[p][:], c.ones[:], c.resid[:, 2 * i + p], start=True, stop=True).then_inc(s[p].mean, 1)
                    for p in range(2):
                        pe.wait_ge(s[p].sq, i + 1)
                        nc.tensor.matmul(c.bank[2 + p][:], c.ones[:], sq[p][:], start=True, stop=True).then_inc(s[p].var, 1)

            @block.scalar
            def _(act):
                nc.scalar.preload_act_table_set(LN_EXP)
                with act.Fori(0, NB // 2) as i:
                    for p in range(2):
                        act.wait_ge(s[p].cent, i + 1)
                        nc.scalar.activation(sq[p][:], cent[p][:], ACT.Square).then_inc(s[p].sq, 1)
                    for p in range(2):
                        var = c.bank[2 + p]
                        act.wait_ge(s[p].var, i + 1)
                        nc.scalar.activation(var[:], var[:], ACT.Ln, bias=c.eps[:]).then_inc(s[p].log, 1)
                        act.wait_ge(s[p].log, i + 1)
                        nc.scalar.activation(var[:], var[:], ACT.Exp, scale=-0.5).then_inc(s[p].rstd, 1)

            @block.vector
            def _(dve):
                for p in range(2):
                    dve.sem_inc(s[p].y, 1)
                with dve.Fori(0, NB // 2) as i:
                    for p in range(2):
                        dve.wait_ge(s[p].mean, i + 1)
                        nc.vector.tensor_tensor(cent[p][:], c.resid[:, 2 * i + p], c.bank[p][:], ALU.subtract).then_inc(s[p].cent, 1)
                    for p in range(2):
                        dve.wait_ge(s[p].rstd, i + 1)
                        nc.vector.tensor_tensor(c.resid[:, 2 * i + p], cent[p][:], c.bank[2 + p][:], ALU.mult).then_inc(s[p].y, 1)


NE = 32
TOP = 4


def gates_of_batches(c, d, ph, gate_parts):
    nc = c.nc
    sel_w = ph.sb("sel_w", [P, NE])
    vec = ph.sb("ln2_vec", [P, 2])
    y, cent, sq, x2 = (ph.sb(f"gate_{n}", [P, T]) for n in ("y", "cent", "sq", "x2"))
    e = ph.sb("gate_exp", [P, NT, NE])
    e1 = ph.sb("gate_exp1", [P, NT, NE])
    prob = ph.sb("gate_prob", [P, NT, NE])
    top8 = ph.sb("gate_top8", [P, NT, 8])
    above = ph.sb("gate_above", [P, NT, NE])
    equal = ph.sb("gate_equal", [P, NT, NE])
    n_above = ph.sb("gate_n_above", [P, NT])
    nth = ph.sb("gate_nth", [P, NT, NE])
    fits = ph.sb("gate_fits", [P, NT, NE])
    tie = ph.sb("gate_tie", [P, NT, NE])
    chosen = ph.sb("gate_chosen", [P, NT, NE])
    gate = ph.sb("gate_value", [P, NT, NE])
    one = ph.sb("gate_one", [P, NE])
    pad = ph.sb("gate_pad", [P, 1])
    rest = ph.sb("gate_rest", [NE, T])
    mid = ph.sb("gate_mid", [NE, T], BF16)
    high = ph.sb("gate_high", [NE, T], BF16)
    loaded, set_up = ph.sem("p3_loaded"), ph.sem("p3_set_up")
    ln = NormSems(ph.sem, "p3n")
    x2_ready, logits, exped = ph.sem("p3_x2"), ph.sem("p3_logits"), ph.sem("p3_exped")
    chain = ph.sem("p3_dve_chain")
    gate_ready, gate_turned = ph.sem("p3_gate"), ph.sem("p3_gate_turned")
    DVE_STEPS = 16
    mean_ps, var_ps, logit_ps, gate_ps = (c.bank[i] for i in range(4))
    logit_v = logit_ps[:, 0:NT * NE].rearrange("p (j e) -> p j e", j=NT)

    with nc.Block() as block:
        @block.sync
        def _(sp):
            sp.dma_start(sel_w[:], d["sel_w"]).then_inc(loaded, 16)
            sp.dma_start(vec[:, 0:1], d["ln2_g"]).then_inc(loaded, 16)
            sp.dma_start(vec[:, 1:2], d["ln2_b"]).then_inc(loaded, 16)

        @block.gpsimd
        def _(pool):
            nc.gpsimd.memset(one[:], 1.0).then_inc(set_up, 1)

        @block.tensor
        def _(pe):
            pe.wait_ge(loaded, 48)
            with pe.Fori(0, NB) as b:
                norm_pe(nc, pe, ln, b + 1, c.ones[:], y[:], sq[:], mean_ps[:], var_ps[:])
                pe.wait_ge(x2_ready, b + 1)
                for j in range(NT):
                    last = nc.tensor.matmul(logit_v[:, j], x2[:, P * j:P * j + P], sel_w[:], start=True, stop=True)
                last.then_inc(logits, 1)
                pe.wait_ge(gate_ready, b + 1)
                for j in range(NT):
                    last = nc.tensor.transpose(gate_ps[0:NE, P * j:P * j + P], gate[:, j], c.ident[:])
                last.then_inc(gate_turned, 1)

        @block.scalar
        def _(act):
            nc.scalar.preload_act_table_set(LN_EXP)
            with act.Fori(0, NB) as b:
                norm_act(nc, act, ln, b + 1, cent[:], sq[:], var_ps[:], c.eps[:])
                act.wait_ge(logits, b + 1)
                nc.scalar.activation(e[:], logit_v, ACT.Exp, scale=-1.0).then_inc(exped, 1)

        @block.vector
        def _(dve):
            dve.wait_ge(loaded, 48)
            dve.wait_ge(set_up, 1)
            with dve.Fori(0, NB) as b:
                steps = [0]

                def then(ins):
                    steps[0] += 1
                    ins.then_inc(chain, 1)
                    dve.wait_ge(chain, DVE_STEPS * b + steps[0])

                nc.vector.tensor_scalar(y[:], c.resid[:, b], 1.0, None, ALU.mult).then_inc(ln.y, 1)
                dve.wait_ge(ln.y, b + 1)
                nc.vector.tensor_tensor(c.resid[:, b], y[:], c.outer[:, b], ALU.add)
                norm_dve(nc, dve, ln, b + 1, y[:], cent[:], mean_ps[:], var_ps[:], y[:])
                dve.wait_ge(ln.out, b + 1)
                nc.vector.tensor_scalar(x2[:], y[:], vec[:, 0:1], vec[:, 1:2], ALU.mult, ALU.add).then_inc(x2_ready, 1)
                dve.wait_ge(x2_ready, b + 1)
                nc.vector.tensor_scalar(c.normed[:, b], x2[:], 1.0, None, ALU.mult)
                dve.wait_ge(exped, b + 1)
                then(nc.vector.tensor_scalar(e1[:], e[:], 1.0, None, ALU.add))
                then(nc.vector.reciprocal(prob[:], e1[:]))
                nc.vector.memset(pad[:], 0.0)
                for j in range(NT):
                    last = nc.vector.max(top8[:, j], prob[:, j])
                then(last)
                for j in range(NT):
                    fourth = top8[:, j, TOP - 1:TOP]
                    nc.vector.tensor_scalar(above[:, j], prob[:, j], fourth, None, ALU.is_gt)
                    last = nc.vector.tensor_scalar(equal[:, j], prob[:, j], fourth, None, ALU.is_equal)
                then(last)
                nc.vector.tensor_reduce(n_above[:], above[:], AX_X, ALU.add)
                for j in range(NT):
                    last = nc.vector.tensor_tensor_scan(nth[:, j], one[:], equal[:, j], 0.0, ALU.mult, ALU.add)
                then(last)
                for j in range(NT):
                    last = nc.vector.tensor_scalar(fits[:, j], nth[:, j], n_above[:, j:j + 1], float(TOP), ALU.add, ALU.is_le)
                then(last)
                then(nc.vector.tensor_tensor(tie[:], equal[:], fits[:], ALU.mult))
                then(nc.vector.tensor_tensor(chosen[:], tie[:], above[:], ALU.add))
                nc.vector.tensor_tensor(gate[:], chosen[:], prob[:], ALU.mult).then_inc(gate_ready, 1)
                dve.wait_ge(gate_turned, b + 1)
                then(nc.vector.tensor_copy(high[:], gate_ps[0:NE, :]))
                then(nc.vector.tensor_tensor(rest[:], gate_ps[0:NE, :], high[:], ALU.subtract))
                nc.vector.tensor_scalar(gate_parts[0:NE, b], high[:], 1.0, None, ALU.mult)
                then(nc.vector.tensor_copy(mid[:], rest[:]))
                nc.vector.tensor_scalar(gate_parts[NE:2 * NE, b], mid[:], 1.0, None, ALU.mult)
                then(nc.vector.tensor_tensor(gate_parts[2 * NE:3 * NE, b], rest[:], mid[:], ALU.subtract))
                for _ in range(DVE_STEPS - steps[0]):
                    dve.sem_inc(chain, 1)


def experts(c, d, ph, gate_parts):
    nc = c.nc
    keys = [ph.sb(f"keys{p}", [P, P]) for p in range(2)]
    values = [ph.sb(f"values{p}", [P, P]) for p in range(2)]
    pick = [ph.sb(f"pick_expert{p}", [3 * NE, P], BF16) for p in range(2)]
    h = [ph.sb(f"hidden{p}", [P, T]) for p in range(2)]
    hg = [ph.sb(f"hidden_gated{p}", [P, T]) for p in range(2)]
    here = [ph.sem(f"p3_expert_here{p}") for p in range(2)]
    h_ready, g_ready = ph.sem("p3_h"), ph.sem("p3_g")
    rectified, gated = ph.sem("p3_rectified"), ph.sem("p3_gated")
    valued = ph.sem("p3_valued")
    added = ph.sem("p3_added")
    h_ps, g_ps, v_ps = c.bank[0:2], c.bank[2:4], c.bank[4:6]

    with nc.Block() as block:
        @block.sync
        def _(sp):
            def load(x, p):
                sp.dma_start(keys[p][:], d["keys"][x]).then_inc(here[p], 16)
                sp.dma_start(values[p][:], d["values"][x]).then_inc(here[p], 16)
                sp.dma_start(pick[p][:], d["pick_expert"][x]).then_inc(here[p], 16)

            load(0, 0)
            load(1, 1)
            with sp.Fori(0, NE // 2 - 1) as i:
                for p in range(2):
                    sp.wait_ge(valued, NB * (2 * i + p + 1))
                    load(2 * i + p + 2, p)

        @block.tensor
        def _(pe):
            with pe.Fori(0, NE // 2) as i:
                def apply_values(k):
                    pe.wait_ge(gated, 2 * NB * i + k + 1)
                    pe.wait_ge(added, 2 * NB * i + k + 1)
                    nc.tensor.matmul(v_ps[k % 2][:], values[k // NB][:], hg[k % 2][:], start=True, stop=True).then_inc(valued, 1)

                for k in range(2 * NB):
                    p, b = divmod(k, NB)
                    if b == 0:
                        pe.wait_ge(here[p], 48 * (i + 1))
                    nc.tensor.matmul(h_ps[k % 2][:], keys[p][:], c.normed[:, b], start=True, stop=True).then_inc(h_ready, 1)
                    nc.tensor.matmul(g_ps[k % 2][:], pick[p][:], gate_parts[:, b], start=True, stop=True).then_inc(g_ready, 1)
                    if k:
                        apply_values(k - 1)
                apply_values(2 * NB - 1)

        @block.scalar
        def _(act):
            with act.Fori(0, NE // 2) as i:
                for k in range(2 * NB):
                    act.wait_ge(h_ready, 2 * NB * i + k + 1)
                    nc.scalar.activation(h[k % 2][:], h_ps[k % 2][:], ACT.Relu).then_inc(rectified, 1)

        @block.vector
        def _(dve):
            dve.sem_inc(added, 2)
            with dve.Fori(0, NE // 2) as i:
                def add(k):
                    dve.wait_ge(valued, 2 * NB * i + k + 1)
                    resid = c.resid[:, k % NB]
                    nc.vector.tensor_tensor(resid, resid, v_ps[k % 2][:], ALU.add).then_inc(added, 1)

                for k in range(2 * NB):
                    dve.wait_ge(rectified, 2 * NB * i + k + 1)
                    dve.wait_ge(g_ready, 2 * NB * i + k + 1)
                    nc.vector.tensor_tensor(hg[k % 2][:], h[k % 2][:], g_ps[k % 2][:], ALU.mult).then_inc(gated, 1)
                    if k:
                        add(k - 1)
                add(2 * NB - 1)


def phase_experts(c, d):
    with ExitStack() as ctx:
        ph = Phase(c, ctx)
        gate_parts = ph.sb("gate_parts", [3 * NE, NB, T], BF16)
        gates_of_batches(c, d, ph, gate_parts)
        experts(c, d, ph, gate_parts)
    phase_norm(c, "ffn0_norm")


NH = 4
DS = 64
NR = NB * NH
DI = NH * DS
TWO_PI_HI = 6.28125
TWO_PI_LO = 2.0 * np.pi - TWO_PI_HI
ROUND = 1.5 * 2.0 ** 23
PI_IN = 3.1415925
NEG = -1e30


def state_space_rows(c, d, ph, dt, ncs, cols):
    nc = c.nc
    w_rows = ph.sb("w_rows", [P, 3, NB, NR])
    bias = ph.sb("dt_bias", [NR, 1])
    absd, absa = ph.sb("ss_absd", [NR, T]), ph.sb("ss_absa", [NR, T])
    one = ph.sb("ss_one", [NR, T])
    m, sp, trap, w1, w2, decay, nadt, cc, n1 = (ph.sb(f"ss_{n}", [NR, T]) for n in (
        "max0", "softplus_a", "trap", "w1", "w2", "decay", "neg_adt", "c", "n1"))
    loaded, set_up = ph.sem("p4_loaded"), ph.sem("p4_set_up")
    rows_ready = ph.sem("p4_rows")
    act_chain, dve_chain = ph.sem("p4_act_chain"), ph.sem("p4_dve_chain")
    dt_log, a_log, trap_exp, decay_ready = ph.sem("p4_dt_log"), ph.sem("p4_a_log"), ph.sem("p4_trap_exp"), ph.sem("p4_decay")
    nadt_ready, cols_in, cols_turned = ph.sem("p4_nadt"), ph.sem("p4_cols_in"), ph.sem("p4_cols_turned")
    dt_ps, a_ps, trap_ps = (c.bank[i][0:NR, :] for i in range(3))

    with nc.Block() as block:
        @block.sync
        def _(sp_):
            sp_.dma_start(w_rows[:], d["ss_w_rows"]).then_inc(loaded, 16)
            sp_.dma_start(bias[:], d["ss_dt_bias"]).then_inc(loaded, 16)

        @block.gpsimd
        def _(pool):
            nc.gpsimd.memset(one[:], 1.0).then_inc(set_up, 1)

        @block.tensor
        def _(pe):
            pe.wait_ge(loaded, 32)
            for q, ps in enumerate((dt_ps, a_ps, trap_ps)):
                for b in range(NB):
                    last = nc.tensor.matmul(ps, w_rows[:, q, b], c.resid[:, b], start=(b == 0), stop=(b == NB - 1))
                last.then_inc(rows_ready, 1)
            pe.wait_ge(cols_in, 1)
            for q, rows in enumerate((cc, n1, w1)):
                for j in range(NT):
                    last = nc.tensor.transpose(c.bank[3 + q][:, NR * j:NR * j + NR], rows[:, P * j:P * j + P], c.ident[0:NR, 0:NR])
            last.then_inc(cols_turned, 1)

        @block.scalar
        def _(act):
            nc.scalar.preload_act_table_set(LN_EXP)
            steps = [0]

            def then(ins):
                steps[0] += 1
                ins.then_inc(act_chain, 1)
                act.wait_ge(act_chain, steps[0])

            act.wait_ge(loaded, 32)
            act.wait_ge(rows_ready, 2)
            then(nc.scalar.activation(absd[:], dt_ps, ACT.Abs, bias=bias[:]))
            then(nc.scalar.activation(absd[:], absd[:], ACT.Exp, scale=-1.0))
            nc.scalar.activation(absd[:], absd[:], ACT.Ln, bias=1.0).then_inc(dt_log, 1)
            then(nc.scalar.activation(absa[:], a_ps, ACT.Abs))
            then(nc.scalar.activation(absa[:], absa[:], ACT.Exp, scale=-1.0))
            nc.scalar.activation(absa[:], absa[:], ACT.Ln, bias=1.0).then_inc(a_log, 1)
            act.wait_ge(rows_ready, 3)
            nc.scalar.activation(trap[:], trap_ps, ACT.Exp, scale=-1.0).then_inc(trap_exp, 1)
            act.wait_ge(nadt_ready, 1)
            nc.scalar.activation(decay[:], nadt[:], ACT.Exp, scale=-1.0).then_inc(decay_ready, 1)

        @block.vector
        def _(dve):
            steps = [0]

            def then(ins):
                steps[0] += 1
                ins.then_inc(dve_chain, 1)
                dve.wait_ge(dve_chain, steps[0])

            dve.wait_ge(loaded, 32)
            dve.wait_ge(set_up, 1)
            dve.wait_ge(dt_log, 1)
            then(nc.vector.tensor_scalar(m[:], dt_ps, bias[:], 0.0, ALU.add, ALU.max))
            then(nc.vector.tensor_tensor(dt[:], m[:], absd[:], ALU.add))
            dve.wait_ge(a_log, 1)
            then(nc.vector.tensor_scalar(m[:], a_ps, 0.0, None, ALU.max))
            then(nc.vector.tensor_tensor(sp[:], m[:], absa[:], ALU.add))
            nc.vector.scalar_tensor_tensor(out=nadt[:], in0=sp[:], scalar=1e-4, in1=dt[:], op0=ALU.max, op1=ALU.mult).then_inc(nadt_ready, 1)
            dve.wait_ge(nadt_ready, 1)
            then(nc.vector.tensor_tensor_scan(ncs[:], one[:], nadt[:], 0.0, ALU.mult, ALU.add))
            dve.wait_ge(trap_exp, 1)
            then(nc.vector.tensor_scalar(m[:], trap[:], 1.0, None, ALU.add))
            then(nc.vector.reciprocal(sp[:], m[:]))
            then(nc.vector.tensor_tensor(w1[:], sp[:], dt[:], ALU.mult))
            then(nc.vector.tensor_tensor(w2[:], dt[:], w1[:], ALU.subtract))
            nc.vector.memset(cc[:, T - 1:T], 0.0)
            nc.vector.memset(n1[:, T - 1:T], 0.0)
            nc.vector.tensor_copy(n1[:, 0:T - 1], ncs[:, 1:T])
            dve.wait_ge(decay_ready, 1)
            then(nc.vector.tensor_tensor(m[:, 0:T - 1], decay[:, 1:T], w1[:, 0:T - 1], ALU.mult))
            nc.vector.tensor_tensor(cc[:, 0:T - 1], m[:, 0:T - 1], w2[:, 1:T], ALU.add).then_inc(cols_in, 1)
            dve.wait_ge(cols_turned, 1)
            for q in range(3):
                nc.vector.tensor_copy(cols[:, q], c.bank[3 + q][:, 0:NT * NR].rearrange("p (j r) -> p j r", j=NT))


def state_space_angles(c, d, ph, dt, cos, sin):
    nc = c.nc
    w_ang = ph.sb("w_angle", [P, P])
    sign = ph.sb("sin_sign", [P, 1])
    pick = ph.sb("pick_mean", [NR, P])
    one = ph.sb("ang_one", [P, T])
    mean_dt, step_, phase, km, k, r1, r2, r, over, rc = (ph.sb(f"ang_{n}", [P, T]) for n in (
        "mean_dt", "step", "phase", "km", "k", "r1", "r2", "r", "over", "rc"))
    loaded, set_up, here = ph.sem("p4a_loaded"), ph.sem("p4a_set_up"), ph.sem("p4a_here")
    projected, copied = ph.sem("p4a_projected"), ph.sem("p4a_copied")
    chain = ph.sem("p4a_chain")
    reduced, turned = ph.sem("p4a_reduced"), ph.sem("p4a_sines")
    STEPS = 9
    ang_ps, mean_ps = c.bank[0], c.bank[1]

    with nc.Block() as block:
        @block.sync
        def _(sp):
            sp.dma_start(w_ang[:], d["ss_w_angle"]).then_inc(loaded, 16)
            sp.dma_start(sign[:], d["ss_sign"]).then_inc(loaded, 16)
            sp.dma_start(pick[:], d["ss_pick"][0, :, NH * P:]).then_inc(here, 16)
            with sp.Fori(0, NB - 1) as b:
                sp.wait_ge(projected, b + 1)
                sp.dma_start(pick[:], d["ss_pick"][b + 1, :, NH * P:]).then_inc(here, 16)

        @block.gpsimd
        def _(pool):
            nc.gpsimd.memset(one[:], 1.0).then_inc(set_up, 1)

        @block.tensor
        def _(pe):
            pe.wait_ge(loaded, 32)
            with pe.Fori(0, NB) as b:
                pe.wait_ge(here, 16 * (b + 1))
                pe.wait_ge(chain, STEPS * b + 1)
                nc.tensor.matmul(ang_ps[:], w_ang[:], c.resid[:, b], start=True, stop=True)
                nc.tensor.matmul(mean_ps[:], pick[:], dt[:], start=True, stop=True).then_inc(projected, 1)

        @block.scalar
        def _(act):
            act.wait_ge(loaded, 32)
            with act.Fori(0, NB) as b:
                act.wait_ge(projected, b + 1)
                nc.scalar.activation(mean_dt[:], mean_ps[:], ACT.Copy).then_inc(copied, 1)
                act.wait_ge(reduced, b + 1)
                nc.scalar.activation(sin[:, b], r[:], ACT.Sin, scale=sign[:])
                nc.scalar.activation(cos[:, b], rc[:], ACT.Sin).then_inc(turned, 1)

        @block.vector
        def _(dve):
            dve.wait_ge(set_up, 1)
            dve.sem_inc(chain, 1)
            dve.sem_inc(turned, 1)
            with dve.Fori(0, NB) as b:
                steps = [0]

                def then(ins):
                    steps[0] += 1
                    ins.then_inc(chain, 1)
                    dve.wait_ge(chain, STEPS * b + steps[0] + 1)

                dve.wait_ge(copied, b + 1)
                then(nc.vector.tensor_tensor(step_[:], ang_ps[:], mean_dt[:], ALU.mult))
                then(nc.vector.tensor_tensor_scan(phase[:], one[:], step_[:], 0.0, ALU.mult, ALU.add))
                then(nc.vector.tensor_scalar(km[:], phase[:], 0.5 / np.pi, ROUND, ALU.mult, ALU.add))
                then(nc.vector.tensor_scalar(k[:], km[:], -ROUND, None, ALU.add))
                then(nc.vector.scalar_tensor_tensor(out=r1[:], in0=k[:], scalar=-TWO_PI_HI, in1=phase[:], op0=ALU.mult, op1=ALU.add))
                then(nc.vector.scalar_tensor_tensor(out=r2[:], in0=k[:], scalar=-TWO_PI_LO, in1=r1[:], op0=ALU.mult, op1=ALU.add))
                dve.wait_ge(turned, b + 1)
                then(nc.vector.tensor_scalar(r[:], r2[:], PI_IN, -PI_IN, ALU.min, ALU.max))
                then(nc.vector.tensor_scalar(over[:], r[:], np.pi / 2, -2.0 * np.pi, ALU.is_gt, ALU.mult))
                then(nc.vector.scalar_tensor_tensor(out=r1[:], in0=r[:], scalar=np.pi / 2, in1=over[:], op0=ALU.add, op1=ALU.add))
                nc.vector.tensor_scalar(rc[:], r1[:], PI_IN, -PI_IN, ALU.min, ALU.max).then_inc(reduced, 1)


def state_space_outputs(c, d, ph, ncs, cols, cos, sin):
    nc = c.nc
    w_bc = ph.sb("w_bc", [P, P])
    w_zx = ph.sb("w_zx", [P, 2 * DI])
    w_out = ph.sb("ss_w_out", [P, 2, P])
    vec = ph.sb("bc_vec", [P, 2])
    ones64 = ph.sb("ones64", [P, P])
    swap = ph.sb("swap_pairs", [P, P])
    later = ph.sb("later", [P, NT, P])
    d_rep = ph.sb("d_rep", [P, NT, NH])
    pick = ph.sb("pick_rows", [NR, NH * P])
    xs = ph.sb("ss_x", [P, T])
    bc, cent, sq, v0, v, t1, t2 = (ph.sb(f"bc_{n}", [P, T]) for n in ("raw", "cent", "sq", "v0", "v", "t1", "t2"))
    brot, crot = ph.sb("b_rot", [DS, T]), ph.sb("c_rot", [DS, T])
    ez, lz = ph.sb("ez", [P, NT, DI]), ph.sb("lz", [P, NT, DI])
    zs, xt, xc = (ph.sb(f"ss_{n}", [P, NT, DI]) for n in ("zs", "xt", "xc"))
    cq = ph.sb("cq", [P, 3, NT, NH])
    cb = ph.sb("cb", [P, NT])
    cbw = ph.sb("cbw", [P, P])
    dcoef = ph.sb("dcoef", [P, NT, NH])
    y1 = ph.sb("y1", [P, NT, DI])
    yg = ph.sb("yg", [P, NT, DI])
    ygt = ph.sb("ygt", [P, 2, T])
    OFF = [0, 512, 896, 1152]
    WID = [512 - P * j for j in range(NT)]
    diag = [ph.sb(f"diag{p}", [P, T]) for p in range(2)]
    e = [ph.sb(f"e_{p}", [P, 1280]) for p in range(2)]
    mm = [ph.sb(f"m_{p}", [P, 1280]) for p in range(2)]

    loaded = ph.sem("p4b_loaded")
    here = ph.sem("p4b_here")
    done = ph.sem("p4b_done")
    bc_ready, zx_ready = ph.sem("p4b_bc"), ph.sem("p4b_zx")
    ln = NormSems(ph.sem, "p4b_n")
    v_ready, swapped, rotated = ph.sem("p4b_v"), ph.sem("p4b_swapped"), ph.sem("p4b_rotated")
    z_exp, z_clamped, z_log, z_sig = ph.sem("p4b_z_exp"), ph.sem("p4b_z_clamped"), ph.sem("p4b_z_log"), ph.sem("p4b_z_sig")
    x_copied, z_used = ph.sem("p4b_x_copied"), ph.sem("p4b_z_used")
    cb_ready, xc_ready = ph.sem("p4b_cb"), ph.sem("p4b_xc")
    n_ready, diag_ready, e_ready, m_ready = ph.sem("p4b_n_row"), ph.sem("p4b_diag"), ph.sem("p4b_e"), ph.sem("p4b_m")
    y_ready, yg_ready, ygt_ready, ygt_copied, o_ready = (ph.sem(f"p4b_{n}") for n in ("y", "yg", "ygt", "ygt_copied", "o"))
    chain = ph.sem("p4b_chain")
    STEPS = 16
    N_LOADS = 12
    bank = c.bank

    with nc.Block() as block:
        @block.sync
        def _(sp):
            sp.dma_start(w_bc[:], d["ss_w_bc"]).then_inc(loaded, 16)
            sp.dma_start(w_zx[:], d["ss_w_zx"]).then_inc(loaded, 16)
            sp.dma_start(w_out[:], d["ss_w_out"]).then_inc(loaded, 16)
            sp.dma_start(vec[:, 0:1], d["ss_gain"]).then_inc(loaded, 16)
            sp.dma_start(vec[:, 1:2], d["ss_shift"]).then_inc(loaded, 16)
            sp.dma_start(ones64[:], d["ones64"]).then_inc(loaded, 16)
            sp.dma_start(swap[:], d["ss_swap"]).then_inc(loaded, 16)
            for j in range(NT):
                sp.dma_start(later[:, j], d["ss_later"]).then_inc(loaded, 16)
            sp.dma_start(d_rep[:], d["ss_d"]).then_inc(loaded, 16)
            with sp.Fori(0, NB) as b:
                sp.wait_ge(done, b + 1)
                sp.dma_start(pick[:], d["ss_pick"][b, :, 0:NH * P]).then_inc(here, 16)
                sp.dma_start(xs[:], c.resid[:, b]).then_inc(here, 16)

        @block.tensor
        def _(pe):
            pe.wait_ge(loaded, 16 * N_LOADS)
            with pe.Fori(0, NB) as b:
                pe.wait_ge(here, 32 * (b + 1))
                nc.tensor.matmul(bank[0][:], w_bc[:], xs[:], start=True, stop=True).then_inc(bc_ready, 1)
                for j in range(NT):
                    nc.tensor.matmul(bank[3 + j][:], xs[:, P * j:P * j + P], w_zx[:], start=True, stop=True).then_inc(zx_ready, 1)
                norm_pe(nc, pe, ln, b + 1, ones64[:], bc[:], sq[:], bank[1][:], bank[2][:])
                pe.wait_ge(v_ready, b + 1)
                nc.tensor.matmul(bank[0][:], swap[:], v[:], start=True, stop=True).then_inc(swapped, 1)
                pe.wait_ge(rotated, b + 1)
                pe.wait_ge(x_copied, b + 1)
                pe.wait_ge(z_used, b + 1)
                for j in range(NT):
                    nc.tensor.matmul(bank[4 + j][:, 0:WID[j]], brot[:, P * j:P * j + P], crot[:, P * j:],
                                     start=True, stop=True).then_inc(cb_ready, 1)

                def row_of(h):
                    nc.tensor.matmul(bank[h % 2][:], pick[:, P * h:P * h + P], ncs[:], start=True, stop=True).then_inc(n_ready, 1)

                row_of(0)
                row_of(1)
                pe.wait_ge(xc_ready, b + 1)
                for h in range(NH):
                    pe.wait_ge(m_ready, NH * b + h + 1)
                    for tt in range(NT):
                        for j in range(tt + 1):
                            at = OFF[j] + P * (tt - j)
                            last = nc.tensor.matmul(bank[2 + tt // 2][:, DI * (tt % 2) + DS * h:DI * (tt % 2) + DS * h + DS],
                                                    mm[h % 2][:, at:at + P], xc[:, j, DS * h:DS * h + DS],
                                                    start=(j == 0), stop=(j == tt))
                    if h + 2 < NH:
                        row_of(h + 2)
                last.then_inc(y_ready, 1)
                pe.wait_ge(yg_ready, b + 1)
                for f in range(2):
                    for tt in range(NT):
                        last = nc.tensor.transpose(bank[4 + f][:, P * tt:P * tt + P], yg[:, tt, P * f:P * f + P], c.ident[:])
                last.then_inc(ygt_ready, 1)
                pe.wait_ge(ygt_copied, b + 1)
                for f in range(2):
                    last = nc.tensor.matmul(bank[0][:], w_out[:, f], ygt[:, f], start=(f == 0), stop=(f == 1))
                last.then_inc(o_ready, 1)

        @block.scalar
        def _(act):
            nc.scalar.preload_act_table_set(LN_EXP)
            act.wait_ge(loaded, 16 * N_LOADS)
            with act.Fori(0, NB) as b:
                act.wait_ge(bc_ready, b + 1)
                nc.scalar.activation(bc[:], bank[0][:], ACT.Copy).then_inc(ln.y, 1)
                for j in range(NT):
                    act.wait_ge(zx_ready, NT * b + j + 1)
                    nc.scalar.activation(ez[:, j], bank[3 + j][:, 0:DI], ACT.Exp, scale=-1.0).then_inc(z_exp, 1)
                norm_act(nc, act, ln, b + 1, cent[:], sq[:], bank[2][:], c.eps[:])
                for j in range(NT):
                    last = nc.scalar.activation(xt[:, j], bank[3 + j][:, DI:], ACT.Copy)
                last.then_inc(x_copied, 1)
                act.wait_ge(z_clamped, b + 1)
                nc.scalar.activation(lz[:], ez[:], ACT.Ln).then_inc(z_log, 1)
                act.wait_ge(z_log, b + 1)
                nc.scalar.activation(lz[:], lz[:], ACT.Exp, scale=-1.0).then_inc(z_sig, 1)
                for h in range(NH):
                    act.wait_ge(diag_ready, NH * b + h + 1)
                    for j in range(NT):
                        n1 = cq[:, 1, j, h:h + 1]
                        last = nc.scalar.activation(e[h % 2][:, OFF[j]:OFF[j] + P], diag[h % 2][:, P * j:P * j + P], ACT.Exp, bias=n1)
                        if j < NT - 1:
                            last = nc.scalar.activation(e[h % 2][:, OFF[j] + P:OFF[j] + WID[j]], bank[h % 2][:, P * (j + 1):],
                                                        ACT.Exp, scale=-1.0, bias=n1)
                    last.then_inc(e_ready, 1)
                act.wait_ge(ygt_ready, b + 1)
                for f in range(2):
                    last = nc.scalar.activation(ygt[:, f], bank[4 + f][:], ACT.Copy)
                last.then_inc(ygt_copied, 1)

        @block.vector
        def _(dve):
            dve.wait_ge(loaded, 16 * N_LOADS)
            dve.sem_inc(done, 1)
            with dve.Fori(0, NB) as b:
                steps = [0]

                def then(ins):
                    steps[0] += 1
                    ins.then_inc(chain, 1)
                    dve.wait_ge(chain, STEPS * b + steps[0])

                nc.vector.tensor_scalar(cq[:], cols[:, :, :, bass.ds(NH * b, NH)], 1.0, None, ALU.mult).then_inc(chain, 1)
                steps[0] += 1
                dve.wait_ge(z_exp, NT * b + NT)
                nc.vector.tensor_scalar(ez[:], ez[:], 1e18, 1.0, ALU.min, ALU.add).then_inc(z_clamped, 1)
                norm_dve(nc, dve, ln, b + 1, bc[:], cent[:], bank[1][:], bank[2][:], v0[:])
                dve.wait_ge(ln.out, b + 1)
                nc.vector.tensor_scalar(v[:], v0[:], vec[:, 0:1], vec[:, 1:2], ALU.mult, ALU.add).then_inc(v_ready, 1)
                dve.wait_ge(v_ready, b + 1)
                nc.vector.tensor_tensor(t1[:], v[:], cos[:, b], ALU.mult)
                dve.wait_ge(swapped, b + 1)
                then(nc.vector.tensor_tensor(t2[:], sin[:, b], bank[0][:], ALU.mult))
                nc.vector.tensor_tensor(brot[:], t1[0:DS], t2[0:DS], ALU.add)
                nc.vector.tensor_tensor(crot[:], t1[DS:P], t2[DS:P], ALU.add).then_inc(rotated, 1)
                dve.wait_ge(z_sig, b + 1)
                for j in range(NT):
                    last = nc.vector.tensor_tensor(zs[:, j], lz[:, j], bank[3 + j][:, 0:DI], ALU.mult)
                last.then_inc(z_used, 1)
                dve.wait_ge(x_copied, b + 1)
                scale = cq[:, 0].rearrange("p j h -> p (j h)").unsqueeze(2).to_broadcast([P, NT * NH, DS])
                nc.vector.tensor_tensor(xc[:].rearrange("p j (h e) -> p (j h) e", e=DS),
                                        xt[:].rearrange("p j (h e) -> p (j h) e", e=DS), scale, ALU.mult).then_inc(xc_ready, 1)
                for h in range(NH):
                    dve.wait_ge(n_ready, NH * b + h + 1)
                    nc.vector.scalar_tensor_tensor(out=diag[h % 2][:], in0=bank[h % 2][:], scalar=-1.0,
                                                   in1=later[:].rearrange("p j t -> p (j t)"),
                                                   op0=ALU.mult, op1=ALU.add).then_inc(diag_ready, 1)
                    if h == 0:
                        dve.wait_ge(cb_ready, NT * b + NT)
                        for j in range(NT):
                            then(nc.vector.tensor_tensor(cbw[:], c.ident[:], bank[4 + j][:, 0:P], ALU.mult))
                            then(nc.vector.tensor_reduce(cb[:, j:j + 1], cbw[:], AX_X, ALU.add))
                        then(nc.vector.tensor_tensor(dcoef[:], cq[:, 2], cb[:].unsqueeze(2).to_broadcast([P, NT, NH]), ALU.mult))
                        then(nc.vector.tensor_tensor(dcoef[:], dcoef[:], d_rep[:], ALU.add))
                    dve.wait_ge(e_ready, NH * b + h + 1)
                    for j in range(NT):
                        part = slice(OFF[j], OFF[j] + WID[j])
                        last = nc.vector.tensor_tensor(mm[h % 2][:, part], e[h % 2][:, part], bank[4 + j][:, 0:WID[j]], ALU.mult)
                    last.then_inc(m_ready, 1)
                then(nc.vector.tensor_tensor(y1[:].rearrange("p j (h e) -> p (j h) e", e=DS),
                                             xt[:].rearrange("p j (h e) -> p (j h) e", e=DS),
                                             dcoef[:].rearrange("p j h -> p (j h)").unsqueeze(2).to_broadcast([P, NT * NH, DS]), ALU.mult))
                dve.wait_ge(y_ready, b + 1)
                for f in range(2):
                    last = nc.vector.tensor_tensor(y1[:, 2 * f:2 * f + 2], y1[:, 2 * f:2 * f + 2],
                                                   bank[2 + f][:].rearrange("p (j e) -> p j e", j=2), ALU.add)
                then(last)
                nc.vector.tensor_tensor(yg[:], y1[:], zs[:], ALU.mult).then_inc(yg_ready, 1)
                dve.wait_ge(o_ready, b + 1)
                nc.vector.tensor_tensor(c.resid[:, b], c.resid[:, b], bank[0][:], ALU.add).then_inc(done, 1)
                for _ in range(STEPS - steps[0]):
                    dve.sem_inc(chain, 1)


def phase_state_space(c, d):
    with ExitStack() as ctx:
        ph = Phase(c, ctx)
        dt, ncs = ph.sb("ss_dt", [NR, T]), ph.sb("ss_ncs", [NR, T])
        cols = ph.sb("ss_cols", [P, 3, NT, NR])
        cos, sin = ph.sb("ss_cos", [P, NB, T]), ph.sb("ss_sin", [P, NB, T])
        with ExitStack() as inner:
            state_space_rows(c, d, Phase(c, inner), dt, ncs, cols)
        with ExitStack() as inner:
            state_space_angles(c, d, Phase(c, inner), dt, cos, sin)
        with ExitStack() as inner:
            state_space_outputs(c, d, Phase(c, inner), ncs, cols, cos, sin)
    phase_norm(c, "ss_norm")


DEPTH = 2
LH = 8
LD = 64
INNER = LH * LD
HID = 341
HC = [(0, 128), (128, 128), (256, HID - 256)]
UNITS = 2 * NT
KW = LD + P
NORM_SCALE = 2.0 ** 20


def head_of(half, slot):
    return 4 * half + 2 * (slot % 2) + slot // 2


class LocalWeights:
    def __init__(self, ph):
        self.qk = ph.sb("l_wqk", [P, 2, INNER])
        self.qk_half = ph.sb("l_wqk_half", [P, 2, INNER])
        self.v = ph.sb("l_wv", [P, INNER])
        self.o = ph.sb("l_wo", [P, NT, P])
        self.w1 = ph.sb("l_w1", [P, 2 * HID])
        self.w2 = ph.sb("l_w2", [P, 3, P])
        self.vec = ph.sb("l_vec", [P, 13])


def local_attention(c, d, ph, w, l, tab, tables, masks, identb, kf, qf):
    nc = c.nc
    s = ph.s
    bank = c.bank
    hx, sq, rinv, th, tsum, v, vh, p, ptb, pta, negmax, psum, prec, o, ot, ssm = (ph.b[n] for n in (
        "hx", "sq", "rinv", "th", "tsum", "v", "vh", "p", "ptb", "pta", "negmax", "psum", "prec", "o", "ot", "ssm"))
    score = [bank[0:2], bank[2:4]]
    N_LOADS = 7
    ones_blk = ph.b["ones_blk"]

    def n_of(b):
        return l * NB + b + 1

    with nc.Block() as block:
        @block.sync
        def _(sp):
            for dst, name in ((w.qk, "l_wqk"), (w.qk_half, "l_wqk_half"), (w.v, "l_wv"), (w.o, "l_wo"),
                              (w.w1, "l_w1"), (w.w2, "l_w2"), (w.vec, "l_vec")):
                sp.dma_start(dst[:], d[name][l]).then_inc(s["w_here"], 16)
            with sp.Fori(0, NB) as b:
                sp.wait_ge(s["projected"], 9 * n_of(b) - 8)
                sp.dma_start(hx[0:LD, :], c.resid[0:LD, b]).then_inc(s["hx_here"], 16)
                sp.dma_start(hx[LD:P, 1:T], c.resid[LD:P, b, 0:T - 1]).then_inc(s["hx_here"], 16)

        @block.gpsimd
        def _(pool):
            with pool.Fori(0, NB) as b:
                for m in range(8):
                    g = (n_of(b) - 1) * 8 + m
                    pool.wait_ge(s["halves"], g + 1 + 2)
                    nc.gpsimd.tensor_tensor(tsum[m % 2][:], th[m % 2][:, 0], th[m % 2][:, 1], ALU.add).then_inc(s["summed"], 1)
                    pool.wait_ge(s["rinv"], g + 1)
                    pool.wait_ge(s["summed"], g + 1)
                    dst = (qf if m % 2 == 0 else kf)[:, m // 2]
                    nc.gpsimd.tensor_tensor(dst, tsum[m % 2][:], rinv[m % 2][:], ALU.mult).then_inc(s["qk_done"], 1)

        @block.tensor
        def _(pe):
            with pe.Fori(0, NB) as b:
                n = n_of(b)
                pe.wait_ge(s["w_here"], 16 * N_LOADS * (l + 1))
                pe.wait_ge(s["hx_here"], 32 * n)
                for j in range(NT):
                    if j >= 2:
                        pe.wait_ge(s["v_copied"], NT * (n - 1) + j - 1)
                    nc.tensor.matmul(bank[4 + j % 2][:], hx[:, P * j:P * j + P], w.v[:], start=True, stop=True).then_inc(s["v_ready"], 1)
                pe.wait_ge(s["added"], n)

                def project(m):
                    q, mm = m % 2, m // 2
                    pe.wait_ge(s["halves"], 8 * (n - 1) + m - 1 + 2)
                    cols = slice(P * mm, P * mm + P)
                    nc.tensor.matmul(bank[2 * q][:], w.qk[:, q, cols], hx[:], start=True, stop=True)
                    nc.tensor.matmul(bank[2 * q + 1][:], w.qk_half[:, q, cols], hx[:], start=True, stop=True).then_inc(s["projected"], 1)

                def norms(m):
                    pe.wait_ge(s["squared"], 8 * (n - 1) + m + 1)
                    pe.wait_ge(s["ss_read"], 8 * (n - 1) + m - 1 + 2)
                    nc.tensor.matmul(bank[6 + m % 2][:], ones_blk[:], sq[m % 2][:], start=True, stop=True).then_inc(s["ss"], 1)

                for m in range(8):
                    project(m)
                    if m:
                        norms(m - 1)
                norms(7)
                pe.sem_inc(s["projected"], 1)

                def scores(u):
                    j, hg = divmod(u, 2)
                    lo = LD if j == 0 else 0
                    if u == 0:
                        pe.wait_ge(s["qk_done"], 8 * n)
                    for k in range(2):
                        ps = score[u % 2][k]
                        for e in range(2):
                            h = head_of(hg, 2 * k + e)
                            rows = slice(LD * (h % 2), LD * (h % 2) + LD)
                            dst = ps[:, 256 * e + lo:256 * e + KW]
                            nc.tensor.matmul(dst, identb[:], masks[:, lo:KW], start=True, stop=False)
                            last = nc.tensor.matmul(dst, qf[rows, h // 2, P * j:P * j + P],
                                                    kf[rows, h // 2, P * j - LD + lo:P * j + P], start=False, stop=True)
                    last.then_inc(s["scored"], 1)

                def turn(u):
                    j = u // 2
                    pe.wait_ge(s["exped"], UNITS * (n - 1) + u + 1)
                    for hh in range(4):
                        last = nc.tensor.transpose(bank[4][:, P * hh:P * hh + P], p[u % 2][:, hh, LD:KW], c.ident[:])
                    if j:
                        for hh in range(4):
                            last = nc.tensor.transpose(bank[5][0:LD, P * hh:P * hh + P], p[u % 2][:, hh, 0:LD], c.ident[:])
                    last.then_inc(s["p_turned"], 1)

                def weigh(u):
                    j, hg = divmod(u, 2)
                    pe.wait_ge(s["ptb_copied"], UNITS * (n - 1) + u + 1)
                    pe.wait_ge(s["pta_copied"], UNITS * (n - 1) + u + 1)
                    for hh in range(4):
                        at = slice(LD * head_of(hg, hh), LD * head_of(hg, hh) + LD)
                        if j:
                            nc.tensor.matmul(bank[6][:, at], pta[u % 2][:, P * hh:P * hh + P], vh[:, j, at], start=True, stop=False)
                        last = nc.tensor.matmul(bank[6][:, at], ptb[u % 2][:, P * hh:P * hh + P], v[:, j, at], start=(j == 0), stop=True)
                    last.then_inc(s["weighed"], 1)

                def turn_out(j):
                    pe.wait_ge(s["o_normed"], NT * (n - 1) + j + 1)
                    if j:
                        pe.wait_ge(s["ot_copied"], NT * (n - 1) + j)
                    for m in range(NT):
                        last = nc.tensor.transpose(bank[7][:, P * m:P * m + P], o[:, P * m:P * m + P], c.ident[:])
                    last.then_inc(s["o_turned"], 1)

                scores(0)
                scores(1)
                for u in range(UNITS):
                    turn(u)
                    if u + 2 < UNITS:
                        scores(u + 2)
                    if u % 2 == 0 and u:
                        turn_out(u // 2 - 1)
                    weigh(u)
                turn_out(NT - 1)
                pe.wait_ge(s["ot_copied"], NT * n)
                for m in range(NT):
                    last = nc.tensor.matmul(bank[7][:], w.o[:, m], ot[:, m], start=(m == 0), stop=(m == NT - 1))
                last.then_inc(s["o_ready"], 1)

        @block.scalar
        def _(act):
            nc.scalar.preload_act_table_set(LN_EXP)
            with act.Fori(0, NB) as b:
                n = n_of(b)
                for j in range(NT):
                    act.wait_ge(s["v_ready"], NT * (n - 1) + j + 1)
                    last = nc.scalar.activation(v[:, j], bank[4 + j % 2][:], ACT.Copy)
                    if j + 1 < NT:
                        last = nc.scalar.activation(vh[:, j + 1], bank[4 + j % 2][LD:P, :], ACT.Copy)
                    last.then_inc(s["v_copied"], 1)

                def square(m):
                    act.wait_ge(s["projected"], 9 * (n - 1) + m + 1 + 1)
                    if m >= 2:
                        act.wait_ge(s["ss"], 8 * (n - 1) + m - 1)
                    nc.scalar.activation(sq[m % 2][:], bank[2 * (m % 2)][:], ACT.Square).then_inc(s["squared"], 1)

                def inverse_norm(m):
                    g = 8 * (n - 1) + m
                    act.wait_ge(s["ss_read"], g + 1 + 2)
                    if m >= 2:
                        act.wait_ge(s["qk_done"], g - 1)
                    nc.scalar.activation(rinv[m % 2][:], ssm[m % 2][:], ACT.Ln, scale=NORM_SCALE).then_inc(s["ss_log"], 1)
                    act.wait_ge(s["ss_log"], g + 1)
                    nc.scalar.activation(rinv[m % 2][:], rinv[m % 2][:], ACT.Exp, scale=-0.5).then_inc(s["rinv"], 1)

                for m in range(8):
                    square(m)
                    if m:
                        inverse_norm(m - 1)
                inverse_norm(7)

                def exps(u):
                    j = u // 2
                    lo = LD if j == 0 else 0
                    act.wait_ge(s["negmax"], UNITS * (n - 1) + u + 1)
                    for hh in range(4):
                        ps = score[u % 2][hh // 2][:, 256 * (hh % 2) + lo:256 * (hh % 2) + KW]
                        last = nc.scalar.activation(p[u % 2][:, hh, lo:KW], ps, ACT.Exp, bias=negmax[u % 2][:, hh:hh + 1],
                                                    accum_out=psum[:, j % 2, head_of(u % 2, hh):head_of(u % 2, hh) + 1])
                    last.then_inc(s["exped"], 1)

                def copy_a(u):
                    act.wait_ge(s["p_turned"], UNITS * (n - 1) + u + 1)
                    if u >= 2:
                        nc.scalar.activation(pta[u % 2][:], bank[5][0:LD, :], ACT.Copy).then_inc(s["pta_copied"], 1)
                    else:
                        act.sem_inc(s["pta_copied"], 1)

                exps(0)
                for u in range(UNITS):
                    if u + 1 < UNITS:
                        exps(u + 1)
                    copy_a(u)

        @block.vector
        def _(dve):
            dve.wait_ge(s["w_here"], 16 * N_LOADS * (l + 1))
            for k in range(4):
                nc.vector.tensor_scalar(tab[:, k], tables[:, k], w.vec[:, k:k + 1], (8.0 if k < 2 else 1.0) * NORM_SCALE ** 0.5,
                                        ALU.mult, ALU.mult).then_inc(s["tables_done"], 1)
            with dve.Fori(0, NB) as b:
                n = n_of(b)
                dve.wait_ge(s["tables_done"], 4 * (l + 1))
                for m in range(8):
                    q = m % 2
                    g = 8 * (n - 1) + m
                    dve.wait_ge(s["squared"], g + 1)
                    if m >= 2:
                        dve.wait_ge(s["summed"], g - 1)
                    nc.vector.tensor_tensor(th[q][:, 0], bank[2 * q][:], tab[:, 2 * q], ALU.mult)
                    nc.vector.tensor_tensor(th[q][:, 1], bank[2 * q + 1][:], tab[:, 2 * q + 1], ALU.mult).then_inc(s["halves"], 1)
                    dve.wait_ge(s["ss"], g + 1)
                    if m >= 2:
                        dve.wait_ge(s["ss_log"], g - 1)
                    nc.vector.tensor_scalar(ssm[q][:], bank[6 + q][:], 1e-24, None, ALU.max).then_inc(s["ss_read"], 1)

                def maxima(u):
                    lo = LD if u < 2 else 0
                    dve.wait_ge(s["scored"], UNITS * (n - 1) + u + 1)
                    for k in range(2):
                        ps = score[u % 2][k][:].rearrange("p (e t) -> p e t", e=2)[:, :, lo:KW]
                        last = nc.vector.tensor_reduce(negmax[u % 2][:, 2 * k:2 * k + 2], ps, AX_X, ALU.max, negate=True)
                    last.then_inc(s["negmax"], 1)

                def copy_b(u):
                    dve.wait_ge(s["p_turned"], UNITS * (n - 1) + u + 1)
                    nc.vector.tensor_scalar(ptb[u % 2][:], bank[4][:], 1.0, None, ALU.mult).then_inc(s["ptb_copied"], 1)

                def normalise(j):
                    dve.wait_ge(s["exped"], UNITS * (n - 1) + 2 * j + 2)
                    nc.vector.reciprocal(prec[:], psum[:, j % 2]).then_inc(s["prec"], 1)
                    dve.wait_ge(s["prec"], NT * (n - 1) + j + 1)
                    dve.wait_ge(s["weighed"], UNITS * (n - 1) + 2 * j + 2)
                    nc.vector.tensor_tensor(o[:].rearrange("p (h e) -> p h e", e=LD), bank[6][:].rearrange("p (h e) -> p h e", e=LD),
                                            prec[:].unsqueeze(2).to_broadcast([P, LH, LD]), ALU.mult).then_inc(s["o_normed"], 1)

                def copy_ot(j):
                    dve.wait_ge(s["o_turned"], NT * (n - 1) + j + 1)
                    nc.vector.tensor_scalar(ot[:, :, P * j:P * j + P], bank[7][:].rearrange("p (m t) -> p m t", m=NT),
                                            1.0, None, ALU.mult).then_inc(s["ot_copied"], 1)

                maxima(0)
                maxima(1)
                for u in range(UNITS):
                    copy_b(u)
                    if u + 2 < UNITS:
                        maxima(u + 2)
                    if u % 2 == 0 and u:
                        copy_ot(u // 2 - 1)
                    if u % 2:
                        normalise(u // 2)
                copy_ot(NT - 1)
                dve.wait_ge(s["o_ready"], n)
                nc.vector.tensor_tensor(c.resid[:, b], c.resid[:, b], bank[7][:], ALU.add).then_inc(s["added"], 1)


def local_norm(c, ph, w, l):
    nc = c.nc
    s = ph.s
    y, cent, sq = ph.b["ny"], ph.b["th"], ph.b["sq"]
    norms = ph.norms
    with nc.Block() as block:
        @block.sync
        def _(sp):
            with sp.Fori(0, NB // 2) as i:
                for p in range(2):
                    n = l * (NB // 2) + i
                    b = 2 * i + p
                    sp.wait_ge(norms[p].cent, n + 1)
                    sp.dma_start(y[p][0:LD, :], c.resid[0:LD, b]).then_inc(norms[p].y, 16)
                    sp.dma_start(y[p][LD:P, 1:T], c.resid[LD:P, b, 0:T - 1]).then_inc(norms[p].y, 16)

        @block.tensor
        def _(pe):
            with pe.Fori(0, NB // 2) as i:
                n = l * (NB // 2) + i + 1
                for p in range(2):
                    pe.wait_ge(norms[p].y, 32 * n)
                    nc.tensor.matmul(c.bank[p][:], c.ones[:], y[p][:], start=True, stop=True).then_inc(norms[p].mean, 1)
                for p in range(2):
                    pe.wait_ge(norms[p].sq, n)
                    pe.wait_ge(norms[p].out, n)
                    nc.tensor.matmul(c.bank[2 + p][:], c.ones[:], sq[p][:], start=True, stop=True).then_inc(norms[p].var, 1)

        @block.scalar
        def _(act):
            nc.scalar.preload_act_table_set(LN_EXP)
            with act.Fori(0, NB // 2) as i:
                n = l * (NB // 2) + i + 1
                for p in range(2):
                    act.wait_ge(norms[p].cent, n + 1)
                    nc.scalar.activation(sq[p][:], cent[p][:, 0], ACT.Square).then_inc(norms[p].sq, 1)
                for p in range(2):
                    var = c.bank[2 + p]
                    act.wait_ge(norms[p].var, n)
                    nc.scalar.activation(var[:], var[:], ACT.Ln, bias=c.eps[:]).then_inc(norms[p].log, 1)
                    act.wait_ge(norms[p].log, n)
                    nc.scalar.activation(var[:], var[:], ACT.Exp, scale=-0.5).then_inc(norms[p].rstd, 1)

        @block.vector
        def _(dve):
            with dve.Fori(0, NB // 2) as i:
                n = l * (NB // 2) + i + 1
                for p in range(2):
                    dve.wait_ge(norms[p].mean, n)
                    nc.vector.tensor_tensor(cent[p][:, 0], y[p][:], c.bank[p][:], ALU.subtract).then_inc(norms[p].cent, 1)
                for p in range(2):
                    dve.wait_ge(norms[p].rstd, n)
                    nc.vector.tensor_tensor(cent[p][:, 1], cent[p][:, 0], c.bank[2 + p][:], ALU.mult).then_inc(norms[p].out, 1)
                for p in range(2):
                    dve.wait_ge(norms[p].out, n + 1)
                    nc.vector.tensor_scalar(c.normed[:, 2 * i + p], cent[p][:, 1], w.vec[:, 4:5], w.vec[:, 5:6], ALU.mult, ALU.add)


def local_feed_forward(c, ph, w, l):
    nc = c.nc
    s = ph.s
    gel, hid = ph.b["gel"], ph.b["hid"]
    a_ps, g_ps, o_ps = (c.bank[0], c.bank[1]), (c.bank[2], c.bank[3]), (c.bank[4], c.bank[5])
    STEPS = 6

    with nc.Block() as block:
        @block.tensor
        def _(pe):
            with pe.Fori(0, NB // 2) as i:
                pair = l * (NB // 2) + i

                def up(k):
                    bb, ch = divmod(k, 3)
                    at, rows = HC[ch]
                    x = c.normed[:, 2 * i + bb]
                    pe.wait_ge(s["gated"], STEPS * pair + k - 1 + 2)
                    nc.tensor.matmul(a_ps[k % 2][0:rows, :], w.w1[:, at:at + rows], x, start=True, stop=True)
                    nc.tensor.matmul(g_ps[k % 2][0:rows, :], w.w1[:, HID + at:HID + at + rows], x, start=True, stop=True).then_inc(s["up"], 1)

                def down(k):
                    bb, ch = divmod(k, 3)
                    rows = HC[ch][1]
                    pe.wait_ge(s["gated"], STEPS * pair + k + 1 + 2)
                    if ch == 0:
                        pe.wait_ge(s["f_added"], 2 * pair + bb + 1)
                    last = nc.tensor.matmul(o_ps[bb][:], w.w2[0:rows, ch], hid[k % 3][0:rows, :], start=(ch == 0), stop=(ch == 2))
                    if ch == 2:
                        last.then_inc(s["down"], 1)

                for k in range(STEPS):
                    up(k)
                    if k:
                        down(k - 1)
                down(STEPS - 1)

        @block.scalar
        def _(act):
            with act.Fori(0, NB // 2) as i:
                for k in range(STEPS):
                    ch = k % 3
                    rows = HC[ch][1]
                    act.wait_ge(s["up"], STEPS * (l * (NB // 2) + i) + k + 1)
                    nc.scalar.activation(gel[k % 2][0:rows, :], g_ps[k % 2][0:rows, :], ACT.Gelu,
                                         bias=w.vec[0:rows, 9 + ch:10 + ch]).then_inc(s["gelu"], 1)

        @block.vector
        def _(dve):
            with dve.Fori(0, NB // 2) as i:
                pair = l * (NB // 2) + i

                def add(bb):
                    dve.wait_ge(s["down"], 2 * pair + bb + 1)
                    x = c.resid[:, 2 * i + bb]
                    nc.vector.scalar_tensor_tensor(out=x, in0=o_ps[bb][:], scalar=w.vec[:, 12:13], in1=x,
                                                   op0=ALU.add, op1=ALU.add).then_inc(s["f_added"], 1)

                for k in range(STEPS):
                    ch = k % 3
                    rows = HC[ch][1]
                    dve.wait_ge(s["gelu"], STEPS * pair + k + 1)
                    nc.vector.scalar_tensor_tensor(out=hid[k % 3][0:rows, :], in0=a_ps[k % 2][0:rows, :],
                                                   scalar=w.vec[0:rows, 6 + ch:7 + ch], in1=gel[k % 2][0:rows, :],
                                                   op0=ALU.add, op1=ALU.mult).then_inc(s["gated"], 1)
                    if k == 3:
                        add(0)
                add(1)


def phase_local(c, d):
    nc = c.nc
    with ExitStack() as ctx:
        ph = Phase(c, ctx)
        w = LocalWeights(ph)
        tables = ph.sb("l_tables", [P, 4, T])
        tab = ph.sb("l_tab", [P, 4, T])
        masks = ph.sb("l_masks", [P, KW], BF16)
        identb = ph.sb("l_identb", [P, P], BF16)
        qf, kf = ph.sb("l_q", [P, NT, T]), ph.sb("l_k", [P, NT, T])
        ph.b = dict(
            hx=ph.sb("l_hx", [P, T]), ones_blk=ph.sb("l_ones_blk", [P, P]),
            sq=[ph.sb(f"l_sq{k}", [P, T]) for k in range(2)], rinv=[ph.sb(f"l_rinv{k}", [P, T]) for k in range(2)],
            ssm=[ph.sb(f"l_ssm{k}", [P, T]) for k in range(2)],
            th=[ph.sb(f"l_th{k}", [P, 2, T]) for k in range(2)], tsum=[ph.sb(f"l_tsum{k}", [P, T]) for k in range(2)],
            v=ph.sb("l_v", [P, NT, INNER]), vh=ph.sb("l_vh", [LD, NT, INNER]),
            p=[ph.sb(f"l_p{k}", [P, 4, KW]) for k in range(2)], ptb=[ph.sb(f"l_ptb{k}", [P, 4 * P]) for k in range(2)],
            pta=[ph.sb(f"l_pta{k}", [LD, 4 * P]) for k in range(2)], negmax=[ph.sb(f"l_negmax{k}", [P, 4]) for k in range(2)],
            psum=ph.sb("l_psum", [P, 2, LH]), prec=ph.sb("l_prec", [P, LH]), o=ph.sb("l_o", [P, INNER]),
            ot=ph.sb("l_ot", [P, NT, T]), ny=[ph.sb(f"l_ny{k}", [P, T]) for k in range(2)],
            gel=[ph.sb(f"l_gel{k}", [P, T]) for k in range(2)], hid=[ph.sb(f"l_hid{k}", [P, T]) for k in range(3)])
        ph.s = {n: ph.sem(f"p5_{n}") for n in (
            "loaded", "w_here", "hx_here", "tables_done", "v_ready", "v_copied", "projected", "squared", "ss", "ss_read",
            "ss_log", "rinv", "halves", "summed", "qk_done", "scored", "negmax", "exped", "p_turned", "ptb_copied",
            "pta_copied", "weighed", "prec", "o_normed", "o_turned", "ot_copied", "o_ready", "added",
            "up", "gelu", "gated", "down", "f_added")}
        ph.norms = [NormSems(ph.sem, f"p5n{p}") for p in range(2)]
        s = ph.s
        with nc.Block() as block:
            @block.sync
            def _(sp):
                for dst, name in ((tables, "l_tables"), (masks, "l_masks"), (identb, "l_identb"), (ph.b["ones_blk"], "l_ones_blk")):
                    sp.dma_start(dst[:], d[name]).then_inc(s["loaded"], 16)
                sp.wait_ge(s["loaded"], 64)

            @block.gpsimd
            def _(pool):
                nc.gpsimd.memset(ph.b["hx"][:], 0.0)
                nc.gpsimd.memset(ph.b["ny"][0][:], 0.0)
                nc.gpsimd.memset(ph.b["ny"][1][:], 0.0)

            @block.vector
            def _(dve):
                dve.sem_inc(s["projected"], 1)
                dve.sem_inc(s["halves"], 2)
                dve.sem_inc(s["ss_read"], 2)
                dve.sem_inc(s["added"], 1)
                dve.sem_inc(s["gated"], 2)
                dve.sem_inc(s["f_added"], 2)
                for p in range(2):
                    dve.sem_inc(ph.norms[p].cent, 1)
                    dve.sem_inc(ph.norms[p].out, 1)

        with nc.Fori(0, DEPTH) as l:
            local_attention(c, d, ph, w, l, tab, tables, masks, identb, kf, qf)
            local_norm(c, ph, w, l)
            local_feed_forward(c, ph, w, l)


def phase_local_attention(c, d):
    nc = c.nc
    with ExitStack() as ctx:
        with nc.Block() as block:
            @block.gpsimd
            def _(pool):
                nc.gpsimd.tensor_copy(c.outer[:], c.resid[:])
        phase_local(c, d)
        with nc.Block() as block:
            @block.vector
            def _(dve):
                for b in range(NB):
                    nc.vector.tensor_tensor(c.resid[:, b], c.resid[:, b], c.outer[:, b], ALU.add)
    phase_norm(c, "last_norm")


def rel_heads_padded(w):
    out = np.zeros((4, P, P), w.dtype)
    for g in range(4):
        for r in range(4):
            h = 4 * g + r
            out[g, :, 32 * r + 1:32 * r + 9] = w[:, 8 * h:8 * h + 8]
    return out


def lay_out(i):
    d = {}
    d["x"] = i["L0_attn_x"].transpose(0, 2, 1)
    w_in = i["L0_attn_w_in"].reshape(16, 3, 8, P)
    b_in = i["L0_attn_b_in"].reshape(16, 3, 8)
    d["wv0"] = w_in[:, 2].reshape(P, P).T
    d["bv0"] = b_in[:, 2].reshape(P, 1)
    d["wo0"] = i["L0_attn_w_out"].T
    d["bo0"] = i["L0_attn_b_out"].reshape(P, 1)
    d["ln1_g"] = i["L0_ffn_ln1_g"].reshape(P, 1)
    d["ln1_b"] = i["L0_ffn_ln1_b"].reshape(P, 1)
    d["ident"] = np.eye(P, dtype=np.float32)
    wp = i["L0_ffn_wp"]
    swapped = np.concatenate([wp[64:], wp[:64]], axis=0)
    q_pad, k_pad = rel_heads_padded(i["L0_ffn_wq"]), rel_heads_padded(i["L0_ffn_wk"])
    a_pad = rel_heads_padded(wp).transpose(0, 2, 1)
    b_pad = rel_heads_padded(swapped).transpose(0, 2, 1)
    wv = i["L0_ffn_wv"].reshape(P, 4, 32).transpose(1, 0, 2)
    d["rel_w"] = np.concatenate([q_pad, k_pad, a_pad, b_pad, wv], axis=2)
    wo = np.zeros((4, 4, 32, P), np.float32)
    wo[:, :, 0:8] = i["L0_ffn_wo"].reshape(4, 4, 8, P)
    d["rel_wo"] = wo.reshape(4, P, P)
    freq = (1.0 / 10000.0 ** (np.arange(0, P, 2, dtype=np.float32) / np.float32(P))).astype(np.float32)
    angle = freq.astype(np.float64)[:, None] * np.arange(T)[None, :]
    sin, cos = np.sin(angle).astype(np.float32), np.cos(angle).astype(np.float32)
    d["rel_cos"] = np.concatenate([cos, cos])
    d["rel_sin"] = np.concatenate([sin, -sin])
    d["rel_angle"] = np.concatenate([sin, cos])
    k_ones = np.zeros((P, 1), np.float32)
    k_ones[0::32] = 1.0
    d["rel_k_ones"] = k_ones
    pick = np.zeros((4, 32, 4, 32), np.float32)
    for r in range(4):
        pick[r, 8, r, :] = 1.0
    d["rel_pick_sum"] = pick.reshape(P, P)
    v_aug = np.zeros((P, NT, 4, 32), np.float32)
    v_aug[..., 8] = 1.0
    d["rel_v_aug"] = v_aug
    d["ln2_g"] = i["L0_ffn_ln2_g"].reshape(P, 1)
    d["ln2_b"] = i["L0_ffn_ln2_b"].reshape(P, 1)
    d["sel_w"] = i["L0_ffn_sel_w"]
    d["keys"] = i["L0_ffn_keys"]
    d["values"] = i["L0_ffn_values"]
    pick_expert = np.zeros((NE, 3, NE, P), mybir.dt.np(BF16))
    for e in range(NE):
        pick_expert[e, :, e] = 1.0
    d["pick_expert"] = pick_expert.reshape(NE, 3 * NE, P)
    w = i["L1_attn_W_in"]
    at = np.cumsum([0, DI, DI, DS, DS, NH, NH, NH, DS // 2])
    z, x, bp, cp, dd_dt, dd_a, trap, ang = (w[:, at[n]:at[n + 1]] for n in range(8))
    w_rows = np.zeros((P, 3, NB, NB, NH), np.float32)
    for q, part in enumerate((dd_dt, dd_a, trap)):
        for b in range(NB):
            w_rows[:, q, b, b] = part
    d["ss_w_rows"] = w_rows.reshape(P, 3, NB, NR)
    d["ss_dt_bias"] = np.tile(i["L1_attn_dt_bias"], NB).reshape(NR, 1)
    d["ss_w_angle"] = np.tile(ang, (1, 4))
    pairs = lambda a: np.concatenate([a[..., 0::2], a[..., 1::2]], axis=-1)
    d["ss_w_bc"] = np.concatenate([pairs(bp), pairs(cp)], axis=1)
    d["ss_gain"] = np.concatenate([pairs(i["L1_attn_Bn_g"]), pairs(i["L1_attn_Cn_g"])]).reshape(P, 1)
    d["ss_shift"] = np.concatenate([pairs(i["L1_attn_Bn_b"]), pairs(i["L1_attn_Cn_b"])]).reshape(P, 1)
    d["ss_w_zx"] = np.concatenate([z, x], axis=1)
    d["ss_w_out"] = i["L1_attn_W_out"].reshape(2, P, P).transpose(1, 0, 2)
    d["ss_d"] = np.broadcast_to(i["L1_attn_D_param"], (P, NT, NH))
    sign = np.ones((4, 32), np.float32)
    sign[0::2] = -1.0
    d["ss_sign"] = sign.reshape(P, 1)
    pick = np.zeros((NB, NB, NH, NH + 1, P), np.float32)
    for b in range(NB):
        for h in range(NH):
            pick[b, b, h, h] = 1.0
        pick[b, b, :, NH] = 1.0 / NH
    d["ss_pick"] = pick.reshape(NB, NR, (NH + 1) * P)
    d["ones64"] = np.kron(np.eye(2, dtype=np.float32), np.full((DS, DS), 1.0 / DS, np.float32))
    swap = np.zeros((P, P), np.float32)
    swap[np.arange(P) ^ 32, np.arange(P)] = 1.0
    d["ss_swap"] = swap
    d["ss_later"] = np.where(np.arange(P)[None, :] > np.arange(P)[:, None], 0.0, NEG).astype(np.float32)
    w = i["L1_ffn_wqkv"]
    halves = lambda a: a.reshape(DEPTH, -1, LH, 2, LD // 2)[:, :, :, ::-1].reshape(DEPTH, -1, INNER)
    d["l_wqk"] = w[:, :, 0:2 * INNER].reshape(DEPTH, P, 2, INNER)
    d["l_wqk_half"] = np.stack([halves(w[:, :, 0:INNER]), halves(w[:, :, INNER:2 * INNER])], axis=2)
    d["l_wv"] = w[:, :, 2 * INNER:]
    d["l_wo"] = i["L1_ffn_wo"].reshape(DEPTH, NT, P, P).transpose(0, 2, 1, 3)
    d["l_w1"] = i["L1_ffn_w1"]
    w2 = np.zeros((DEPTH, 3 * P, P), np.float32)
    w2[:, 0:HID] = i["L1_ffn_w2"]
    d["l_w2"] = w2.reshape(DEPTH, 3, P, P).transpose(0, 2, 1, 3)
    vec = np.zeros((DEPTH, P, 13), np.float32)
    for k, g in enumerate((i["L1_ffn_q_scale"], i["L1_ffn_k_scale"])):
        vec[:, :, 2 * k] = np.tile(g, (1, 2))
        vec[:, :, 2 * k + 1] = np.tile(np.roll(g, LD // 2, axis=1), (1, 2))
    vec[:, :, 4] = i["L1_ffn_ln_g"]
    vec[:, :, 5] = i["L1_ffn_ln_b"]
    for ch, (at, rows) in enumerate(HC):
        vec[:, 0:rows, 6 + ch] = i["L1_ffn_b1"][:, at:at + rows]
        vec[:, 0:rows, 9 + ch] = i["L1_ffn_b1"][:, HID + at:HID + at + rows]
    vec[:, :, 12] = i["L1_ffn_b2"]
    d["l_vec"] = vec
    half = np.arange(0, LD, 2, dtype=np.float32)
    freq = (1.0 / 10000.0 ** (half / np.float32(LD))).astype(np.float32).astype(np.float64)
    t = np.arange(T, dtype=np.float64)
    base = (half.astype(np.float64) + 0.4 * LD) / (1.4 * LD)
    scale = base[:, None] ** ((t[None, :] - T // 2) / (LD // 2))
    cos, sin = np.cos(freq[:, None] * t), np.sin(freq[:, None] * t)
    tables = np.zeros((P, 4, T), np.float32)
    for k, f in enumerate((scale, 1.0 / scale)):
        tables[:, 2 * k] = np.tile(cos * f, (4, 1))
        tables[:, 2 * k + 1] = np.concatenate([-sin * f, sin * f, -sin * f, sin * f])
    d["l_tables"] = tables
    col, row = np.arange(KW)[None, :], np.arange(P)[:, None]
    d["l_masks"] = np.where((col >= row) & (col <= row + LD), 0.0, NEG).astype(mybir.dt.np(BF16))
    d["l_identb"] = np.eye(P).astype(mybir.dt.np(BF16))
    d["l_ones_blk"] = np.kron(np.eye(2, dtype=np.float32), np.ones((LD, LD), np.float32))
    return d



def build(nc, d, out):
    with ExitStack() as ctx:
        c = Core(nc, ctx)
        phase_first_attention(c, d)
        phase_relative_attention(c, d)
        phase_experts(c, d)
        phase_state_space(c, d)
        phase_local_attention(c, d)
        store(c, out)


def store(c, out):
    nc = c.nc
    with ExitStack() as ctx:
        stored = Phase(c, ctx).sem("stored")
        with nc.Block() as block:
            @block.sync
            def _(sp):
                sp.dma_start(out.rearrange("b p t -> p b t"), c.resid[:]).then_inc(stored, 16)
                sp.wait_ge(stored, 16)


def kernel(**inputs):
    import numpy as _np
    import concourse.bacc as _bacc
    from concourse import mybir as _mybir
    from concourse.bass_utils import run_bass_kernel_spmd as _run

    arrays = lay_out({k: _np.asarray(v) for k, v in inputs.items()})
    nc = _bacc.Bacc("TRN2", target_bir_lowering=False, num_devices=1)
    feeds, d = {}, {}
    for name, a in arrays.items():
        a = _np.ascontiguousarray(a)
        feeds[f"in_{name}"] = a
        d[name] = nc.dram_tensor(f"in_{name}", a.shape, _mybir.dt.from_np(a.dtype), kind="ExternalInput").ap()
    out = nc.dram_tensor("out_0", (NB, P, T), F32, kind="ExternalOutput").ap()
    build(nc, d, out)
    r = _run(nc, [feeds], core_ids=[0])
    return _np.ascontiguousarray(r.results[0]["out_0"].transpose(0, 2, 1))
```

```python
from contextlib import ExitStack

import numpy as np

import concourse.bass as bass
from concourse import mybir

ALU = mybir.AluOpType
ACT = mybir.ActivationFunctionType
F32 = mybir.dt.float32
BF16 = mybir.dt.bfloat16
F16 = mybir.dt.float16
LN_EXP = "natural_log_exp_and_others"
AX_X = mybir.AxisListType.X

P = 128
NB = 8
T = 512
NT = T // P
EPS = 1e-5


class NormSems:
    def __init__(self, sem, name):
        self.y = sem(f"{name}_y_ready")
        self.mean = sem(f"{name}_mean_ready")
        self.cent = sem(f"{name}_centred")
        self.sq = sem(f"{name}_squared")
        self.var = sem(f"{name}_var_ready")
        self.log = sem(f"{name}_log_var")
        self.rstd = sem(f"{name}_rstd")
        self.out = sem(f"{name}_out")


def norm_pe(nc, pe, s, n, ones, y, sq, mean_ps, var_ps):
    pe.wait_ge(s.y, n)
    nc.tensor.matmul(mean_ps, ones, y, start=True, stop=True).then_inc(s.mean, 1)
    pe.wait_ge(s.sq, n)
    nc.tensor.matmul(var_ps, ones, sq, start=True, stop=True).then_inc(s.var, 1)


def norm_act(nc, act, s, n, cent, sq, var_ps, eps):
    act.wait_ge(s.cent, n)
    nc.scalar.activation(sq, cent, ACT.Square).then_inc(s.sq, 1)
    act.wait_ge(s.var, n)
    nc.scalar.activation(var_ps, var_ps, ACT.Ln, bias=eps).then_inc(s.log, 1)
    act.wait_ge(s.log, n)
    nc.scalar.activation(var_ps, var_ps, ACT.Exp, scale=-0.5).then_inc(s.rstd, 1)


def norm_dve(nc, dve, s, n, y, cent, mean_ps, var_ps, out):
    dve.wait_ge(s.mean, n)
    nc.vector.tensor_tensor(cent, y, mean_ps, ALU.subtract).then_inc(s.cent, 1)
    dve.wait_ge(s.rstd, n)
    nc.vector.tensor_tensor(out, cent, var_ps, ALU.mult).then_inc(s.out, 1)


class Core:

    def __init__(self, nc, ctx):
        self.nc = nc
        self.ctx = ctx
        self.psum = ctx.enter_context(nc.psum_tensor("psum", [P, 8, 512], F32))
        self.bank = [self.psum[:, i] for i in range(8)]
        self.resid = self.sb("resid", [P, NB, T])
        self.normed = self.sb("normed", [P, NB, T])
        self.outer = self.sb("outer", [P, NB, T])
        self.ones = self.sb("ones_mean", [P, P])
        self.eps = self.sb("eps", [P, 1])
        self.ident = self.sb("ident", [P, P])

    def sb(self, name, shape, dt=F32):
        return self.ctx.enter_context(self.nc.sbuf_tensor(name, shape, dt))


class Phase:

    def __init__(self, core, ctx):
        self.nc, self.ctx, self.sems = core.nc, ctx, []
        ctx.callback(self.clear)

    def sb(self, name, shape, dt=F32):
        return self.ctx.enter_context(self.nc.sbuf_tensor(name, shape, dt))

    def sem(self, name):
        s = self.nc.alloc_semaphore(name)
        self.sems.append(s)
        return s

    def clear(self):
        nums = sorted(s.num for s in self.sems)
        with self.nc.Block() as block:
            @block.sync
            def _(sp):
                at = 0
                while at < len(nums):
                    end = at
                    while end + 1 < len(nums) and nums[end + 1] == nums[end] + 1:
                        end += 1
                    sp.sem_clear(range(nums[at], nums[end] + 1))
                    at = end + 1
        for s in self.sems:
            self.nc.release_semaphore(s)


def phase_first_attention(c, d):
    nc = c.nc
    with ExitStack() as ctx:
        ph = Phase(c, ctx)
        wv = ph.sb("wv0", [P, P])
        wo = ph.sb("wo0", [P, P])
        vec = ph.sb("vec0", [P, 4])
        v_sb = ph.sb("v0_sb", [P, T])
        y = ph.sb("y0", [P, T])
        cent = ph.sb("cent0", [P, T])
        sq = ph.sb("sq0", [P, T])
        bias_v, bias_o, gain, shift = (vec[:, i:i + 1] for i in range(4))
        loaded = ph.sem("p1_loaded")
        ones_set = ph.sem("p1_ones_set")
        v_ready, v_biased, o_ready = ph.sem("p1_v"), ph.sem("p1_v_biased"), ph.sem("p1_o")
        na, nb_ = NormSems(ph.sem, "p1a"), NormSems(ph.sem, "p1b")
        affine = ph.sem("p1_affine")
        v_ps, o_ps, mean_ps, var_ps = (c.bank[i] for i in range(4))
        N_LOADS = 8

        with nc.Block() as block:
            @block.sync
            def _(sp):
                sp.dma_start(c.resid[:], d["x"].rearrange("b p t -> p b t")).then_inc(loaded, 16)
                sp.dma_start(wv[:], d["wv0"]).then_inc(loaded, 16)
                sp.dma_start(wo[:], d["wo0"]).then_inc(loaded, 16)
                sp.dma_start(vec[:, 0:1], d["bv0"]).then_inc(loaded, 16)
                sp.dma_start(vec[:, 1:2], d["bo0"]).then_inc(loaded, 16)
                sp.dma_start(vec[:, 2:3], d["ln1_g"]).then_inc(loaded, 16)
                sp.dma_start(vec[:, 3:4], d["ln1_b"]).then_inc(loaded, 16)
                sp.dma_start(c.ident[:], d["ident"]).then_inc(loaded, 16)

            @block.gpsimd
            def _(pool):
                nc.gpsimd.memset(c.ones[:], 1.0 / P).then_inc(ones_set, 1)
                nc.gpsimd.memset(c.eps[:], EPS).then_inc(ones_set, 1)

            @block.tensor
            def _(pe):
                pe.wait_ge(loaded, 16 * N_LOADS)
                pe.wait_ge(ones_set, 2)
                with pe.Fori(0, NB) as b:
                    nc.tensor.matmul(v_ps[:], wv[:], c.resid[:, b], start=True, stop=True).then_inc(v_ready, 1)
                    pe.wait_ge(v_biased, b + 1)
                    nc.tensor.matmul(o_ps[:], wo[:], v_sb[:], start=True, stop=True).then_inc(o_ready, 1)
                    norm_pe(nc, pe, na, b + 1, c.ones[:], y[:], sq[:], mean_ps[:], var_ps[:])
                    norm_pe(nc, pe, nb_, b + 1, c.ones[:], y[:], sq[:], mean_ps[:], var_ps[:])

            @block.scalar
            def _(act):
                nc.scalar.preload_act_table_set(LN_EXP)
                act.wait_ge(loaded, 16 * N_LOADS)
                act.wait_ge(ones_set, 2)
                with act.Fori(0, NB) as b:
                    act.wait_ge(v_ready, b + 1)
                    nc.scalar.activation(v_sb[:], v_ps[:], ACT.Identity, bias=bias_v).then_inc(v_biased, 1)
                    norm_act(nc, act, na, b + 1, cent[:], sq[:], var_ps[:], c.eps[:])
                    norm_act(nc, act, nb_, b + 1, cent[:], sq[:], var_ps[:], c.eps[:])

            @block.vector
            def _(dve):
                dve.wait_ge(loaded, 16 * N_LOADS)
                with dve.Fori(0, NB) as b:
                    dve.wait_ge(o_ready, b + 1)
                    nc.vector.scalar_tensor_tensor(out=y[:], in0=o_ps[:], scalar=bias_o, in1=c.resid[:, b],
                                                   op0=ALU.add, op1=ALU.add).then_inc(na.y, 1)
                    norm_dve(nc, dve, na, b + 1, y[:], cent[:], mean_ps[:], var_ps[:], y[:])
                    dve.wait_ge(na.out, b + 1)
                    nc.vector.tensor_scalar(c.outer[:, b], y[:], 1.0, None, ALU.mult)
                    nc.vector.tensor_scalar(c.resid[:, b], y[:], 1.0, None, ALU.mult).then_inc(nb_.y, 1)
                    norm_dve(nc, dve, nb_, b + 1, y[:], cent[:], mean_ps[:], var_ps[:], cent[:])
                    dve.wait_ge(nb_.out, b + 1)
                    nc.vector.tensor_scalar(c.normed[:, b], cent[:], gain, shift, ALU.mult, ALU.add).then_inc(affine, 1)


HG = 4
TURNS = NB * 4
HR = 64
SLOT = 9
Q_PART = (0, 0, 1, 0, 2, 1)
K_PART = (0, 1, 0, 2, 0, 1)
W_Q, W_K, W_V = 0, 2 * P, 4 * P
W_COLS = 4 * P + 32


def first(u):
    return isinstance(u, int) and u == 0


def phase_relative_attention(c, d):
    nc = c.nc
    SCALE = 8.0 ** -0.5
    with ExitStack() as ctx:
        ph = Phase(c, ctx)
        cos_q = ph.sb("cos_q", [P, T])
        sin_q = ph.sb("sin_q", [P, T])
        angle_k = ph.sb("angle_k", [P, T])
        angle_kb = ph.sb("angle_kb", [P, T], BF16)
        part_vec = ph.sb("part_vec", [P, 5])
        q_less_h, q_less_m, k_less_h, k_less_m, k_ones = (part_vec[:, n:n + 1] for n in range(5))
        pick_sum = ph.sb("pick_sum", [P, P])
        wp_raw = ph.sb("wp_raw", [P, 4, 4 * P])
        wp_h = ph.sb("wp_h", [P, 4, 4 * P], BF16)
        wp_parts = ph.sb("wp_parts", [P, 4, 4 * P], BF16)
        w = [ph.sb(f"w_group{p}", [P, W_COLS]) for p in range(2)]
        wp = [ph.sb(f"wp_group{p}", [P, 4 * P], BF16) for p in range(2)]
        wo = [ph.sb(f"wo_group{p}", [P, P]) for p in range(2)]
        xs = [ph.sb(f"x_staged{p}", [P, T]) for p in range(2)]
        h6 = ph.sb("split_h", [P, 2, T], BF16)
        rest = ph.sb("split_rest", [P, 2, T])
        m6 = ph.sb("split_m", [P, 2, T], BF16)
        qs = [ph.sb(f"q_parts{p}", [P, 2, T], BF16) for p in range(2)]
        ks = [ph.sb(f"k_parts{p}", [P, 2, T], BF16) for p in range(2)]
        v_rest = ph.sb("v_rest", [P, NT, HG, 8])
        v_m = ph.sb("v_m", [P, NT, HG, 8], BF16)
        v_h = ph.sb("v_h", [P, NT, HG, 8], BF16)
        vaug = [ph.sb(f"v_aug{p}", [P, NT, HG, 32], BF16) for p in range(2)]
        half = ph.sb("turned_halves", [P, 2, 2, T])
        rot = [ph.sb(f"rot{p}", [P, HG, T]) for p in range(2)]
        rotb = ph.sb("rot_bf", [P, HG, T], BF16)
        mx = ph.sb("mx", [P, NT, HG])
        mx_rest = ph.sb("mx_rest", [P, NT, HG])
        mx_part = ph.sb("mx_part", [P, 2, NT, HG], BF16)
        max_wide = ph.sb("max_wide", [P, NT, 2, 2, HR])
        p32 = ph.sb("p32", [P, 4, T])
        p_hi = ph.sb("p_hi", [P, 2, NT, T], F16)
        p_lo = ph.sb("p_lo", [P, 2, NT, T], F16)
        av = ph.sb("av", [P, T])
        rden = ph.sb("rden", [P, T])
        avn = ph.sb("av_normed", [P, T])

        score_ps = c.bank[0:2]
        av_ps, a_ps, b_ps, misc_ps = c.bank[2], c.bank[3], c.bank[4], c.bank[5]
        rough_ps = c.bank[6:8]

        tables = ph.sem("p2_tables")
        set_up = ph.sem("p2_set_up")
        wp_split = ph.sem("p2_wp_split")
        w_here = [ph.sem(f"p2_w_here{p}") for p in range(2)]
        wo_here = [ph.sem(f"p2_wo_here{p}") for p in range(2)]
        qk_ready = ph.sem("p2_qk_ready")
        v_ready = ph.sem("p2_v")
        h_done, rest_done, m_done = ph.sem("p2_h_done"), ph.sem("p2_rest_done"), ph.sem("p2_m_done")
        parts_done = ph.sem("p2_parts_done")
        v_chain, v_done = ph.sem("p2_v_chain"), ph.sem("p2_v_done")
        turned = ph.sem("p2_turned")
        halves = ph.sem("p2_halves")
        rot_ready = ph.sem("p2_rot")
        rotb_ready = ph.sem("p2_rotb")
        rough = ph.sem("p2_rough")
        maxed = ph.sem("p2_maxed")
        mx_chain, mx_wide = ph.sem("p2_mx_chain"), ph.sem("p2_mx_wide")
        max_turned = ph.sem("p2_max_turned")
        q_final = ph.sem("p2_q_final")
        scored = ph.sem("p2_scored")
        exped = ph.sem("p2_exped")
        hi_done, lo_done = ph.sem("p2_hi_done"), ph.sem("p2_lo_done")
        av_ready, av_copied = ph.sem("p2_av"), ph.sem("p2_av_copied")
        den_ready, den_log, den_inv = ph.sem("p2_den"), ph.sem("p2_den_log"), ph.sem("p2_den_inv")
        avn_ready, o_ready = ph.sem("p2_avn"), ph.sem("p2_o")
        added = ph.sem("p2_added")
        N_TABLES = 8
        MX_STEPS = 4

        with nc.Block() as block:
            @block.sync
            def _(sp):
                sp.dma_start(cos_q[:], d["rel_cos"]).then_inc(tables, 16)
                sp.dma_start(sin_q[:], d["rel_sin"]).then_inc(tables, 16)
                sp.dma_start(angle_k[:], d["rel_angle"]).then_inc(tables, 16)
                sp.dma_start(part_vec[:], d["rel_part_vec"]).then_inc(tables, 16)
                sp.dma_start(pick_sum[:], d["rel_pick_sum"]).then_inc(tables, 16)
                sp.dma_start(wp_raw[:], d["rel_wp"]).then_inc(tables, 16)
                sp.dma_start(vaug[0][:], d["rel_v_aug"]).then_inc(tables, 16)
                sp.dma_start(vaug[1][:], d["rel_v_aug"]).then_inc(tables, 16)

                def load_w(u, p):
                    sp.dma_start(w[p][:], d["rel_w"][u % 4]).then_inc(w_here[p], 16)
                    sp.dma_start(xs[p][:], c.normed[:, (u // 4) % NB]).then_inc(w_here[p], 16)
                    sp.dma_start(wp[p][:], wp_parts[:, u % 4]).then_inc(w_here[p], 16)

                def load_wo(t, p):
                    sp.dma_start(wo[p][:], d["rel_wo"][t % 4]).then_inc(wo_here[p], 16)

                sp.wait_ge(wp_split, 4)
                for p in range(2):
                    load_w(p, p)
                    load_wo(p, p)
                with sp.Fori(0, TURNS // 2 - 1) as i:
                    for p in range(2):
                        t = 2 * i + p
                        sp.wait_ge(turned, HG * (t + 1))
                        load_w(t + 2, p)
                        sp.wait_ge(o_ready, t + 1)
                        load_wo(t + 2, p)

            @block.gpsimd
            def _(pool):
                nc.gpsimd.memset(max_wide[:], 0.0).then_inc(set_up, 1)
                pool.sem_inc(lo_done, 4)

                def turn(u, p, r):
                    pool.wait_ge(halves, HG * u + r + 1)
                    nc.gpsimd.tensor_tensor(rot[p][:, r], half[:, r % 2, 0], half[:, r % 2, 1], ALU.add).then_inc(rot_ready, 1)

                def low_parts(t, r, tiles=range(NT)):
                    for j in tiles:
                        pool.wait_ge(hi_done, 16 * t + 4 * r + j + 1)
                        nc.gpsimd.tensor_tensor(p_lo[:, r % 2, j], p32[:, j], p_hi[:, r % 2, j], ALU.subtract).then_inc(lo_done, 1)

                def step(t, p):
                    u, n = t + 1, 1 - p
                    turn(u, n, 0)
                    low_parts(t, 1, (0, 1))
                    turn(u, n, 1)
                    low_parts(t, 1, (2, 3))
                    low_parts(t, 2, (0, 1))
                    turn(u, n, 2)
                    low_parts(t, 2, (2, 3))
                    turn(u, n, 3)
                    low_parts(t, 3)
                    low_parts(u, 0)

                for r in range(HG):
                    turn(0, 0, r)
                low_parts(0, 0)
                with pool.Fori(0, TURNS // 2 - 1) as i:
                    step(2 * i, 0)
                    step(2 * i + 1, 1)
                step(TURNS - 2, 0)
                for r in range(1, HG):
                    low_parts(TURNS - 1, r)

            @block.tensor
            def _(pe):
                pe.wait_ge(tables, 16 * N_TABLES)
                pe.wait_ge(set_up, 2)

                def rows_of(r):
                    return slice(HR * (r % 2), HR * (r % 2) + HR)

                def project_q(u, i, p):
                    pe.wait_ge(w_here[p], 48 * (i + 1))
                    if not first(u):
                        pe.wait_ge(halves, HG * u)
                    for tt, ps in enumerate((a_ps, b_ps)):
                        nc.tensor.matmul(ps, w[p][:, W_Q + P * tt:W_Q + P * tt + P], xs[p][:], start=True, stop=True).then_inc(qk_ready, 1)

                def project_kv(u, p):
                    pe.wait_ge(halves, HG * u + 2)
                    for tt, ps in enumerate((a_ps, b_ps)):
                        nc.tensor.matmul(ps, w[p][:, W_K + P * tt:W_K + P * tt + P], xs[p][:], start=True, stop=True).then_inc(qk_ready, 1)
                    for j in range(NT):
                        last = nc.tensor.matmul(misc_ps[:, 32 * j:32 * j + 32], xs[p][:, P * j:P * j + P],
                                                w[p][:, W_V:W_V + 32], start=True, stop=True)
                    last.then_inc(v_ready, 1)

                def turn(u, p, r):
                    if r % 2 == 0:
                        pe.wait_ge(parts_done, 4 * u + 2 + r)
                    else:
                        pe.wait_ge(halves, HG * u + r)
                    for n, ps in enumerate((a_ps, b_ps)):
                        at = 2 * P * (r // 2) + P * n
                        last = nc.tensor.matmul(ps, wp[p][rows_of(r), at:at + P], qs[p][rows_of(r), r // 2], start=True, stop=True)
                    last.then_inc(turned, 1)

                def rough_scores(u, p, r, tiles=range(NT)):
                    pe.wait_ge(rotb_ready, HG * u + r + 1)
                    for k in tiles:
                        pe.wait_ge(maxed, 16 * u + 4 * r + k + 1)
                        q_tile = slice(P * k, P * k + P)
                        ps = rough_ps[k % 2]
                        nc.tensor.matmul(ps, rotb[:, r, q_tile], angle_kb[:], start=True, stop=False)
                        nc.tensor.matmul(ps, qs[p][rows_of(r), r // 2, q_tile], ks[p][rows_of(r), r // 2],
                                         start=False, stop=True).then_inc(rough, 1)

                def turn_maxima(u):
                    pe.wait_ge(mx_wide, u + 1)
                    for tt, ps in enumerate(rough_ps):
                        for k in range(NT):
                            last = nc.tensor.transpose(ps[:, P * k:P * k + P], max_wide[:, k, tt].rearrange("p a b -> p (a b)"), c.ident[:])
                    last.then_inc(max_turned, 1)

                def scores(t, p, r, tiles=range(NT)):
                    if r == 0:
                        pe.wait_ge(q_final, 2 * t + 2)
                        pe.wait_ge(rot_ready, HG * (t + 1))
                    for j in tiles:
                        keys = slice(P * j, P * j + P)
                        pe.wait_ge(exped, 16 * t + 4 * r + j + 1)
                        ps = score_ps[j % 2]
                        nc.tensor.matmul(ps, angle_k[:, keys], rot[p][:, r], start=True, stop=False)
                        nc.tensor.matmul(ps, ks[p][rows_of(r), r // 2, keys], qs[p][rows_of(r), r // 2], start=False, stop=True).then_inc(scored, 1)

                def weigh_v(t, p, r):
                    if r == 0:
                        pe.wait_ge(added, t + 1)
                    pe.wait_ge(lo_done, 16 * t + 4 * r + 4 + 4)
                    for j in range(NT):
                        for part in (p_hi, p_lo):
                            last = nc.tensor.matmul(av_ps[32 * r:32 * r + 32, :], vaug[p][:, j, r], part[:, r % 2, j],
                                                    start=(j == 0 and part is p_hi), stop=(j == NT - 1 and part is p_lo))
                    if r == HG - 1:
                        last.then_inc(av_ready, 1)

                def denominators(t):
                    pe.wait_ge(av_copied, t + 1)
                    nc.tensor.matmul(av_ps, pick_sum[:], av[:], start=True, stop=True).then_inc(den_ready, 1)

                def project_out(t, i, p):
                    pe.wait_ge(wo_here[p], 16 * (i + 1))
                    pe.wait_ge(avn_ready, t + 1)
                    nc.tensor.matmul(av_ps, wo[p][:], avn[:], start=True, stop=True).then_inc(o_ready, 1)

                def step(t, i, p, last=False):
                    u, n = t + 1, 1 - p
                    turn(u, n, 0)
                    scores(t, p, 1, (0, 1))
                    turn(u, n, 1)
                    scores(t, p, 1, (2, 3))
                    project_kv(u, n)
                    weigh_v(t, p, 0)
                    scores(t, p, 2, (0, 1))
                    turn(u, n, 2)
                    rough_scores(u, n, 0, (0, 1))
                    scores(t, p, 2, (2,))
                    rough_scores(u, n, 0, (2,))
                    scores(t, p, 2, (3,))
                    rough_scores(u, n, 0, (3,))
                    turn(u, n, 3)
                    weigh_v(t, p, 1)
                    rough_scores(u, n, 1, (0,))
                    scores(t, p, 3, (0,))
                    rough_scores(u, n, 1, (1, 2))
                    scores(t, p, 3, (1,))
                    rough_scores(u, n, 1, (3,))
                    rough_scores(u, n, 2, (0,))
                    scores(t, p, 3, (2,))
                    rough_scores(u, n, 2, (1, 2))
                    scores(t, p, 3, (3,))
                    rough_scores(u, n, 2, (3,))
                    rough_scores(u, n, 3, (0,))
                    weigh_v(t, p, 2)
                    rough_scores(u, n, 3, (1, 2, 3))
                    weigh_v(t, p, 3)
                    if not last:
                        project_q(t + 2, i + 1, p)
                    turn_maxima(u)
                    denominators(t)
                    scores(u, n, 0)
                    project_out(t, i, p)

                project_q(0, 0, 0)
                turn(0, 0, 0)
                turn(0, 0, 1)
                project_kv(0, 0)
                turn(0, 0, 2)
                rough_scores(0, 0, 0)
                turn(0, 0, 3)
                for r in range(1, HG):
                    rough_scores(0, 0, r)
                project_q(1, 0, 1)
                turn_maxima(0)
                scores(0, 0, 0)
                with pe.Fori(0, TURNS // 2 - 1) as i:
                    step(2 * i, i, 0)
                    step(2 * i + 1, i, 1)
                step(TURNS - 2, TURNS // 2 - 1, 0, last=True)
                t = TURNS - 1
                for r in range(1, HG):
                    scores(t, 1, r)
                    weigh_v(t, 1, r - 1)
                weigh_v(t, 1, HG - 1)
                denominators(t)
                project_out(t, TURNS // 2 - 1, 1)

            @block.scalar
            def _(act):
                act.wait_ge(tables, 16 * N_TABLES)
                nc.scalar.activation(angle_kb[:], angle_k[:], ACT.Copy).then_inc(set_up, 1)
                nc.scalar.activation(wp_h[:], wp_raw[:], ACT.Copy).then_inc(wp_split, 1)
                act.wait_ge(wp_split, 2)
                nc.scalar.activation(wp_h[:], wp_raw[:], ACT.Copy).then_inc(wp_split, 1)
                act.sem_inc(exped, 2)

                def split(u, k):
                    for tt, ps in enumerate((a_ps, b_ps)):
                        act.wait_ge(qk_ready, 4 * u + 2 * k + tt + 1)
                        if k == 0:
                            nc.scalar.activation(h6[:, tt], ps, ACT.Copy).then_inc(h_done, 1)
                        else:
                            nc.scalar.activation(h6[:, tt], ps, ACT.Identity, bias=k_ones).then_inc(h_done, 1)
                    for tt in range(2):
                        act.wait_ge(rest_done, 4 * u + 2 * k + tt + 1)
                        nc.scalar.activation(m6[:, tt], rest[:, tt], ACT.Copy).then_inc(m_done, 1)

                def narrow(u, p, r):
                    act.wait_ge(rot_ready, HG * u + r + 1)
                    nc.scalar.activation(rotb[:, r], rot[p][:, r], ACT.Copy).then_inc(rotb_ready, 1)

                def exps(t, r, tiles=range(NT)):
                    for j in tiles:
                        act.wait_ge(scored, 16 * t + 4 * r + j + 1)
                        act.wait_ge(lo_done, 16 * t + 4 * r + j + 1)
                        nc.scalar.activation(p32[:, j], score_ps[j % 2], ACT.Exp, scale=SCALE).then_inc(exped, 1)

                def copy_av(t):
                    act.wait_ge(av_ready, t + 1)
                    nc.scalar.activation(av[:], av_ps, ACT.Copy).then_inc(av_copied, 1)

                def invert_denominators(t):
                    act.wait_ge(den_ready, t + 1)
                    nc.scalar.activation(rden[:], av_ps, ACT.Ln).then_inc(den_log, 1)
                    act.wait_ge(den_log, t + 1)
                    nc.scalar.activation(rden[:], rden[:], ACT.Exp, scale=-1.0).then_inc(den_inv, 1)

                def step(t, p, last=False):
                    u, n = t + 1, 1 - p
                    exps(t, 1, (0, 1))
                    narrow(u, n, 0)
                    exps(t, 1, (2, 3))
                    narrow(u, n, 1)
                    split(u, 1)
                    exps(t, 2)
                    narrow(u, n, 2)
                    exps(t, 3, (0, 1))
                    narrow(u, n, 3)
                    exps(t, 3, (2, 3))
                    copy_av(t)
                    if not last:
                        split(t + 2, 0)
                    invert_denominators(t)
                    exps(u, 0)

                split(0, 0)
                narrow(0, 0, 0)
                narrow(0, 0, 1)
                split(0, 1)
                narrow(0, 0, 2)
                narrow(0, 0, 3)
                split(1, 0)
                exps(0, 0)
                with act.Fori(0, TURNS // 2 - 1) as i:
                    step(2 * i, 0)
                    step(2 * i + 1, 1)
                step(TURNS - 2, 0, last=True)
                for r in range(1, HG):
                    exps(TURNS - 1, r)
                copy_av(TURNS - 1)
                invert_denominators(TURNS - 1)

            @block.vector
            def _(dve):
                dve.wait_ge(tables, 16 * N_TABLES)
                dve.wait_ge(set_up, 2)
                dve.sem_inc(maxed, 2)
                dve.sem_inc(added, 1)
                dve.wait_ge(wp_split, 1)
                nc.vector.scalar_tensor_tensor(out=wp_raw[:], in0=wp_h[:], scalar=k_less_h, in1=wp_raw[:],
                                               op0=ALU.mult, op1=ALU.add).then_inc(wp_split, 1)
                dve.wait_ge(wp_split, 3)
                nc.vector.scalar_tensor_tensor(out=wp_parts[:], in0=wp_h[:], scalar=k_less_m, in1=wp_raw[:],
                                               op0=ALU.mult, op1=ALU.add).then_inc(wp_split, 1)

                def parts(u, p, k):
                    dst, less_h, less_m = (qs, q_less_h, q_less_m) if k == 0 else (ks, k_less_h, k_less_m)
                    for tt, ps in enumerate((a_ps, b_ps)):
                        dve.wait_ge(h_done, 4 * u + 2 * k + tt + 1)
                        if k or not first(u):
                            dve.wait_ge(parts_done, 4 * u + 2 * k + tt - 1)
                        nc.vector.scalar_tensor_tensor(out=rest[:, tt], in0=h6[:, tt], scalar=less_h, in1=ps,
                                                       op0=ALU.mult, op1=ALU.add).then_inc(rest_done, 1)
                    for tt in range(2):
                        dve.wait_ge(m_done, 4 * u + 2 * k + tt + 1)
                        nc.vector.scalar_tensor_tensor(out=dst[p][:, tt], in0=m6[:, tt], scalar=less_m, in1=rest[:, tt],
                                                       op0=ALU.mult, op1=ALU.add).then_inc(parts_done, 1)

                def v_parts(u, p):
                    v_ps = misc_ps[:, 0:P].rearrange("p (j r e) -> p j r e", j=NT, r=HG)
                    dve.wait_ge(v_ready, u + 1)
                    if not first(u):
                        dve.wait_ge(v_done, 2 * u)
                    nc.vector.tensor_scalar(v_h[:], v_ps, 1.0, None, ALU.mult).then_inc(v_chain, 1)
                    dve.wait_ge(v_chain, 3 * u + 1)
                    nc.vector.tensor_scalar(vaug[p][:, :, :, 0:8], v_h[:], 1.0, None, ALU.mult)
                    nc.vector.tensor_tensor(v_rest[:], v_h[:], v_ps, ALU.subtract).then_inc(v_chain, 1)
                    dve.wait_ge(v_chain, 3 * u + 2)
                    nc.vector.tensor_scalar(v_m[:], v_rest[:], -1.0, None, ALU.mult).then_inc(v_chain, 1)
                    dve.wait_ge(v_chain, 3 * u + 3)
                    nc.vector.tensor_scalar(vaug[p][:, :, :, 9:17], v_m[:], 1.0, None, ALU.mult)
                    nc.vector.tensor_tensor(v_rest[:], v_rest[:], v_m[:], ALU.add).then_inc(v_done, 1)
                    dve.wait_ge(v_done, 2 * u + 1)
                    nc.vector.tensor_scalar(vaug[p][:, :, :, 18:26], v_rest[:], -1.0, None, ALU.mult).then_inc(v_done, 1)

                def turn(u, r):
                    dve.wait_ge(turned, HG * u + r + 1)
                    if r >= 2:
                        dve.wait_ge(rot_ready, HG * u + r - 1)
                    nc.vector.tensor_tensor(half[:, r % 2, 0], a_ps, cos_q[:], ALU.mult)
                    nc.vector.tensor_tensor(half[:, r % 2, 1], b_ps, sin_q[:], ALU.mult).then_inc(halves, 1)

                def maxima(u, r, tiles=range(NT)):
                    for k in tiles:
                        dve.wait_ge(rough, 16 * u + 4 * r + k + 1)
                        nc.vector.tensor_reduce(mx[:, k, r:r + 1], rough_ps[k % 2], AX_X, ALU.max).then_inc(maxed, 1)

                def spread_maxima(u):
                    def then(k, ins):
                        ins.then_inc(mx_chain, 1)
                        dve.wait_ge(mx_chain, MX_STEPS * u + k)

                    def wide(s):
                        return max_wide[:, :, :, :, SLOT * s + 8]

                    def heads(a):
                        return a.rearrange("p j (t r) -> p j t r", t=2)

                    dve.wait_ge(maxed, 16 * u + 18)
                    then(1, nc.vector.tensor_scalar(mx_part[:, 0], mx[:], 1.0, None, ALU.mult))
                    nc.vector.tensor_scalar(wide(0), heads(mx_part[:, 0]), 1.0, None, ALU.mult)
                    then(2, nc.vector.tensor_tensor(mx_rest[:], mx[:], mx_part[:, 0], ALU.subtract))
                    then(3, nc.vector.tensor_scalar(mx_part[:, 1], mx_rest[:], 1.0, None, ALU.mult))
                    nc.vector.tensor_scalar(wide(1), heads(mx_part[:, 1]), 1.0, None, ALU.mult)
                    then(4, nc.vector.tensor_tensor(mx_part[:, 0], mx_rest[:], mx_part[:, 1], ALU.subtract))
                    nc.vector.tensor_scalar(wide(2), heads(mx_part[:, 0]), 1.0, None, ALU.mult).then_inc(mx_wide, 1)

                def finish_q(u, p):
                    dve.wait_ge(max_turned, u + 1)
                    for tt, ps in enumerate(rough_ps):
                        nc.vector.tensor_tensor(qs[p][:, tt], qs[p][:, tt], ps, ALU.subtract).then_inc(q_final, 1)

                def high_parts(t, r, tiles=range(NT)):
                    for j in tiles:
                        dve.wait_ge(exped, 16 * t + 4 * r + j + 1 + 2)
                        nc.vector.tensor_scalar(p_hi[:, r % 2, j], p32[:, j], 1.0, None, ALU.mult).then_inc(hi_done, 1)

                def normalise(t):
                    dve.wait_ge(den_inv, t + 1)
                    nc.vector.tensor_tensor(avn[:], av[:], rden[:], ALU.mult).then_inc(avn_ready, 1)

                def add(t, b):
                    dve.wait_ge(o_ready, t + 1)
                    nc.vector.tensor_tensor(c.resid[:, b], c.resid[:, b], av_ps, ALU.add).then_inc(added, 1)

                def step(t, b, p, last=False):
                    u, n = t + 1, 1 - p
                    turn(u, 0)
                    high_parts(t, 1, (0, 1))
                    turn(u, 1)
                    high_parts(t, 1, (2, 3))
                    parts(u, n, 1)
                    high_parts(t, 2, (0, 1))
                    turn(u, 2)
                    maxima(u, 0, (0, 1))
                    high_parts(t, 2, (2,))
                    maxima(u, 0, (2,))
                    high_parts(t, 2, (3,))
                    maxima(u, 0, (3,))
                    turn(u, 3)
                    maxima(u, 1, (0,))
                    high_parts(t, 3, (0,))
                    maxima(u, 1, (1, 2))
                    high_parts(t, 3, (1,))
                    maxima(u, 1, (3,))
                    maxima(u, 2, (0,))
                    high_parts(t, 3, (2,))
                    maxima(u, 2, (1, 2))
                    high_parts(t, 3, (3,))
                    maxima(u, 2, (3,))
                    maxima(u, 3)
                    spread_maxima(u)
                    finish_q(u, n)
                    if not last:
                        parts(t + 2, p, 0)
                    high_parts(u, 0, (0,))
                    normalise(t)
                    v_parts(u, n)
                    high_parts(u, 0, (1, 2, 3))
                    add(t, b)

                parts(0, 0, 0)
                turn(0, 0)
                turn(0, 1)
                parts(0, 0, 1)
                v_parts(0, 0)
                turn(0, 2)
                maxima(0, 0)
                turn(0, 3)
                for r in range(1, HG):
                    maxima(0, r)
                spread_maxima(0)
                finish_q(0, 0)
                parts(1, 1, 0)
                high_parts(0, 0)
                with dve.Fori(0, TURNS // 2 - 1) as i:
                    step(2 * i, i // 2, 0)
                    step(2 * i + 1, i // 2, 1)
                step(TURNS - 2, NB - 1, 0, last=True)
                for r in range(1, HG):
                    high_parts(TURNS - 1, r)
                normalise(TURNS - 1)
                add(TURNS - 1, NB - 1)


def phase_norm(c, name):
    nc = c.nc
    with ExitStack() as ctx:
        ph = Phase(c, ctx)
        cent = [ph.sb(f"{name}_cent{p}", [P, T]) for p in range(2)]
        sq = [ph.sb(f"{name}_sq{p}", [P, T]) for p in range(2)]
        s = [NormSems(ph.sem, f"{name}{p}") for p in range(2)]

        with nc.Block() as block:
            @block.tensor
            def _(pe):
                with pe.Fori(0, NB // 2) as i:
                    for p in range(2):
                        pe.wait_ge(s[p].y, i + 1)
                        nc.tensor.matmul(c.bank[p][:], c.ones[:], c.resid[:, 2 * i + p], start=True, stop=True).then_inc(s[p].mean, 1)
                    for p in range(2):
                        pe.wait_ge(s[p].sq, i + 1)
                        nc.tensor.matmul(c.bank[2 + p][:], c.ones[:], sq[p][:], start=True, stop=True).then_inc(s[p].var, 1)

            @block.scalar
            def _(act):
                nc.scalar.preload_act_table_set(LN_EXP)
                with act.Fori(0, NB // 2) as i:
                    for p in range(2):
                        act.wait_ge(s[p].cent, i + 1)
                        nc.scalar.activation(sq[p][:], cent[p][:], ACT.Square).then_inc(s[p].sq, 1)
                    for p in range(2):
                        var = c.bank[2 + p]
                        act.wait_ge(s[p].var, i + 1)
                        nc.scalar.activation(var[:], var[:], ACT.Ln, bias=c.eps[:]).then_inc(s[p].log, 1)
                        act.wait_ge(s[p].log, i + 1)
                        nc.scalar.activation(var[:], var[:], ACT.Exp, scale=-0.5).then_inc(s[p].rstd, 1)

            @block.vector
            def _(dve):
                for p in range(2):
                    dve.sem_inc(s[p].y, 1)
                with dve.Fori(0, NB // 2) as i:
                    for p in range(2):
                        dve.wait_ge(s[p].mean, i + 1)
                        nc.vector.tensor_tensor(cent[p][:], c.resid[:, 2 * i + p], c.bank[p][:], ALU.subtract).then_inc(s[p].cent, 1)
                    for p in range(2):
                        dve.wait_ge(s[p].rstd, i + 1)
                        nc.vector.tensor_tensor(c.resid[:, 2 * i + p], cent[p][:], c.bank[2 + p][:], ALU.mult).then_inc(s[p].y, 1)


NE = 32
TOP = 4


def gates_of_batches(c, d, ph, gate_parts):
    nc = c.nc
    sel_w = ph.sb("sel_w", [P, NE])
    vec = ph.sb("ln2_vec", [P, 2])
    y, cent, sq, x2 = (ph.sb(f"gate_{n}", [P, T]) for n in ("y", "cent", "sq", "x2"))
    e = ph.sb("gate_exp", [P, NT, NE])
    e1 = ph.sb("gate_exp1", [P, NT, NE])
    prob = ph.sb("gate_prob", [P, NT, NE])
    top8 = ph.sb("gate_top8", [P, NT, 8])
    above = ph.sb("gate_above", [P, NT, NE])
    equal = ph.sb("gate_equal", [P, NT, NE])
    n_above = ph.sb("gate_n_above", [P, NT])
    nth = ph.sb("gate_nth", [P, NT, NE])
    fits = ph.sb("gate_fits", [P, NT, NE])
    tie = ph.sb("gate_tie", [P, NT, NE])
    chosen = ph.sb("gate_chosen", [P, NT, NE])
    gate = ph.sb("gate_value", [P, NT, NE])
    one = ph.sb("gate_one", [P, NE])
    pad = ph.sb("gate_pad", [P, 1])
    rest = ph.sb("gate_rest", [NE, T])
    mid = ph.sb("gate_mid", [NE, T], BF16)
    high = ph.sb("gate_high", [NE, T], BF16)
    loaded, set_up = ph.sem("p3_loaded"), ph.sem("p3_set_up")
    ln = NormSems(ph.sem, "p3n")
    x2_ready, logits, exped = ph.sem("p3_x2"), ph.sem("p3_logits"), ph.sem("p3_exped")
    chain = ph.sem("p3_dve_chain")
    gate_ready, gate_turned = ph.sem("p3_gate"), ph.sem("p3_gate_turned")
    DVE_STEPS = 16
    mean_ps, var_ps, logit_ps, gate_ps = (c.bank[i] for i in range(4))
    logit_v = logit_ps[:, 0:NT * NE].rearrange("p (j e) -> p j e", j=NT)

    with nc.Block() as block:
        @block.sync
        def _(sp):
            sp.dma_start(sel_w[:], d["sel_w"]).then_inc(loaded, 16)
            sp.dma_start(vec[:, 0:1], d["ln2_g"]).then_inc(loaded, 16)
            sp.dma_start(vec[:, 1:2], d["ln2_b"]).then_inc(loaded, 16)

        @block.gpsimd
        def _(pool):
            nc.gpsimd.memset(one[:], 1.0).then_inc(set_up, 1)

        @block.tensor
        def _(pe):
            pe.wait_ge(loaded, 48)
            with pe.Fori(0, NB) as b:
                norm_pe(nc, pe, ln, b + 1, c.ones[:], y[:], sq[:], mean_ps[:], var_ps[:])
                pe.wait_ge(x2_ready, b + 1)
                for j in range(NT):
                    last = nc.tensor.matmul(logit_v[:, j], x2[:, P * j:P * j + P], sel_w[:], start=True, stop=True)
                last.then_inc(logits, 1)
                pe.wait_ge(gate_ready, b + 1)
                for j in range(NT):
                    last = nc.tensor.transpose(gate_ps[0:NE, P * j:P * j + P], gate[:, j], c.ident[:])
                last.then_inc(gate_turned, 1)

        @block.scalar
        def _(act):
            nc.scalar.preload_act_table_set(LN_EXP)
            with act.Fori(0, NB) as b:
                norm_act(nc, act, ln, b + 1, cent[:], sq[:], var_ps[:], c.eps[:])
                act.wait_ge(logits, b + 1)
                nc.scalar.activation(e[:], logit_v, ACT.Exp, scale=-1.0).then_inc(exped, 1)

        @block.vector
        def _(dve):
            dve.wait_ge(loaded, 48)
            dve.wait_ge(set_up, 1)
            with dve.Fori(0, NB) as b:
                steps = [0]

                def then(ins):
                    steps[0] += 1
                    ins.then_inc(chain, 1)
                    dve.wait_ge(chain, DVE_STEPS * b + steps[0])

                nc.vector.tensor_scalar(y[:], c.resid[:, b], 1.0, None, ALU.mult).then_inc(ln.y, 1)
                dve.wait_ge(ln.y, b + 1)
                nc.vector.tensor_tensor(c.resid[:, b], y[:], c.outer[:, b], ALU.add)
                norm_dve(nc, dve, ln, b + 1, y[:], cent[:], mean_ps[:], var_ps[:], y[:])
                dve.wait_ge(ln.out, b + 1)
                nc.vector.tensor_scalar(x2[:], y[:], vec[:, 0:1], vec[:, 1:2], ALU.mult, ALU.add).then_inc(x2_ready, 1)
                dve.wait_ge(x2_ready, b + 1)
                nc.vector.tensor_scalar(c.normed[:, b], x2[:], 1.0, None, ALU.mult)
                dve.wait_ge(exped, b + 1)
                then(nc.vector.tensor_scalar(e1[:], e[:], 1.0, None, ALU.add))
                then(nc.vector.reciprocal(prob[:], e1[:]))
                nc.vector.memset(pad[:], 0.0)
                for j in range(NT):
                    last = nc.vector.max(top8[:, j], prob[:, j])
                then(last)
                for j in range(NT):
                    fourth = top8[:, j, TOP - 1:TOP]
                    nc.vector.tensor_scalar(above[:, j], prob[:, j], fourth, None, ALU.is_gt)
                    last = nc.vector.tensor_scalar(equal[:, j], prob[:, j], fourth, None, ALU.is_equal)
                then(last)
                nc.vector.tensor_reduce(n_above[:], above[:], AX_X, ALU.add)
                for j in range(NT):
                    last = nc.vector.tensor_tensor_scan(nth[:, j], one[:], equal[:, j], 0.0, ALU.mult, ALU.add)
                then(last)
                for j in range(NT):
                    last = nc.vector.tensor_scalar(fits[:, j], nth[:, j], n_above[:, j:j + 1], float(TOP), ALU.add, ALU.is_le)
                then(last)
                then(nc.vector.tensor_tensor(tie[:], equal[:], fits[:], ALU.mult))
                then(nc.vector.tensor_tensor(chosen[:], tie[:], above[:], ALU.add))
                nc.vector.tensor_tensor(gate[:], chosen[:], prob[:], ALU.mult).then_inc(gate_ready, 1)
                dve.wait_ge(gate_turned, b + 1)
                then(nc.vector.tensor_copy(high[:], gate_ps[0:NE, :]))
                then(nc.vector.tensor_tensor(rest[:], gate_ps[0:NE, :], high[:], ALU.subtract))
                nc.vector.tensor_scalar(gate_parts[0:NE, b], high[:], 1.0, None, ALU.mult)
                then(nc.vector.tensor_copy(mid[:], rest[:]))
                nc.vector.tensor_scalar(gate_parts[NE:2 * NE, b], mid[:], 1.0, None, ALU.mult)
                then(nc.vector.tensor_tensor(gate_parts[2 * NE:3 * NE, b], rest[:], mid[:], ALU.subtract))
                for _ in range(DVE_STEPS - steps[0]):
                    dve.sem_inc(chain, 1)


def experts(c, d, ph, gate_parts):
    nc = c.nc
    keys = [ph.sb(f"keys{p}", [P, P]) for p in range(2)]
    values = [ph.sb(f"values{p}", [P, P]) for p in range(2)]
    pick = [ph.sb(f"pick_expert{p}", [3 * NE, P], BF16) for p in range(2)]
    h = [ph.sb(f"hidden{p}", [P, T]) for p in range(2)]
    hg = [ph.sb(f"hidden_gated{p}", [P, T]) for p in range(2)]
    here = [ph.sem(f"p3_expert_here{p}") for p in range(2)]
    h_ready, g_ready = ph.sem("p3_h"), ph.sem("p3_g")
    rectified, gated = ph.sem("p3_rectified"), ph.sem("p3_gated")
    valued = ph.sem("p3_valued")
    added = ph.sem("p3_added")
    h_ps, g_ps, v_ps = c.bank[0:2], c.bank[2:4], c.bank[4:6]

    with nc.Block() as block:
        @block.sync
        def _(sp):
            def load(x, p):
                sp.dma_start(keys[p][:], d["keys"][x]).then_inc(here[p], 16)
                sp.dma_start(values[p][:], d["values"][x]).then_inc(here[p], 16)
                sp.dma_start(pick[p][:], d["pick_expert"][x]).then_inc(here[p], 16)

            load(0, 0)
            load(1, 1)
            with sp.Fori(0, NE // 2 - 1) as i:
                for p in range(2):
                    sp.wait_ge(valued, NB * (2 * i + p + 1))
                    load(2 * i + p + 2, p)

        @block.tensor
        def _(pe):
            with pe.Fori(0, NE // 2) as i:
                def apply_values(k):
                    pe.wait_ge(gated, 2 * NB * i + k + 1)
                    pe.wait_ge(added, 2 * NB * i + k + 1)
                    nc.tensor.matmul(v_ps[k % 2][:], values[k // NB][:], hg[k % 2][:], start=True, stop=True).then_inc(valued, 1)

                for k in range(2 * NB):
                    p, b = divmod(k, NB)
                    if b == 0:
                        pe.wait_ge(here[p], 48 * (i + 1))
                    nc.tensor.matmul(h_ps[k % 2][:], keys[p][:], c.normed[:, b], start=True, stop=True).then_inc(h_ready, 1)
                    nc.tensor.matmul(g_ps[k % 2][:], pick[p][:], gate_parts[:, b], start=True, stop=True).then_inc(g_ready, 1)
                    if k:
                        apply_values(k - 1)
                apply_values(2 * NB - 1)

        @block.scalar
        def _(act):
            with act.Fori(0, NE // 2) as i:
                for k in range(2 * NB):
                    act.wait_ge(h_ready, 2 * NB * i + k + 1)
                    nc.scalar.activation(h[k % 2][:], h_ps[k % 2][:], ACT.Relu).then_inc(rectified, 1)

        @block.vector
        def _(dve):
            dve.sem_inc(added, 2)
            with dve.Fori(0, NE // 2) as i:
                def add(k):
                    dve.wait_ge(valued, 2 * NB * i + k + 1)
                    resid = c.resid[:, k % NB]
                    nc.vector.tensor_tensor(resid, resid, v_ps[k % 2][:], ALU.add).then_inc(added, 1)

                for k in range(2 * NB):
                    dve.wait_ge(rectified, 2 * NB * i + k + 1)
                    dve.wait_ge(g_ready, 2 * NB * i + k + 1)
                    nc.vector.tensor_tensor(hg[k % 2][:], h[k % 2][:], g_ps[k % 2][:], ALU.mult).then_inc(gated, 1)
                    if k:
                        add(k - 1)
                add(2 * NB - 1)


def phase_experts(c, d):
    with ExitStack() as ctx:
        ph = Phase(c, ctx)
        gate_parts = ph.sb("gate_parts", [3 * NE, NB, T], BF16)
        gates_of_batches(c, d, ph, gate_parts)
        experts(c, d, ph, gate_parts)
    phase_norm(c, "ffn0_norm")


NH = 4
DS = 64
NR = NB * NH
DI = NH * DS
TWO_PI_HI = 6.28125
TWO_PI_LO = 2.0 * np.pi - TWO_PI_HI
ROUND = 1.5 * 2.0 ** 23
PI_IN = 3.1415925
NEG = -1e30


def state_space_rows(c, d, ph, dt, ncs, cols):
    nc = c.nc
    w_rows = ph.sb("w_rows", [P, 3, NB, NR])
    bias = ph.sb("dt_bias", [NR, 1])
    absd, absa = ph.sb("ss_absd", [NR, T]), ph.sb("ss_absa", [NR, T])
    one = ph.sb("ss_one", [NR, T])
    m, sp, trap, w1, w2, decay, nadt, cc, n1 = (ph.sb(f"ss_{n}", [NR, T]) for n in (
        "max0", "softplus_a", "trap", "w1", "w2", "decay", "neg_adt", "c", "n1"))
    loaded, set_up = ph.sem("p4_loaded"), ph.sem("p4_set_up")
    rows_ready = ph.sem("p4_rows")
    act_chain, dve_chain = ph.sem("p4_act_chain"), ph.sem("p4_dve_chain")
    dt_log, a_log, trap_exp, decay_ready = ph.sem("p4_dt_log"), ph.sem("p4_a_log"), ph.sem("p4_trap_exp"), ph.sem("p4_decay")
    nadt_ready, cols_in, cols_turned = ph.sem("p4_nadt"), ph.sem("p4_cols_in"), ph.sem("p4_cols_turned")
    dt_ps, a_ps, trap_ps = (c.bank[i][0:NR, :] for i in range(3))

    with nc.Block() as block:
        @block.sync
        def _(sp_):
            sp_.dma_start(w_rows[:], d["ss_w_rows"]).then_inc(loaded, 16)
            sp_.dma_start(bias[:], d["ss_dt_bias"]).then_inc(loaded, 16)

        @block.gpsimd
        def _(pool):
            nc.gpsimd.memset(one[:], 1.0).then_inc(set_up, 1)

        @block.tensor
        def _(pe):
            pe.wait_ge(loaded, 32)
            for q, ps in enumerate((dt_ps, a_ps, trap_ps)):
                for b in range(NB):
                    last = nc.tensor.matmul(ps, w_rows[:, q, b], c.resid[:, b], start=(b == 0), stop=(b == NB - 1))
                last.then_inc(rows_ready, 1)
            pe.wait_ge(cols_in, 1)
            for q, rows in enumerate((cc, n1, w1)):
                for j in range(NT):
                    last = nc.tensor.transpose(c.bank[3 + q][:, NR * j:NR * j + NR], rows[:, P * j:P * j + P], c.ident[0:NR, 0:NR])
            last.then_inc(cols_turned, 1)

        @block.scalar
        def _(act):
            nc.scalar.preload_act_table_set(LN_EXP)
            steps = [0]

            def then(ins):
                steps[0] += 1
                ins.then_inc(act_chain, 1)
                act.wait_ge(act_chain, steps[0])

            act.wait_ge(loaded, 32)
            act.wait_ge(rows_ready, 2)
            then(nc.scalar.activation(absd[:], dt_ps, ACT.Abs, bias=bias[:]))
            then(nc.scalar.activation(absd[:], absd[:], ACT.Exp, scale=-1.0))
            nc.scalar.activation(absd[:], absd[:], ACT.Ln, bias=1.0).then_inc(dt_log, 1)
            then(nc.scalar.activation(absa[:], a_ps, ACT.Abs))
            then(nc.scalar.activation(absa[:], absa[:], ACT.Exp, scale=-1.0))
            nc.scalar.activation(absa[:], absa[:], ACT.Ln, bias=1.0).then_inc(a_log, 1)
            act.wait_ge(rows_ready, 3)
            nc.scalar.activation(trap[:], trap_ps, ACT.Exp, scale=-1.0).then_inc(trap_exp, 1)
            act.wait_ge(nadt_ready, 1)
            nc.scalar.activation(decay[:], nadt[:], ACT.Exp, scale=-1.0).then_inc(decay_ready, 1)

        @block.vector
        def _(dve):
            steps = [0]

            def then(ins):
                steps[0] += 1
                ins.then_inc(dve_chain, 1)
                dve.wait_ge(dve_chain, steps[0])

            dve.wait_ge(loaded, 32)
            dve.wait_ge(set_up, 1)
            dve.wait_ge(dt_log, 1)
            then(nc.vector.tensor_scalar(m[:], dt_ps, bias[:], 0.0, ALU.add, ALU.max))
            then(nc.vector.tensor_tensor(dt[:], m[:], absd[:], ALU.add))
            dve.wait_ge(a_log, 1)
            then(nc.vector.tensor_scalar(m[:], a_ps, 0.0, None, ALU.max))
            then(nc.vector.tensor_tensor(sp[:], m[:], absa[:], ALU.add))
            nc.vector.scalar_tensor_tensor(out=nadt[:], in0=sp[:], scalar=1e-4, in1=dt[:], op0=ALU.max, op1=ALU.mult).then_inc(nadt_ready, 1)
            dve.wait_ge(nadt_ready, 1)
            then(nc.vector.tensor_tensor_scan(ncs[:], one[:], nadt[:], 0.0, ALU.mult, ALU.add))
            dve.wait_ge(trap_exp, 1)
            then(nc.vector.tensor_scalar(m[:], trap[:], 1.0, None, ALU.add))
            then(nc.vector.reciprocal(sp[:], m[:]))
            then(nc.vector.tensor_tensor(w1[:], sp[:], dt[:], ALU.mult))
            then(nc.vector.tensor_tensor(w2[:], dt[:], w1[:], ALU.subtract))
            nc.vector.memset(cc[:, T - 1:T], 0.0)
            nc.vector.memset(n1[:, T - 1:T], 0.0)
            nc.vector.tensor_copy(n1[:, 0:T - 1], ncs[:, 1:T])
            dve.wait_ge(decay_ready, 1)
            then(nc.vector.tensor_tensor(m[:, 0:T - 1], decay[:, 1:T], w1[:, 0:T - 1], ALU.mult))
            nc.vector.tensor_tensor(cc[:, 0:T - 1], m[:, 0:T - 1], w2[:, 1:T], ALU.add).then_inc(cols_in, 1)
            dve.wait_ge(cols_turned, 1)
            for q in range(3):
                nc.vector.tensor_copy(cols[:, q], c.bank[3 + q][:, 0:NT * NR].rearrange("p (j r) -> p j r", j=NT))


def state_space_angles(c, d, ph, dt, cos, sin):
    nc = c.nc
    w_ang = ph.sb("w_angle", [P, P])
    sign = ph.sb("sin_sign", [P, 1])
    pick = ph.sb("pick_mean", [NR, P])
    one = ph.sb("ang_one", [P, T])
    mean_dt, step_, phase, km, k, r1, r2, r, over, rc = (ph.sb(f"ang_{n}", [P, T]) for n in (
        "mean_dt", "step", "phase", "km", "k", "r1", "r2", "r", "over", "rc"))
    loaded, set_up, here = ph.sem("p4a_loaded"), ph.sem("p4a_set_up"), ph.sem("p4a_here")
    projected, copied = ph.sem("p4a_projected"), ph.sem("p4a_copied")
    chain = ph.sem("p4a_chain")
    reduced, turned = ph.sem("p4a_reduced"), ph.sem("p4a_sines")
    STEPS = 9
    ang_ps, mean_ps = c.bank[0], c.bank[1]

    with nc.Block() as block:
        @block.sync
        def _(sp):
            sp.dma_start(w_ang[:], d["ss_w_angle"]).then_inc(loaded, 16)
            sp.dma_start(sign[:], d["ss_sign"]).then_inc(loaded, 16)
            sp.dma_start(pick[:], d["ss_pick"][0, :, NH * P:]).then_inc(here, 16)
            with sp.Fori(0, NB - 1) as b:
                sp.wait_ge(projected, b + 1)
                sp.dma_start(pick[:], d["ss_pick"][b + 1, :, NH * P:]).then_inc(here, 16)

        @block.gpsimd
        def _(pool):
            nc.gpsimd.memset(one[:], 1.0).then_inc(set_up, 1)

        @block.tensor
        def _(pe):
            pe.wait_ge(loaded, 32)
            with pe.Fori(0, NB) as b:
                pe.wait_ge(here, 16 * (b + 1))
                pe.wait_ge(chain, STEPS * b + 1)
                nc.tensor.matmul(ang_ps[:], w_ang[:], c.resid[:, b], start=True, stop=True)
                nc.tensor.matmul(mean_ps[:], pick[:], dt[:], start=True, stop=True).then_inc(projected, 1)

        @block.scalar
        def _(act):
            act.wait_ge(loaded, 32)
            with act.Fori(0, NB) as b:
                act.wait_ge(projected, b + 1)
                nc.scalar.activation(mean_dt[:], mean_ps[:], ACT.Copy).then_inc(copied, 1)
                act.wait_ge(reduced, b + 1)
                nc.scalar.activation(sin[:, b], r[:], ACT.Sin, scale=sign[:])
                nc.scalar.activation(cos[:, b], rc[:], ACT.Sin).then_inc(turned, 1)

        @block.vector
        def _(dve):
            dve.wait_ge(set_up, 1)
            dve.sem_inc(chain, 1)
            dve.sem_inc(turned, 1)
            with dve.Fori(0, NB) as b:
                steps = [0]

                def then(ins):
                    steps[0] += 1
                    ins.then_inc(chain, 1)
                    dve.wait_ge(chain, STEPS * b + steps[0] + 1)

                dve.wait_ge(copied, b + 1)
                then(nc.vector.tensor_tensor(step_[:], ang_ps[:], mean_dt[:], ALU.mult))
                then(nc.vector.tensor_tensor_scan(phase[:], one[:], step_[:], 0.0, ALU.mult, ALU.add))
                then(nc.vector.tensor_scalar(km[:], phase[:], 0.5 / np.pi, ROUND, ALU.mult, ALU.add))
                then(nc.vector.tensor_scalar(k[:], km[:], -ROUND, None, ALU.add))
                then(nc.vector.scalar_tensor_tensor(out=r1[:], in0=k[:], scalar=-TWO_PI_HI, in1=phase[:], op0=ALU.mult, op1=ALU.add))
                then(nc.vector.scalar_tensor_tensor(out=r2[:], in0=k[:], scalar=-TWO_PI_LO, in1=r1[:], op0=ALU.mult, op1=ALU.add))
                dve.wait_ge(turned, b + 1)
                then(nc.vector.tensor_scalar(r[:], r2[:], PI_IN, -PI_IN, ALU.min, ALU.max))
                then(nc.vector.tensor_scalar(over[:], r[:], np.pi / 2, -2.0 * np.pi, ALU.is_gt, ALU.mult))
                then(nc.vector.scalar_tensor_tensor(out=r1[:], in0=r[:], scalar=np.pi / 2, in1=over[:], op0=ALU.add, op1=ALU.add))
                nc.vector.tensor_scalar(rc[:], r1[:], PI_IN, -PI_IN, ALU.min, ALU.max).then_inc(reduced, 1)


def state_space_outputs(c, d, ph, ncs, cols, cos, sin):
    nc = c.nc
    w_bc = ph.sb("w_bc", [P, P])
    w_zx = ph.sb("w_zx", [P, 2 * DI])
    w_out = ph.sb("ss_w_out", [P, 2, P])
    vec = ph.sb("bc_vec", [P, 2])
    ones64 = ph.sb("ones64", [P, P])
    swap = ph.sb("swap_pairs", [P, P])
    later = ph.sb("later", [P, NT, P])
    d_rep = ph.sb("d_rep", [P, NT, NH])
    pick = ph.sb("pick_rows", [NR, NH * P])
    xs = ph.sb("ss_x", [P, T])
    bc, cent, sq, v0, v, t1, t2 = (ph.sb(f"bc_{n}", [P, T]) for n in ("raw", "cent", "sq", "v0", "v", "t1", "t2"))
    brot, crot = ph.sb("b_rot", [DS, T]), ph.sb("c_rot", [DS, T])
    ez, z = ph.sb("ez", [P, NT, DI]), ph.sb("ss_z", [P, NT, DI])
    zs, xt, xc = ([ph.sb(f"ss_{n}{p}", [P, NT, DI]) for p in range(2)] for n in ("zs", "xt", "xc"))
    cq = [ph.sb(f"cq{p}", [P, 3, NT, NH]) for p in range(2)]
    dcoef = [ph.sb(f"dcoef{p}", [P, NT, NH]) for p in range(2)]
    OFF = [0, 512, 896, 1152]
    WID = [512 - P * j for j in range(NT)]
    ALL = OFF[-1] + WID[-1]
    cbs = [ph.sb(f"cb_products{p}", [P, ALL]) for p in range(2)]
    cbw = ph.sb("cbw", [P, NT, P])
    cb = ph.sb("cb", [P, NT])
    y1 = ph.sb("y1", [P, NT, DI])
    ygt = ph.sb("ygt", [P, 2, T])
    diag = [ph.sb(f"diag{p}", [P, T]) for p in range(2)]
    e = [ph.sb(f"e_{p}", [P, ALL]) for p in range(2)]
    mm = [ph.sb(f"m_{p}", [P, ALL]) for p in range(2)]

    loaded = ph.sem("p4b_loaded")
    xs_here, pick_here = ph.sem("p4b_xs_here"), ph.sem("p4b_pick_here")
    done = ph.sem("p4b_done")
    zx_ready = ph.sem("p4b_zx")
    bc_ready = ph.sem("p4b_bc")
    ln = NormSems(ph.sem, "p4b_n")
    cq_ready, v_ready, swapped, turned, rotated = (ph.sem(f"p4b_{n}") for n in ("cq", "v", "swapped", "turned", "rotated"))
    zx_copied = ph.sem("p4b_zx_copied")
    z_clamped, z_log, z_sig, zs_ready = (ph.sem(f"p4b_{n}") for n in ("z_clamped", "z_log", "z_sig", "zs"))
    cb_ready, cb_copied, xc_ready = ph.sem("p4b_cb"), ph.sem("p4b_cb_copied"), ph.sem("p4b_xc")
    cbw_ready, cb_diag, dc_part, dc_ready = (ph.sem(f"p4b_{n}") for n in ("cbw", "cb_diag", "dc_part", "dc"))
    n_ready = ph.sem("p4b_n_row")
    diag_ready = ph.sem("p4b_diag")
    e_ready, m_ready, weighed = ph.sem("p4b_e"), ph.sem("p4b_m"), ph.sem("p4b_weighed")
    y_part, y_sum, yg_ready, ygt_ready, ygt_copied, o_ready = (ph.sem(f"p4b_{n}") for n in (
        "y_part", "y_sum", "yg", "ygt", "ygt_copied", "o"))
    N_LOADS = 12
    bank = c.bank
    n_ps = bank[0:2]
    y_ps = bank[2:4]
    bc_ps, var_ps = bank[4], bank[4]
    zx_ps = bank[5:7]
    mean_ps, swap_ps = bank[7], bank[7]
    cb_ps = bank[4:8]

    def over_batches(engine, front, cycle):
        front(0, 0)
        with engine.Fori(0, NB // 2 - 1) as i:
            cycle(2 * i, 0, True)
            cycle(2 * i + 1, 1, True)
        cycle(NB - 2, 0, True)
        cycle(NB - 1, 1, False)

    def by_head(a):
        return a.rearrange("p j (h e) -> p (j h) e", e=DS)

    with nc.Block() as block:
        @block.sync
        def _(sp):
            sp.dma_start(w_bc[:], d["ss_w_bc"]).then_inc(loaded, 16)
            sp.dma_start(w_zx[:], d["ss_w_zx"]).then_inc(loaded, 16)
            sp.dma_start(w_out[:], d["ss_w_out"]).then_inc(loaded, 16)
            sp.dma_start(vec[:, 0:1], d["ss_gain"]).then_inc(loaded, 16)
            sp.dma_start(vec[:, 1:2], d["ss_shift"]).then_inc(loaded, 16)
            sp.dma_start(ones64[:], d["ones64"]).then_inc(loaded, 16)
            sp.dma_start(swap[:], d["ss_swap"]).then_inc(loaded, 16)
            for j in range(NT):
                sp.dma_start(later[:, j], d["ss_later"]).then_inc(loaded, 16)
            sp.dma_start(d_rep[:], d["ss_d"]).then_inc(loaded, 16)
            sp.dma_start(xs[:], c.resid[:, 0]).then_inc(xs_here, 16)
            sp.dma_start(pick[:], d["ss_pick"][0, :, 0:NH * P]).then_inc(pick_here, 16)
            with sp.Fori(0, NB - 1) as b:
                sp.wait_ge(zx_ready, NT * b + NT)
                sp.dma_start(xs[:], c.resid[:, b + 1]).then_inc(xs_here, 16)
                sp.wait_ge(n_ready, NH * b + NH)
                sp.dma_start(pick[:], d["ss_pick"][b + 1, :, 0:NH * P]).then_inc(pick_here, 16)

        @block.gpsimd
        def _(pool):
            pool.sem_inc(m_ready, 2)

            def masked(b, p, h):
                pool.wait_ge(e_ready, NH * b + h + 1 + 2)
                pool.wait_ge(weighed, NH * b + h + 1)
                if h == 0:
                    pool.wait_ge(cb_copied, b + 1)
                nc.gpsimd.tensor_tensor(mm[h % 2][:], e[h % 2][:], cbs[p][:], ALU.mult).then_inc(m_ready, 1)

            def gate(u, p):
                pool.wait_ge(z_sig, u + 1)
                nc.gpsimd.tensor_tensor(zs[p][:], ez[:], z[:], ALU.mult).then_inc(zs_ready, 1)

            def front(u, p):
                gate(u, p)
                masked(u, p, 0)

            def cycle(b, p, more):
                for h in range(1, NH):
                    masked(b, p, h)
                if more:
                    front(b + 1, 1 - p)

            over_batches(pool, front, cycle)

        @block.tensor
        def _(pe):
            pe.wait_ge(loaded, 16 * N_LOADS)
            pe.sem_inc(weighed, 2)

            def project_bc(u):
                pe.wait_ge(xs_here, 16 * (u + 1))
                if not first(u):
                    pe.wait_ge(cb_copied, u)
                nc.tensor.matmul(bc_ps, w_bc[:], xs[:], start=True, stop=True).then_inc(bc_ready, 1)

            def project_zx(u, j):
                if j >= 2:
                    pe.wait_ge(zx_copied, NT * u + j - 1)
                nc.tensor.matmul(zx_ps[j % 2], xs[:, P * j:P * j + P], w_zx[:], start=True, stop=True).then_inc(zx_ready, 1)

            def mean(u):
                pe.wait_ge(ln.y, u + 1)
                nc.tensor.matmul(mean_ps, ones64[:], bc[:], start=True, stop=True).then_inc(ln.mean, 1)

            def variance(u):
                pe.wait_ge(ln.sq, u + 1)
                nc.tensor.matmul(var_ps, ones64[:], sq[:], start=True, stop=True).then_inc(ln.var, 1)

            def swap_pairs(u):
                pe.wait_ge(v_ready, u + 1)
                nc.tensor.matmul(swap_ps, swap[:], v[:], start=True, stop=True).then_inc(swapped, 1)

            def row_of(b, h):
                if h == 0:
                    pe.wait_ge(pick_here, 16 * (b + 1))
                pe.wait_ge(e_ready, NH * b + h + 1)
                nc.tensor.matmul(n_ps[h % 2], pick[:, P * h:P * h + P], ncs[:], start=True, stop=True).then_inc(n_ready, 1)

            def c_times_b(u):
                pe.wait_ge(rotated, u + 1)
                pe.wait_ge(zx_copied, NT * u + NT)
                for j in range(NT):
                    nc.tensor.matmul(cb_ps[j][:, 0:WID[j]], brot[:, P * j:P * j + P], crot[:, P * j:],
                                     start=True, stop=True).then_inc(cb_ready, 1)

            def head(b, p, h):
                if h == 0:
                    pe.wait_ge(xc_ready, b + 1)
                    pe.wait_ge(done, b + 1)
                pe.wait_ge(m_ready, NH * b + h + 1 + 2)
                for tt in range(NT):
                    for j in range(tt + 1):
                        at = OFF[j] + P * (tt - j)
                        last = nc.tensor.matmul(y_ps[tt // 2][:, DI * (tt % 2) + DS * h:DI * (tt % 2) + DS * h + DS],
                                                mm[h % 2][:, at:at + P], xc[p][:, j, DS * h:DS * h + DS],
                                                start=(j == 0), stop=(j == tt))
                last.then_inc(weighed, 1)

            def turn_y(b):
                pe.wait_ge(yg_ready, b + 1)
                for f in range(2):
                    for tt in range(NT):
                        last = nc.tensor.transpose(y_ps[f][:, P * tt:P * tt + P], y1[:, tt, P * f:P * f + P], c.ident[:])
                last.then_inc(ygt_ready, 1)

            def project_out(b):
                pe.wait_ge(ygt_copied, b + 1)
                for f in range(2):
                    last = nc.tensor.matmul(y_ps[0], w_out[:, f], ygt[:, f], start=(f == 0), stop=(f == 1))
                last.then_inc(o_ready, 1)

            def front(u, p):
                project_bc(u)
                for j in range(NT):
                    project_zx(u, j)
                mean(u)
                variance(u)
                swap_pairs(u)
                row_of(u, 0)
                row_of(u, 1)
                c_times_b(u)

            def cycle(b, p, more):
                u = b + 1
                if more:
                    project_bc(u)
                head(b, p, 0)
                if more:
                    project_zx(u, 0)
                    project_zx(u, 1)
                    mean(u)
                row_of(b, 2)
                head(b, p, 1)
                if more:
                    project_zx(u, 2)
                    project_zx(u, 3)
                    variance(u)
                row_of(b, 3)
                head(b, p, 2)
                if more:
                    swap_pairs(u)
                head(b, p, 3)
                if more:
                    row_of(u, 0)
                    row_of(u, 1)
                    c_times_b(u)
                turn_y(b)
                project_out(b)

            over_batches(pe, front, cycle)

        @block.scalar
        def _(act):
            nc.scalar.preload_act_table_set(LN_EXP)
            act.wait_ge(loaded, 16 * N_LOADS)

            def copy_bc(u):
                act.wait_ge(bc_ready, u + 1)
                nc.scalar.activation(bc[:], bc_ps, ACT.Copy).then_inc(ln.y, 1)

            def copy_zx(u, p, j):
                act.wait_ge(zx_ready, NT * u + j + 1)
                if j == 0 and not first(u):
                    act.wait_ge(zs_ready, u)
                ps = zx_ps[j % 2]
                nc.scalar.activation(ez[:, j], ps[:, 0:DI], ACT.Exp, scale=-1.0)
                nc.scalar.activation(z[:, j], ps[:, 0:DI], ACT.Copy)
                nc.scalar.activation(xt[p][:, j], ps[:, DI:], ACT.Copy).then_inc(zx_copied, 1)

            def square(u):
                act.wait_ge(ln.cent, u + 1)
                nc.scalar.activation(sq[:], cent[:], ACT.Square).then_inc(ln.sq, 1)

            def inverse_deviation(u):
                act.wait_ge(ln.var, u + 1)
                nc.scalar.activation(var_ps, var_ps, ACT.Ln, bias=c.eps[:]).then_inc(ln.log, 1)
                act.wait_ge(ln.log, u + 1)
                nc.scalar.activation(var_ps, var_ps, ACT.Exp, scale=-0.5).then_inc(ln.rstd, 1)

            def sigmoid(u):
                act.wait_ge(z_clamped, u + 1)
                nc.scalar.activation(ez[:], ez[:], ACT.Ln).then_inc(z_log, 1)
                act.wait_ge(z_log, u + 1)
                nc.scalar.activation(ez[:], ez[:], ACT.Exp, scale=-1.0).then_inc(z_sig, 1)

            def decays(b, p, h):
                act.wait_ge(diag_ready, NH * b + h + 1)
                act.wait_ge(m_ready, NH * b + h + 1)
                for j in range(NT):
                    n1 = cq[p][:, 1, j, h:h + 1]
                    last = nc.scalar.activation(e[h % 2][:, OFF[j]:OFF[j] + P], diag[h % 2][:, P * j:P * j + P], ACT.Exp, bias=n1)
                    if j < NT - 1:
                        last = nc.scalar.activation(e[h % 2][:, OFF[j] + P:OFF[j] + WID[j]], n_ps[h % 2][:, P * (j + 1):],
                                                    ACT.Exp, scale=-1.0, bias=n1)
                last.then_inc(e_ready, 1)

            def copy_cb(u, p):
                for j in range(NT):
                    act.wait_ge(cb_ready, NT * u + j + 1)
                    last = nc.scalar.activation(cbs[p][:, OFF[j]:OFF[j] + WID[j]], cb_ps[j][:, 0:WID[j]], ACT.Copy)
                last.then_inc(cb_copied, 1)

            def copy_y(b):
                act.wait_ge(ygt_ready, b + 1)
                for f in range(2):
                    last = nc.scalar.activation(ygt[:, f], y_ps[f], ACT.Copy)
                last.then_inc(ygt_copied, 1)

            def front(u, p):
                copy_bc(u)
                for j in range(NT):
                    copy_zx(u, p, j)
                square(u)
                inverse_deviation(u)
                sigmoid(u)
                decays(u, p, 0)
                copy_cb(u, p)
                decays(u, p, 1)

            def cycle(b, p, more):
                u, n = b + 1, 1 - p
                if more:
                    copy_bc(u)
                    copy_zx(u, n, 0)
                    copy_zx(u, n, 1)
                decays(b, p, 2)
                if more:
                    square(u)
                    copy_zx(u, n, 2)
                    copy_zx(u, n, 3)
                    inverse_deviation(u)
                decays(b, p, 3)
                if more:
                    sigmoid(u)
                    decays(u, n, 0)
                    copy_cb(u, n)
                copy_y(b)
                if more:
                    decays(u, n, 1)

            over_batches(act, front, cycle)

        @block.vector
        def _(dve):
            dve.wait_ge(loaded, 16 * N_LOADS)
            dve.sem_inc(done, 1)
            dve.sem_inc(e_ready, 2)

            def coefficients(u, p):
                nc.vector.tensor_scalar(cq[p][:], cols[:, :, :, bass.ds(NH * u, NH)], 1.0, None, ALU.mult).then_inc(cq_ready, 1)

            def centre(u):
                dve.wait_ge(ln.mean, u + 1)
                nc.vector.tensor_tensor(cent[:], bc[:], mean_ps, ALU.subtract).then_inc(ln.cent, 1)

            def clamp(u):
                dve.wait_ge(zx_copied, NT * u + NT)
                nc.vector.tensor_scalar(ez[:], ez[:], 1e18, 1.0, ALU.min, ALU.add).then_inc(z_clamped, 1)

            def scale_bc(u):
                dve.wait_ge(ln.rstd, u + 1)
                nc.vector.tensor_tensor(v0[:], cent[:], var_ps, ALU.mult).then_inc(ln.out, 1)
                dve.wait_ge(ln.out, u + 1)
                nc.vector.tensor_scalar(v[:], v0[:], vec[:, 0:1], vec[:, 1:2], ALU.mult, ALU.add).then_inc(v_ready, 1)
                dve.wait_ge(v_ready, u + 1)
                nc.vector.tensor_tensor(t1[:], v[:], cos[:, u], ALU.mult)

            def rotate(u):
                dve.wait_ge(swapped, u + 1)
                nc.vector.tensor_tensor(t2[:], sin[:, u], swap_ps, ALU.mult).then_inc(turned, 1)
                dve.wait_ge(turned, u + 1)
                nc.vector.tensor_tensor(brot[:], t1[0:DS], t2[0:DS], ALU.add)
                nc.vector.tensor_tensor(crot[:], t1[DS:P], t2[DS:P], ALU.add).then_inc(rotated, 1)

            def weigh_x(u, p):
                dve.wait_ge(cq_ready, u + 1)
                scale = cq[p][:, 0].rearrange("p j h -> p (j h)").unsqueeze(2).to_broadcast([P, NT * NH, DS])
                nc.vector.tensor_tensor(by_head(xc[p][:]), by_head(xt[p][:]), scale, ALU.mult).then_inc(xc_ready, 1)

            def diagonals(b, h):
                dve.wait_ge(n_ready, NH * b + h + 1)
                dve.wait_ge(e_ready, NH * b + h + 1)
                nc.vector.scalar_tensor_tensor(out=diag[h % 2][:], in0=n_ps[h % 2], scalar=-1.0,
                                               in1=later[:].rearrange("p j t -> p (j t)"),
                                               op0=ALU.mult, op1=ALU.add).then_inc(diag_ready, 1)

            def own_token(u, p):
                dve.wait_ge(cb_copied, u + 1)
                for j in range(NT):
                    last = nc.vector.tensor_tensor(cbw[:, j], c.ident[:], cbs[p][:, OFF[j]:OFF[j] + P], ALU.mult)
                last.then_inc(cbw_ready, 1)
                dve.wait_ge(cbw_ready, u + 1)
                nc.vector.tensor_reduce(cb[:], cbw[:], AX_X, ALU.add).then_inc(cb_diag, 1)
                dve.wait_ge(cb_diag, u + 1)
                nc.vector.tensor_tensor(dcoef[p][:], cq[p][:, 2], cb[:].unsqueeze(2).to_broadcast([P, NT, NH]), ALU.mult).then_inc(dc_part, 1)
                dve.wait_ge(dc_part, u + 1)
                nc.vector.tensor_tensor(dcoef[p][:], dcoef[p][:], d_rep[:], ALU.add).then_inc(dc_ready, 1)

            def gated_y(b, p):
                dve.wait_ge(dc_ready, b + 1)
                nc.vector.tensor_tensor(by_head(y1[:]), by_head(xt[p][:]),
                                        dcoef[p][:].rearrange("p j h -> p (j h)").unsqueeze(2).to_broadcast([P, NT * NH, DS]),
                                        ALU.mult).then_inc(y_part, 1)
                dve.wait_ge(y_part, b + 1)
                dve.wait_ge(weighed, NH * b + NH + 2)
                for f in range(2):
                    last = nc.vector.tensor_tensor(y1[:, 2 * f:2 * f + 2], y1[:, 2 * f:2 * f + 2],
                                                   y_ps[f].rearrange("p (j e) -> p j e", j=2), ALU.add)
                last.then_inc(y_sum, 1)
                dve.wait_ge(y_sum, b + 1)
                dve.wait_ge(zs_ready, b + 1)
                nc.vector.tensor_tensor(y1[:], y1[:], zs[p][:], ALU.mult).then_inc(yg_ready, 1)

            def add(b):
                dve.wait_ge(o_ready, b + 1)
                nc.vector.tensor_tensor(c.resid[:, b], c.resid[:, b], y_ps[0], ALU.add).then_inc(done, 1)

            def front(u, p):
                coefficients(u, p)
                centre(u)
                clamp(u)
                scale_bc(u)
                rotate(u)
                weigh_x(u, p)
                diagonals(u, 0)
                diagonals(u, 1)
                own_token(u, p)

            def cycle(b, p, more):
                u, n = b + 1, 1 - p
                if more:
                    coefficients(u, n)
                    centre(u)
                diagonals(b, 2)
                if more:
                    clamp(u)
                diagonals(b, 3)
                if more:
                    scale_bc(u)
                    rotate(u)
                    weigh_x(u, n)
                    diagonals(u, 0)
                gated_y(b, p)
                if more:
                    diagonals(u, 1)
                    own_token(u, n)
                add(b)

            over_batches(dve, front, cycle)


def phase_state_space(c, d):
    with ExitStack() as ctx:
        ph = Phase(c, ctx)
        dt, ncs = ph.sb("ss_dt", [NR, T]), ph.sb("ss_ncs", [NR, T])
        cols = ph.sb("ss_cols", [P, 3, NT, NR])
        cos, sin = ph.sb("ss_cos", [P, NB, T]), ph.sb("ss_sin", [P, NB, T])
        with ExitStack() as inner:
            state_space_rows(c, d, Phase(c, inner), dt, ncs, cols)
        with ExitStack() as inner:
            state_space_angles(c, d, Phase(c, inner), dt, cos, sin)
        with ExitStack() as inner:
            state_space_outputs(c, d, Phase(c, inner), ncs, cols, cos, sin)
    phase_norm(c, "ss_norm")


DEPTH = 2
LH = 8
LD = 64
INNER = LH * LD
HID = 341
HC = [(0, 128), (128, 128), (256, HID - 256)]
UNITS = 2 * NT
KW = LD + P
NORM_SCALE = 2.0 ** 20


def head_of(half, slot):
    return 4 * half + 2 * (slot % 2) + slot // 2


class LocalWeights:
    def __init__(self, ph):
        self.qk = ph.sb("l_wqk", [P, 2, INNER])
        self.qk_half = ph.sb("l_wqk_half", [P, 2, INNER])
        self.v = ph.sb("l_wv", [P, INNER])
        self.o = ph.sb("l_wo", [P, NT, P])
        self.w1 = ph.sb("l_w1", [P, 2 * HID])
        self.w2 = ph.sb("l_w2", [P, 3, P])
        self.vec = ph.sb("l_vec", [P, 13])


def local_attention(c, d, ph, w, l, tab, tables, masks, identb, kf, qf):
    nc = c.nc
    s = ph.s
    bank = c.bank
    hx, sq, rinv, th, tsum, v, vh, p, ptb, pta, maxraw, negmax, psum, prec, o, ot, ssm, ssq, rq = (ph.b[n] for n in (
        "hx", "sq", "rinv", "th", "tsum", "v", "vh", "p", "ptb", "pta", "maxraw", "negmax", "psum", "prec", "o", "ot",
        "ssm", "ssq", "rq"))
    score = [bank[0:2], bank[2:4]]
    v_bank = [bank[4], bank[7]]
    k_ss_bank = bank[5]
    q_ss_bank = bank[6][:, 0:NT * LH].rearrange("p (j g e t) -> p j g e t", j=NT, g=2, e=2)
    N_LOADS = 7
    ones_blk, ones_pair = ph.b["ones_blk"], ph.b["ones_pair"]

    def n_of(b):
        return l * NB + b + 1

    def over_batches(engine, front, attention):
        front(n_of(0))
        with engine.Fori(0, NB - 1) as b:
            attention(n_of(b), b, True)
        attention(n_of(NB - 1), NB - 1, False)

    with nc.Block() as block:
        @block.sync
        def _(sp):
            for dst, name in ((w.qk, "l_wqk"), (w.qk_half, "l_wqk_half"), (w.v, "l_wv"), (w.o, "l_wo"),
                              (w.w1, "l_w1"), (w.w2, "l_w2"), (w.vec, "l_vec")):
                sp.dma_start(dst[:], d[name][l]).then_inc(s["w_here"], 16)
            with sp.Fori(0, NB) as b:
                sp.wait_ge(s["hx_used"], n_of(b))
                sp.dma_start(hx[0:LD, :], c.resid[0:LD, b]).then_inc(s["hx_here"], 16)
                sp.dma_start(hx[LD:P, 1:T], c.resid[LD:P, b, 0:T - 1]).then_inc(s["hx_here"], 16)

        @block.gpsimd
        def _(pool):
            with pool.Fori(0, NB) as b:
                for m in range(8):
                    g = (n_of(b) - 1) * 8 + m
                    pool.wait_ge(s["halves"], g + 1 + 2)
                    if m % 2 == 0:
                        nc.gpsimd.tensor_tensor(qf[:, m // 2], th[0][:, 0], th[0][:, 1], ALU.add).then_inc(s["qk_done"], 1)
                    else:
                        gk = (n_of(b) - 1) * 4 + m // 2
                        nc.gpsimd.tensor_tensor(tsum[m // 2 % 2][:], th[1][:, 0], th[1][:, 1], ALU.add).then_inc(s["k_summed"], 1)
                        pool.wait_ge(s["rinv"], gk + 1)
                        pool.wait_ge(s["k_summed"], gk + 1)
                        nc.gpsimd.tensor_tensor(kf[:, m // 2], tsum[m // 2 % 2][:], rinv[m // 2 % 2][:], ALU.mult).then_inc(s["qk_done"], 1)

        @block.tensor
        def _(pe):
            def project(n, m):
                q, mm = m % 2, m // 2
                pe.wait_ge(s["halves"], 8 * (n - 1) + m - 1 + 2)
                cols = slice(P * mm, P * mm + P)
                nc.tensor.matmul(bank[2 * q], w.qk[:, q, cols], hx[:], start=True, stop=True)
                nc.tensor.matmul(bank[2 * q + 1], w.qk_half[:, q, cols], hx[:], start=True, stop=True).then_inc(s["projected"], 1)

            def norms(n, m):
                pe.wait_ge(s["squared"], 8 * (n - 1) + m + 1)
                if m % 2:
                    pe.wait_ge(s["k_ss_read"], 4 * (n - 1) + m // 2 + 1)
                    nc.tensor.matmul(k_ss_bank, ones_blk[:], sq[m % 3][:], start=True, stop=True).then_inc(s["k_ss"], 1)
                else:
                    mm = m // 2
                    for j in range(NT):
                        last = nc.tensor.matmul(q_ss_bank[:, j, mm // 2, :, mm % 2], sq[m % 3][:, P * j:P * j + P], ones_pair[:],
                                                start=True, stop=True)
                    last.then_inc(s["q_ss"], 1)

            def values(n, j, after_batch):
                if j == 1 and after_batch:
                    pe.wait_ge(s["added"], n - 1)
                if j >= 2:
                    pe.wait_ge(s["v_copied"], NT * (n - 1) + j - 1)
                nc.tensor.matmul(v_bank[j % 2], hx[:, P * j:P * j + P], w.v[:], start=True, stop=True).then_inc(s["v_ready"], 1)

            def front_end(n, after_batch):
                for m in range(4, 8):
                    project(n, m)
                    norms(n, m - 1)
                norms(n, 7)
                for j in range(NT):
                    values(n, j, after_batch)

            def front(n):
                pe.wait_ge(s["w_here"], 16 * N_LOADS * (l + 1))
                pe.wait_ge(s["hx_here"], 32 * n)
                for m in range(4):
                    project(n, m)
                    if m:
                        norms(n, m - 1)
                front_end(n, False)

            def attention(n, b, more):
                def scores(u):
                    j, hg = divmod(u, 2)
                    lo = LD if j == 0 else 0
                    if u < 2:
                        pe.wait_ge(s["qk_done"], 8 * (n - 1) + 4 + 4 * u)
                    for e in range(2):
                        for k in range(2):
                            nc.tensor.matmul(score[u % 2][k][:, 256 * e + lo:256 * e + KW], identb[:], masks[:, lo:KW],
                                             start=True, stop=False)
                        for k in range(2):
                            h = head_of(hg, 2 * k + e)
                            rows = slice(LD * (h % 2), LD * (h % 2) + LD)
                            last = nc.tensor.matmul(score[u % 2][k][:, 256 * e + lo:256 * e + KW],
                                                    qf[rows, h // 2, P * j:P * j + P],
                                                    kf[rows, h // 2, P * j - LD + lo:P * j + P], start=False, stop=True)
                    last.then_inc(s["scored"], 1)

                def turn(u):
                    j = u // 2
                    pe.wait_ge(s["exped"], UNITS * (n - 1) + u + 1)
                    for hh in range(4):
                        last = nc.tensor.transpose(bank[4][:, P * hh:P * hh + P], p[u % 2][:, hh, LD:KW], c.ident[:])
                    if j:
                        for hh in range(4):
                            last = nc.tensor.transpose(bank[5][0:LD, P * hh:P * hh + P], p[u % 2][:, hh, 0:LD], c.ident[:])
                    last.then_inc(s["p_turned"], 1)

                def weigh(u):
                    j, hg = divmod(u, 2)
                    pe.wait_ge(s["ptb_copied"], UNITS * (n - 1) + u + 1)
                    pe.wait_ge(s["pta_copied"], UNITS * (n - 1) + u + 1)
                    for hh in range(4):
                        at = slice(LD * head_of(hg, hh), LD * head_of(hg, hh) + LD)
                        if j:
                            nc.tensor.matmul(bank[6][:, at], pta[u % 2][:, P * hh:P * hh + P], vh[:, j, at], start=True, stop=False)
                        last = nc.tensor.matmul(bank[6][:, at], ptb[u % 2][:, P * hh:P * hh + P], v[:, j, at], start=(j == 0), stop=True)
                    last.then_inc(s["weighed"], 1)

                def turn_out(j):
                    pe.wait_ge(s["o_normed"], NT * (n - 1) + j + 1)
                    if j:
                        pe.wait_ge(s["ot_copied"], NT * (n - 1) + j)
                    for m in range(NT):
                        last = nc.tensor.transpose(bank[7][:, P * m:P * m + P], o[:, P * m:P * m + P], c.ident[:])
                    last.then_inc(s["o_turned"], 1)

                def project_out():
                    pe.wait_ge(s["ot_copied"], NT * n)
                    for m in range(NT):
                        last = nc.tensor.matmul(bank[7], w.o[:, m], ot[:, m], start=(m == 0), stop=(m == NT - 1))
                    last.then_inc(s["o_ready"], 1)

                scores(0)
                scores(1)
                pe.wait_ge(s["v_copied"], NT * n)
                pe.sem_inc(s["hx_used"], 1)
                for u in range(UNITS - 1):
                    turn(u)
                    if u + 2 < UNITS:
                        scores(u + 2)
                    if u % 2 == 0 and u:
                        turn_out(u // 2 - 1)
                    weigh(u)
                if more:
                    pe.wait_ge(s["hx_here"], 32 * n + 32)
                    project(n + 1, 0)
                turn(UNITS - 1)
                if more:
                    project(n + 1, 1)
                weigh(UNITS - 1)
                if more:
                    project(n + 1, 2)
                    norms(n + 1, 1)
                turn_out(NT - 1)
                if more:
                    norms(n + 1, 0)
                    project(n + 1, 3)
                    norms(n + 1, 2)
                project_out()
                if more:
                    front_end(n + 1, True)

            over_batches(pe, front, attention)

        @block.scalar
        def _(act):
            nc.scalar.preload_act_table_set(LN_EXP)

            def square(n, m):
                act.wait_ge(s["projected"], 8 * (n - 1) + m + 1)
                if m >= 3:
                    act.wait_ge(s["q_ss" if m % 2 else "k_ss"], 4 * (n - 1) + (m - 3) // 2 + 1)
                nc.scalar.activation(sq[m % 3][:], bank[2 * (m % 2)], ACT.Square).then_inc(s["squared"], 1)

            def k_inverse_norm(n, mm):
                g = 4 * (n - 1) + mm
                act.wait_ge(s["k_ss_read"], g + 1 + 1)
                if mm >= 2:
                    act.wait_ge(s["qk_done"], 8 * (n - 1) + 2 * mm - 2)
                nc.scalar.activation(rinv[mm % 2][:], ssm[mm % 2][:], ACT.Ln, scale=NORM_SCALE).then_inc(s["ss_log"], 1)
                act.wait_ge(s["ss_log"], g + 1)
                nc.scalar.activation(rinv[mm % 2][:], rinv[mm % 2][:], ACT.Exp, scale=-0.5).then_inc(s["rinv"], 1)

            def q_inverse_norms(n):
                act.wait_ge(s["q_ss_read"], n)
                nc.scalar.activation(rq[:], ssq[:], ACT.Ln, scale=NORM_SCALE).then_inc(s["q_ss_log"], 1)
                act.wait_ge(s["q_ss_log"], n)
                nc.scalar.activation(rq[:], rq[:], ACT.Exp, scale=-0.5).then_inc(s["rq"], 1)

            def copy_v(n, j):
                act.wait_ge(s["v_ready"], NT * (n - 1) + j + 1)
                last = nc.scalar.activation(v[:, j], v_bank[j % 2], ACT.Copy)
                if j + 1 < NT:
                    last = nc.scalar.activation(vh[:, j + 1], v_bank[j % 2][LD:P, :], ACT.Copy)
                last.then_inc(s["v_copied"], 1)

            def front_end(n):
                for m in range(4, 8):
                    square(n, m)
                    if m % 2 == 0:
                        k_inverse_norm(n, m // 2 - 1)
                q_inverse_norms(n)
                copy_v(n, 0)
                k_inverse_norm(n, 3)
                for j in range(1, NT):
                    copy_v(n, j)

            def front(n):
                for m in range(3):
                    square(n, m)
                k_inverse_norm(n, 0)
                square(n, 3)
                front_end(n)

            def attention(n, b, more):
                def exps(u):
                    j = u // 2
                    lo = LD if j == 0 else 0
                    act.wait_ge(s["negmax"], UNITS * (n - 1) + u + 1)
                    for hh in range(4):
                        ps = score[u % 2][hh // 2][:, 256 * (hh % 2) + lo:256 * (hh % 2) + KW]
                        at = 4 * (u % 2) + hh
                        last = nc.scalar.activation(p[u % 2][:, hh, lo:KW], ps, ACT.Exp, bias=negmax[u % 2][:, hh:hh + 1],
                                                    scale=rq[:, j, at:at + 1],
                                                    accum_out=psum[:, j % 2, head_of(u % 2, hh):head_of(u % 2, hh) + 1])
                    last.then_inc(s["exped"], 1)

                def copy_a(u):
                    act.wait_ge(s["p_turned"], UNITS * (n - 1) + u + 1)
                    if u >= 2:
                        nc.scalar.activation(pta[u % 2][:], bank[5][0:LD, :], ACT.Copy).then_inc(s["pta_copied"], 1)
                    else:
                        act.sem_inc(s["pta_copied"], 1)

                exps(0)
                for u in range(UNITS - 1):
                    exps(u + 1)
                    copy_a(u)
                if more:
                    square(n + 1, 0)
                copy_a(UNITS - 1)
                if more:
                    square(n + 1, 1)
                    square(n + 1, 2)
                    k_inverse_norm(n + 1, 0)
                    square(n + 1, 3)
                    front_end(n + 1)

            over_batches(act, front, attention)

        @block.vector
        def _(dve):
            dve.wait_ge(s["w_here"], 16 * N_LOADS * (l + 1))
            for k in range(4):
                nc.vector.tensor_scalar(tab[:, k], tables[:, k], w.vec[:, k:k + 1], (8.0 if k < 2 else 1.0) * NORM_SCALE ** 0.5,
                                        ALU.mult, ALU.mult).then_inc(s["tables_done"], 1)
            dve.wait_ge(s["tables_done"], 4 * (l + 1))

            def halves(n, m):
                q = m % 2
                g = 8 * (n - 1) + m
                dve.wait_ge(s["squared"], g + 1)
                if m >= 2:
                    if q:
                        dve.wait_ge(s["k_summed"], 4 * (n - 1) + m // 2)
                    else:
                        dve.wait_ge(s["qk_done"], g - 1)
                nc.vector.tensor_tensor(th[q][:, 0], bank[2 * q], tab[:, 2 * q], ALU.mult)
                nc.vector.tensor_tensor(th[q][:, 1], bank[2 * q + 1], tab[:, 2 * q + 1], ALU.mult).then_inc(s["halves"], 1)

            def read_k_norm(n, mm):
                dve.wait_ge(s["k_ss"], 4 * (n - 1) + mm + 1)
                if mm >= 2:
                    dve.wait_ge(s["ss_log"], 4 * (n - 1) + mm - 1)
                nc.vector.tensor_scalar(ssm[mm % 2][:], k_ss_bank, 1e-24, None, ALU.max).then_inc(s["k_ss_read"], 1)

            def front_end(n):
                for m in range(4, 8):
                    halves(n, m)
                    if m % 2 == 0:
                        read_k_norm(n, m // 2 - 1)
                dve.wait_ge(s["q_ss"], 4 * n)
                nc.vector.tensor_scalar(ssq[:], bank[6][:, 0:NT * LH].rearrange("p (j h) -> p j h", j=NT),
                                        1e-24, None, ALU.max).then_inc(s["q_ss_read"], 1)
                read_k_norm(n, 3)

            def front(n):
                for m in range(3):
                    halves(n, m)
                read_k_norm(n, 0)
                halves(n, 3)
                front_end(n)

            def attention(n, b, more):
                def maxima(u):
                    j, hg = divmod(u, 2)
                    lo = LD if u < 2 else 0
                    if u == 0:
                        dve.wait_ge(s["rq"], n)
                    dve.wait_ge(s["scored"], UNITS * (n - 1) + u + 1)
                    for k in range(2):
                        ps = score[u % 2][k].rearrange("p (e t) -> p e t", e=2)[:, :, lo:KW]
                        last = nc.vector.tensor_reduce(maxraw[u % 2][:, 2 * k:2 * k + 2], ps, AX_X, ALU.max, negate=True)
                    last.then_inc(s["maxraw"], 1)
                    dve.wait_ge(s["maxraw"], UNITS * (n - 1) + u + 1)
                    nc.vector.tensor_tensor(negmax[u % 2][:], maxraw[u % 2][:], rq[:, j, 4 * hg:4 * hg + 4], ALU.mult).then_inc(s["negmax"], 1)

                def copy_b(u):
                    dve.wait_ge(s["p_turned"], UNITS * (n - 1) + u + 1)
                    nc.vector.tensor_scalar(ptb[u % 2][:], bank[4], 1.0, None, ALU.mult).then_inc(s["ptb_copied"], 1)

                def normalise(j):
                    dve.wait_ge(s["exped"], UNITS * (n - 1) + 2 * j + 2)
                    nc.vector.reciprocal(prec[:], psum[:, j % 2]).then_inc(s["prec"], 1)
                    dve.wait_ge(s["prec"], NT * (n - 1) + j + 1)
                    dve.wait_ge(s["weighed"], UNITS * (n - 1) + 2 * j + 2)
                    nc.vector.tensor_tensor(o[:].rearrange("p (h e) -> p h e", e=LD), bank[6].rearrange("p (h e) -> p h e", e=LD),
                                            prec[:].unsqueeze(2).to_broadcast([P, LH, LD]), ALU.mult).then_inc(s["o_normed"], 1)

                def copy_ot(j):
                    dve.wait_ge(s["o_turned"], NT * (n - 1) + j + 1)
                    nc.vector.tensor_scalar(ot[:, :, P * j:P * j + P], bank[7].rearrange("p (m t) -> p m t", m=NT),
                                            1.0, None, ALU.mult).then_inc(s["ot_copied"], 1)

                def add():
                    dve.wait_ge(s["o_ready"], n)
                    nc.vector.tensor_tensor(c.resid[:, b], c.resid[:, b], bank[7], ALU.add).then_inc(s["added"], 1)

                maxima(0)
                maxima(1)
                for u in range(UNITS - 1):
                    copy_b(u)
                    if u + 2 < UNITS:
                        maxima(u + 2)
                    if u % 2 == 0 and u:
                        copy_ot(u // 2 - 1)
                    if u % 2:
                        normalise(u // 2)
                if more:
                    halves(n + 1, 0)
                copy_b(UNITS - 1)
                if more:
                    halves(n + 1, 1)
                normalise(NT - 1)
                if more:
                    halves(n + 1, 2)
                    read_k_norm(n + 1, 0)
                copy_ot(NT - 1)
                if more:
                    halves(n + 1, 3)
                add()
                if more:
                    front_end(n + 1)

            over_batches(dve, front, attention)


def local_norm(c, ph, w, l):
    nc = c.nc
    s = ph.s
    y, cent, sq = ph.b["ny"], ph.b["th"], ph.b["sq"]
    norms = ph.norms
    with nc.Block() as block:
        @block.sync
        def _(sp):
            with sp.Fori(0, NB // 2) as i:
                for p in range(2):
                    n = l * (NB // 2) + i
                    b = 2 * i + p
                    sp.wait_ge(norms[p].cent, n + 1)
                    sp.dma_start(y[p][0:LD, :], c.resid[0:LD, b]).then_inc(norms[p].y, 16)
                    sp.dma_start(y[p][LD:P, 1:T], c.resid[LD:P, b, 0:T - 1]).then_inc(norms[p].y, 16)

        @block.tensor
        def _(pe):
            with pe.Fori(0, NB // 2) as i:
                n = l * (NB // 2) + i + 1
                for p in range(2):
                    pe.wait_ge(norms[p].y, 32 * n)
                    nc.tensor.matmul(c.bank[p][:], c.ones[:], y[p][:], start=True, stop=True).then_inc(norms[p].mean, 1)
                for p in range(2):
                    pe.wait_ge(norms[p].sq, n)
                    pe.wait_ge(norms[p].out, n)
                    nc.tensor.matmul(c.bank[2 + p][:], c.ones[:], sq[p][:], start=True, stop=True).then_inc(norms[p].var, 1)

        @block.scalar
        def _(act):
            nc.scalar.preload_act_table_set(LN_EXP)
            with act.Fori(0, NB // 2) as i:
                n = l * (NB // 2) + i + 1
                for p in range(2):
                    act.wait_ge(norms[p].cent, n + 1)
                    nc.scalar.activation(sq[p][:], cent[p][:, 0], ACT.Square).then_inc(norms[p].sq, 1)
                for p in range(2):
                    var = c.bank[2 + p]
                    act.wait_ge(norms[p].var, n)
                    nc.scalar.activation(var[:], var[:], ACT.Ln, bias=c.eps[:]).then_inc(norms[p].log, 1)
                    act.wait_ge(norms[p].log, n)
                    nc.scalar.activation(var[:], var[:], ACT.Exp, scale=-0.5).then_inc(norms[p].rstd, 1)

        @block.vector
        def _(dve):
            with dve.Fori(0, NB // 2) as i:
                n = l * (NB // 2) + i + 1
                for p in range(2):
                    dve.wait_ge(norms[p].mean, n)
                    nc.vector.tensor_tensor(cent[p][:, 0], y[p][:], c.bank[p][:], ALU.subtract).then_inc(norms[p].cent, 1)
                for p in range(2):
                    dve.wait_ge(norms[p].rstd, n)
                    nc.vector.tensor_tensor(cent[p][:, 1], cent[p][:, 0], c.bank[2 + p][:], ALU.mult).then_inc(norms[p].out, 1)
                for p in range(2):
                    dve.wait_ge(norms[p].out, n + 1)
                    nc.vector.tensor_scalar(c.normed[:, 2 * i + p], cent[p][:, 1], w.vec[:, 4:5], w.vec[:, 5:6], ALU.mult, ALU.add)


def local_feed_forward(c, ph, w, l):
    nc = c.nc
    s = ph.s
    gel, hid = ph.b["gel"], ph.b["hid"]
    a_ps, g_ps, o_ps = (c.bank[0], c.bank[1]), (c.bank[2], c.bank[3]), (c.bank[4], c.bank[5])
    STEPS = 6

    with nc.Block() as block:
        @block.tensor
        def _(pe):
            with pe.Fori(0, NB // 2) as i:
                pair = l * (NB // 2) + i

                def up(k):
                    bb, ch = divmod(k, 3)
                    at, rows = HC[ch]
                    x = c.normed[:, 2 * i + bb]
                    pe.wait_ge(s["gated"], STEPS * pair + k - 1 + 2)
                    nc.tensor.matmul(a_ps[k % 2][0:rows, :], w.w1[:, at:at + rows], x, start=True, stop=True)
                    nc.tensor.matmul(g_ps[k % 2][0:rows, :], w.w1[:, HID + at:HID + at + rows], x, start=True, stop=True).then_inc(s["up"], 1)

                def down(k):
                    bb, ch = divmod(k, 3)
                    rows = HC[ch][1]
                    pe.wait_ge(s["gated"], STEPS * pair + k + 1 + 2)
                    if ch == 0:
                        pe.wait_ge(s["f_added"], 2 * pair + bb + 1)
                    last = nc.tensor.matmul(o_ps[bb][:], w.w2[0:rows, ch], hid[k % 3][0:rows, :], start=(ch == 0), stop=(ch == 2))
                    if ch == 2:
                        last.then_inc(s["down"], 1)

                for k in range(STEPS):
                    up(k)
                    if k:
                        down(k - 1)
                down(STEPS - 1)

        @block.scalar
        def _(act):
            with act.Fori(0, NB // 2) as i:
                for k in range(STEPS):
                    ch = k % 3
                    rows = HC[ch][1]
                    act.wait_ge(s["up"], STEPS * (l * (NB // 2) + i) + k + 1)
                    nc.scalar.activation(gel[k % 2][0:rows, :], g_ps[k % 2][0:rows, :], ACT.Gelu,
                                         bias=w.vec[0:rows, 9 + ch:10 + ch]).then_inc(s["gelu"], 1)

        @block.vector
        def _(dve):
            with dve.Fori(0, NB // 2) as i:
                pair = l * (NB // 2) + i

                def add(bb):
                    dve.wait_ge(s["down"], 2 * pair + bb + 1)
                    x = c.resid[:, 2 * i + bb]
                    nc.vector.scalar_tensor_tensor(out=x, in0=o_ps[bb][:], scalar=w.vec[:, 12:13], in1=x,
                                                   op0=ALU.add, op1=ALU.add).then_inc(s["f_added"], 1)

                for k in range(STEPS):
                    ch = k % 3
                    rows = HC[ch][1]
                    dve.wait_ge(s["gelu"], STEPS * pair + k + 1)
                    nc.vector.scalar_tensor_tensor(out=hid[k % 3][0:rows, :], in0=a_ps[k % 2][0:rows, :],
                                                   scalar=w.vec[0:rows, 6 + ch:7 + ch], in1=gel[k % 2][0:rows, :],
                                                   op0=ALU.add, op1=ALU.mult).then_inc(s["gated"], 1)
                    if k == 3:
                        add(0)
                add(1)


def phase_local(c, d):
    nc = c.nc
    with ExitStack() as ctx:
        ph = Phase(c, ctx)
        w = LocalWeights(ph)
        tables = ph.sb("l_tables", [P, 4, T])
        tab = ph.sb("l_tab", [P, 4, T])
        masks = ph.sb("l_masks", [P, KW], BF16)
        identb = ph.sb("l_identb", [P, P], BF16)
        qf, kf = ph.sb("l_q", [P, NT, T]), ph.sb("l_k", [P, NT, T])
        ph.b = dict(
            hx=ph.sb("l_hx", [P, T]), ones_blk=ph.sb("l_ones_blk", [P, P]), ones_pair=ph.sb("l_ones_pair", [P, 2]),
            ssq=ph.sb("l_ssq", [P, NT, LH]), rq=ph.sb("l_rq", [P, NT, LH]), maxraw=[ph.sb(f"l_maxraw{k}", [P, 4]) for k in range(2)],
            sq=[ph.sb(f"l_sq{k}", [P, T]) for k in range(3)], rinv=[ph.sb(f"l_rinv{k}", [P, T]) for k in range(2)],
            ssm=[ph.sb(f"l_ssm{k}", [P, T]) for k in range(2)],
            th=[ph.sb(f"l_th{k}", [P, 2, T]) for k in range(2)], tsum=[ph.sb(f"l_tsum{k}", [P, T]) for k in range(2)],
            v=ph.sb("l_v", [P, NT, INNER]), vh=ph.sb("l_vh", [LD, NT, INNER]),
            p=[ph.sb(f"l_p{k}", [P, 4, KW]) for k in range(2)], ptb=[ph.sb(f"l_ptb{k}", [P, 4 * P]) for k in range(2)],
            pta=[ph.sb(f"l_pta{k}", [LD, 4 * P]) for k in range(2)], negmax=[ph.sb(f"l_negmax{k}", [P, 4]) for k in range(2)],
            psum=ph.sb("l_psum", [P, 2, LH]), prec=ph.sb("l_prec", [P, LH]), o=ph.sb("l_o", [P, INNER]),
            ot=ph.sb("l_ot", [P, NT, T]), ny=[ph.sb(f"l_ny{k}", [P, T]) for k in range(2)],
            gel=[ph.sb(f"l_gel{k}", [P, T]) for k in range(2)], hid=[ph.sb(f"l_hid{k}", [P, T]) for k in range(3)])
        ph.s = {n: ph.sem(f"p5_{n}") for n in (
            "loaded", "w_here", "hx_here", "hx_used", "tables_done", "v_ready", "v_copied", "projected", "squared",
            "k_ss", "k_ss_read", "q_ss", "q_ss_read", "ss_log", "rinv", "q_ss_log", "rq", "halves", "k_summed", "qk_done",
            "scored", "maxraw", "negmax", "exped", "p_turned", "ptb_copied",
            "pta_copied", "weighed", "prec", "o_normed", "o_turned", "ot_copied", "o_ready", "added",
            "up", "gelu", "gated", "down", "f_added")}
        ph.norms = [NormSems(ph.sem, f"p5n{p}") for p in range(2)]
        s = ph.s
        with nc.Block() as block:
            @block.sync
            def _(sp):
                for dst, name in ((tables, "l_tables"), (masks, "l_masks"), (identb, "l_identb"), (ph.b["ones_blk"], "l_ones_blk"),
                                  (ph.b["ones_pair"], "l_ones_pair")):
                    sp.dma_start(dst[:], d[name]).then_inc(s["loaded"], 16)
                sp.wait_ge(s["loaded"], 80)

            @block.gpsimd
            def _(pool):
                nc.gpsimd.memset(ph.b["hx"][:], 0.0)
                nc.gpsimd.memset(ph.b["ny"][0][:], 0.0)
                nc.gpsimd.memset(ph.b["ny"][1][:], 0.0)

            @block.vector
            def _(dve):
                dve.sem_inc(s["hx_used"], 1)
                dve.sem_inc(s["halves"], 2)
                dve.sem_inc(s["k_ss_read"], 1)
                dve.sem_inc(s["gated"], 2)
                dve.sem_inc(s["f_added"], 2)
                for p in range(2):
                    dve.sem_inc(ph.norms[p].cent, 1)
                    dve.sem_inc(ph.norms[p].out, 1)

        with nc.Fori(0, DEPTH) as l:
            local_attention(c, d, ph, w, l, tab, tables, masks, identb, kf, qf)
            local_norm(c, ph, w, l)
            local_feed_forward(c, ph, w, l)


def phase_local_attention(c, d):
    nc = c.nc
    with ExitStack() as ctx:
        with nc.Block() as block:
            @block.gpsimd
            def _(pool):
                nc.gpsimd.tensor_copy(c.outer[:], c.resid[:])
        phase_local(c, d)
        with nc.Block() as block:
            @block.vector
            def _(dve):
                for b in range(NB):
                    nc.vector.tensor_tensor(c.resid[:, b], c.resid[:, b], c.outer[:, b], ALU.add)
    phase_norm(c, "last_norm")


def in_slots(w):
    heads = w.reshape(P, 4, 2, 2, 8).transpose(1, 2, 0, 3, 4)
    out = np.zeros((4, 2, P, 2, HR), w.dtype)
    for s in range(len(Q_PART)):
        out[..., SLOT * s:SLOT * s + 8] = heads
    return out.reshape(4, 2, P, P)


def lay_out(i):
    d = {}
    d["x"] = i["L0_attn_x"].transpose(0, 2, 1)
    w_in = i["L0_attn_w_in"].reshape(16, 3, 8, P)
    b_in = i["L0_attn_b_in"].reshape(16, 3, 8)
    d["wv0"] = w_in[:, 2].reshape(P, P).T
    d["bv0"] = b_in[:, 2].reshape(P, 1)
    d["wo0"] = i["L0_attn_w_out"].T
    d["bo0"] = i["L0_attn_b_out"].reshape(P, 1)
    d["ln1_g"] = i["L0_ffn_ln1_g"].reshape(P, 1)
    d["ln1_b"] = i["L0_ffn_ln1_b"].reshape(P, 1)
    d["ident"] = np.eye(P, dtype=np.float32)
    wp = i["L0_ffn_wp"]
    swapped = np.concatenate([wp[64:], wp[:64]], axis=0)
    flat = lambda a: a.transpose(0, 2, 1, 3).reshape(4, P, 2 * P)
    wv = i["L0_ffn_wv"].reshape(P, 4, 32).transpose(1, 0, 2)
    d["rel_w"] = np.concatenate([flat(in_slots(i["L0_ffn_wq"])), flat(in_slots(i["L0_ffn_wk"])), wv], axis=2)
    ab = np.stack([in_slots(wp), in_slots(swapped)], axis=2)
    d["rel_wp"] = ab.transpose(4, 0, 1, 2, 3).reshape(P, 4, 4 * P)
    wo = np.zeros((4, 4, 32, P), np.float32)
    for part in range(3):
        wo[:, :, SLOT * part:SLOT * part + 8] = i["L0_ffn_wo"].reshape(4, 4, 8, P)
    d["rel_wo"] = wo.reshape(4, P, P)
    freq = (1.0 / 10000.0 ** (np.arange(0, P, 2, dtype=np.float32) / np.float32(P))).astype(np.float32)
    angle = freq.astype(np.float64)[:, None] * np.arange(T)[None, :]
    sin, cos = np.sin(angle).astype(np.float32), np.cos(angle).astype(np.float32)
    d["rel_cos"] = np.concatenate([cos, cos])
    d["rel_sin"] = np.concatenate([sin, -sin])
    d["rel_angle"] = np.concatenate([sin, cos])
    part_vec = np.zeros((2, HR, 5), np.float32)
    for s, (qp, kp) in enumerate(zip(Q_PART, K_PART)):
        rows = slice(SLOT * s, SLOT * s + 8)
        part_vec[:, rows, 0] = -float(qp > 0)
        part_vec[:, rows, 1] = -float(qp > 1)
        part_vec[:, rows, 2] = -float(kp > 0)
        part_vec[:, rows, 3] = -float(kp > 1)
        if s < 3:
            part_vec[:, SLOT * s + 8, 2] = 1.0
            part_vec[:, SLOT * s + 8, 4] = 1.0
    d["rel_part_vec"] = part_vec.reshape(P, 5)
    pick = np.zeros((4, 32, 4, 32), np.float32)
    for r in range(4):
        pick[r, 8, r, :] = 1.0
    d["rel_pick_sum"] = pick.reshape(P, P)
    v_aug = np.zeros((P, NT, 4, 32), mybir.dt.np(BF16))
    v_aug[..., 8] = 1.0
    d["rel_v_aug"] = v_aug
    d["ln2_g"] = i["L0_ffn_ln2_g"].reshape(P, 1)
    d["ln2_b"] = i["L0_ffn_ln2_b"].reshape(P, 1)
    d["sel_w"] = i["L0_ffn_sel_w"]
    d["keys"] = i["L0_ffn_keys"]
    d["values"] = i["L0_ffn_values"]
    pick_expert = np.zeros((NE, 3, NE, P), mybir.dt.np(BF16))
    for e in range(NE):
        pick_expert[e, :, e] = 1.0
    d["pick_expert"] = pick_expert.reshape(NE, 3 * NE, P)
    w = i["L1_attn_W_in"]
    at = np.cumsum([0, DI, DI, DS, DS, NH, NH, NH, DS // 2])
    z, x, bp, cp, dd_dt, dd_a, trap, ang = (w[:, at[n]:at[n + 1]] for n in range(8))
    w_rows = np.zeros((P, 3, NB, NB, NH), np.float32)
    for q, part in enumerate((dd_dt, dd_a, trap)):
        for b in range(NB):
            w_rows[:, q, b, b] = part
    d["ss_w_rows"] = w_rows.reshape(P, 3, NB, NR)
    d["ss_dt_bias"] = np.tile(i["L1_attn_dt_bias"], NB).reshape(NR, 1)
    d["ss_w_angle"] = np.tile(ang, (1, 4))
    pairs = lambda a: np.concatenate([a[..., 0::2], a[..., 1::2]], axis=-1)
    d["ss_w_bc"] = np.concatenate([pairs(bp), pairs(cp)], axis=1)
    d["ss_gain"] = np.concatenate([pairs(i["L1_attn_Bn_g"]), pairs(i["L1_attn_Cn_g"])]).reshape(P, 1)
    d["ss_shift"] = np.concatenate([pairs(i["L1_attn_Bn_b"]), pairs(i["L1_attn_Cn_b"])]).reshape(P, 1)
    d["ss_w_zx"] = np.concatenate([z, x], axis=1)
    d["ss_w_out"] = i["L1_attn_W_out"].reshape(2, P, P).transpose(1, 0, 2)
    d["ss_d"] = np.broadcast_to(i["L1_attn_D_param"], (P, NT, NH))
    sign = np.ones((4, 32), np.float32)
    sign[0::2] = -1.0
    d["ss_sign"] = sign.reshape(P, 1)
    pick = np.zeros((NB, NB, NH, NH + 1, P), np.float32)
    for b in range(NB):
        for h in range(NH):
            pick[b, b, h, h] = 1.0
        pick[b, b, :, NH] = 1.0 / NH
    d["ss_pick"] = pick.reshape(NB, NR, (NH + 1) * P)
    d["ones64"] = np.kron(np.eye(2, dtype=np.float32), np.full((DS, DS), 1.0 / DS, np.float32))
    swap = np.zeros((P, P), np.float32)
    swap[np.arange(P) ^ 32, np.arange(P)] = 1.0
    d["ss_swap"] = swap
    d["ss_later"] = np.where(np.arange(P)[None, :] > np.arange(P)[:, None], 0.0, NEG).astype(np.float32)
    w = i["L1_ffn_wqkv"]
    halves = lambda a: a.reshape(DEPTH, -1, LH, 2, LD // 2)[:, :, :, ::-1].reshape(DEPTH, -1, INNER)
    d["l_wqk"] = w[:, :, 0:2 * INNER].reshape(DEPTH, P, 2, INNER)
    d["l_wqk_half"] = np.stack([halves(w[:, :, 0:INNER]), halves(w[:, :, INNER:2 * INNER])], axis=2)
    d["l_wv"] = w[:, :, 2 * INNER:]
    d["l_wo"] = i["L1_ffn_wo"].reshape(DEPTH, NT, P, P).transpose(0, 2, 1, 3)
    d["l_w1"] = i["L1_ffn_w1"]
    w2 = np.zeros((DEPTH, 3 * P, P), np.float32)
    w2[:, 0:HID] = i["L1_ffn_w2"]
    d["l_w2"] = w2.reshape(DEPTH, 3, P, P).transpose(0, 2, 1, 3)
    vec = np.zeros((DEPTH, P, 13), np.float32)
    for k, g in enumerate((i["L1_ffn_q_scale"], i["L1_ffn_k_scale"])):
        vec[:, :, 2 * k] = np.tile(g, (1, 2))
        vec[:, :, 2 * k + 1] = np.tile(np.roll(g, LD // 2, axis=1), (1, 2))
    vec[:, :, 4] = i["L1_ffn_ln_g"]
    vec[:, :, 5] = i["L1_ffn_ln_b"]
    for ch, (at, rows) in enumerate(HC):
        vec[:, 0:rows, 6 + ch] = i["L1_ffn_b1"][:, at:at + rows]
        vec[:, 0:rows, 9 + ch] = i["L1_ffn_b1"][:, HID + at:HID + at + rows]
    vec[:, :, 12] = i["L1_ffn_b2"]
    d["l_vec"] = vec
    half = np.arange(0, LD, 2, dtype=np.float32)
    freq = (1.0 / 10000.0 ** (half / np.float32(LD))).astype(np.float32).astype(np.float64)
    t = np.arange(T, dtype=np.float64)
    base = (half.astype(np.float64) + 0.4 * LD) / (1.4 * LD)
    scale = base[:, None] ** ((t[None, :] - T // 2) / (LD // 2))
    cos, sin = np.cos(freq[:, None] * t), np.sin(freq[:, None] * t)
    tables = np.zeros((P, 4, T), np.float32)
    for k, f in enumerate((scale, 1.0 / scale)):
        tables[:, 2 * k] = np.tile(cos * f, (4, 1))
        tables[:, 2 * k + 1] = np.concatenate([-sin * f, sin * f, -sin * f, sin * f])
    d["l_tables"] = tables
    col, row = np.arange(KW)[None, :], np.arange(P)[:, None]
    d["l_masks"] = np.where((col >= row) & (col <= row + LD), 0.0, NEG).astype(mybir.dt.np(BF16))
    d["l_identb"] = np.eye(P).astype(mybir.dt.np(BF16))
    d["l_ones_blk"] = np.kron(np.eye(2, dtype=np.float32), np.ones((LD, LD), np.float32))
    d["l_ones_pair"] = np.kron(np.eye(2, dtype=np.float32), np.ones((LD, 1), np.float32))
    return d



def build(nc, d, out):
    with ExitStack() as ctx:
        c = Core(nc, ctx)
        phase_first_attention(c, d)
        phase_relative_attention(c, d)
        phase_experts(c, d)
        phase_state_space(c, d)
        phase_local_attention(c, d)
        store(c, out)


def store(c, out):
    nc = c.nc
    with ExitStack() as ctx:
        stored = Phase(c, ctx).sem("stored")
        with nc.Block() as block:
            @block.sync
            def _(sp):
                sp.dma_start(out.rearrange("b p t -> p b t"), c.resid[:]).then_inc(stored, 16)
                sp.wait_ge(stored, 16)


def kernel(**inputs):
    import numpy as _np
    import concourse.bacc as _bacc
    from concourse import mybir as _mybir
    from concourse.bass_utils import run_bass_kernel_spmd as _run

    arrays = lay_out({k: _np.asarray(v) for k, v in inputs.items()})
    nc = _bacc.Bacc("TRN2", target_bir_lowering=False, num_devices=1)
    feeds, d = {}, {}
    for name, a in arrays.items():
        a = _np.ascontiguousarray(a)
        feeds[f"in_{name}"] = a
        d[name] = nc.dram_tensor(f"in_{name}", a.shape, _mybir.dt.from_np(a.dtype), kind="ExternalInput").ap()
    out = nc.dram_tensor("out_0", (NB, P, T), F32, kind="ExternalOutput").ap()
    build(nc, d, out)
    r = _run(nc, [feeds], core_ids=[0])
    return _np.ascontiguousarray(r.results[0]["out_0"].transpose(0, 2, 1))
```

```python
from contextlib import ExitStack

import numpy as np

import concourse.bass as bass
from concourse import mybir

ALU = mybir.AluOpType
ACT = mybir.ActivationFunctionType
F32 = mybir.dt.float32
BF16 = mybir.dt.bfloat16
F16 = mybir.dt.float16
LN_EXP = "natural_log_exp_and_others"
AX_X = mybir.AxisListType.X

P = 128
NB = 8
T = 512
NT = T // P
EPS = 1e-5


class NormSems:
    def __init__(self, sem, name):
        self.y = sem(f"{name}_y_ready")
        self.mean = sem(f"{name}_mean_ready")
        self.cent = sem(f"{name}_centred")
        self.sq = sem(f"{name}_squared")
        self.var = sem(f"{name}_var_ready")
        self.log = sem(f"{name}_log_var")
        self.rstd = sem(f"{name}_rstd")
        self.out = sem(f"{name}_out")


def norms_pe(nc, pe, s, n, ones, y, sq, mean_ps, var_ps):
    for p in range(2):
        pe.wait_ge(s[p].y, n)
        nc.tensor.matmul(mean_ps[p], ones, y[p][:], start=True, stop=True).then_inc(s[p].mean, 1)
    for p in range(2):
        pe.wait_ge(s[p].sq, n)
        nc.tensor.matmul(var_ps[p], ones, sq[p][:], start=True, stop=True).then_inc(s[p].var, 1)


def norms_act(nc, act, s, n, cent, sq, var_ps, eps):
    for p in range(2):
        act.wait_ge(s[p].cent, n)
        nc.scalar.activation(sq[p][:], cent[p][:], ACT.Square).then_inc(s[p].sq, 1)
    for p in range(2):
        act.wait_ge(s[p].var, n)
        nc.scalar.activation(var_ps[p], var_ps[p], ACT.Ln, bias=eps).then_inc(s[p].log, 1)
        act.wait_ge(s[p].log, n)
        nc.scalar.activation(var_ps[p], var_ps[p], ACT.Exp, scale=-0.5).then_inc(s[p].rstd, 1)


def norms_dve(nc, dve, s, n, y, cent, mean_ps, var_ps, out):
    for p in range(2):
        dve.wait_ge(s[p].mean, n)
        nc.vector.tensor_tensor(cent[p][:], y[p][:], mean_ps[p], ALU.subtract).then_inc(s[p].cent, 1)
    for p in range(2):
        dve.wait_ge(s[p].rstd, n)
        nc.vector.tensor_tensor(out[p][:], cent[p][:], var_ps[p], ALU.mult).then_inc(s[p].out, 1)


class Core:

    def __init__(self, nc, ctx):
        self.nc = nc
        self.ctx = ctx
        self.psum = ctx.enter_context(nc.psum_tensor("psum", [P, 8, 512], F32))
        self.bank = [self.psum[:, i] for i in range(8)]
        self.resid = self.sb("resid", [P, NB, T])
        self.normed = self.sb("normed", [P, NB, T])
        self.outer = self.sb("outer", [P, NB, T])
        self.ones = self.sb("ones_mean", [P, P])
        self.eps = self.sb("eps", [P, 1])
        self.ident = self.sb("ident", [P, P])

    def sb(self, name, shape, dt=F32):
        return self.ctx.enter_context(self.nc.sbuf_tensor(name, shape, dt))


class Phase:

    def __init__(self, core, ctx):
        self.nc, self.ctx, self.sems = core.nc, ctx, []
        ctx.callback(self.clear)

    def sb(self, name, shape, dt=F32):
        return self.ctx.enter_context(self.nc.sbuf_tensor(name, shape, dt))

    def sem(self, name):
        s = self.nc.alloc_semaphore(name)
        self.sems.append(s)
        return s

    def clear(self):
        nums = sorted(s.num for s in self.sems)
        with self.nc.Block() as block:
            @block.sync
            def _(sp):
                at = 0
                while at < len(nums):
                    end = at
                    while end + 1 < len(nums) and nums[end + 1] == nums[end] + 1:
                        end += 1
                    sp.sem_clear(range(nums[at], nums[end] + 1))
                    at = end + 1
        for s in self.sems:
            self.nc.release_semaphore(s)


def phase_first_attention(c, d):
    nc = c.nc
    with ExitStack() as ctx:
        ph = Phase(c, ctx)
        wv = ph.sb("wv0", [P, P])
        wo = ph.sb("wo0", [P, P])
        vec = ph.sb("vec0", [P, 4])
        v_sb, y, cent, sq = ([ph.sb(f"{n}0_{p}", [P, T]) for p in range(2)] for n in ("v", "y", "cent", "sq"))
        bias_v, bias_o, gain, shift = (vec[:, i:i + 1] for i in range(4))
        loaded = ph.sem("p1_loaded")
        ones_set = ph.sem("p1_ones_set")
        v_ready, v_biased, o_ready, affine = ([ph.sem(f"p1_{n}{p}") for p in range(2)] for n in ("v", "v_biased", "o", "affine"))
        na, nb_ = ([NormSems(ph.sem, f"p1{n}{p}") for p in range(2)] for n in "ab")
        v_ps, o_ps, mean_ps, var_ps = (c.bank[2 * i:2 * i + 2] for i in range(4))
        N_LOADS = 8

        with nc.Block() as block:
            @block.sync
            def _(sp):
                sp.dma_start(c.resid[:], d["x"].rearrange("b p t -> p b t")).then_inc(loaded, 16)
                sp.dma_start(wv[:], d["wv0"]).then_inc(loaded, 16)
                sp.dma_start(wo[:], d["wo0"]).then_inc(loaded, 16)
                sp.dma_start(vec[:, 0:1], d["bv0"]).then_inc(loaded, 16)
                sp.dma_start(vec[:, 1:2], d["bo0"]).then_inc(loaded, 16)
                sp.dma_start(vec[:, 2:3], d["ln1_g"]).then_inc(loaded, 16)
                sp.dma_start(vec[:, 3:4], d["ln1_b"]).then_inc(loaded, 16)
                sp.dma_start(c.ident[:], d["ident"]).then_inc(loaded, 16)

            @block.gpsimd
            def _(pool):
                nc.gpsimd.memset(c.ones[:], 1.0 / P).then_inc(ones_set, 1)
                nc.gpsimd.memset(c.eps[:], EPS).then_inc(ones_set, 1)

            @block.tensor
            def _(pe):
                pe.wait_ge(loaded, 16 * N_LOADS)
                pe.wait_ge(ones_set, 2)
                with pe.Fori(0, NB // 2) as i:
                    for p in range(2):
                        nc.tensor.matmul(v_ps[p], wv[:], c.resid[:, 2 * i + p], start=True, stop=True).then_inc(v_ready[p], 1)
                    for p in range(2):
                        pe.wait_ge(v_biased[p], i + 1)
                        nc.tensor.matmul(o_ps[p], wo[:], v_sb[p][:], start=True, stop=True).then_inc(o_ready[p], 1)
                    norms_pe(nc, pe, na, i + 1, c.ones[:], y, sq, mean_ps, var_ps)
                    norms_pe(nc, pe, nb_, i + 1, c.ones[:], y, sq, mean_ps, var_ps)

            @block.scalar
            def _(act):
                nc.scalar.preload_act_table_set(LN_EXP)
                act.wait_ge(loaded, 16 * N_LOADS)
                act.wait_ge(ones_set, 2)
                with act.Fori(0, NB // 2) as i:
                    for p in range(2):
                        act.wait_ge(v_ready[p], i + 1)
                        nc.scalar.activation(v_sb[p][:], v_ps[p], ACT.Identity, bias=bias_v).then_inc(v_biased[p], 1)
                    norms_act(nc, act, na, i + 1, cent, sq, var_ps, c.eps[:])
                    norms_act(nc, act, nb_, i + 1, cent, sq, var_ps, c.eps[:])

            @block.vector
            def _(dve):
                dve.wait_ge(loaded, 16 * N_LOADS)
                with dve.Fori(0, NB // 2) as i:
                    for p in range(2):
                        dve.wait_ge(o_ready[p], i + 1)
                        nc.vector.scalar_tensor_tensor(out=y[p][:], in0=o_ps[p], scalar=bias_o, in1=c.resid[:, 2 * i + p],
                                                       op0=ALU.add, op1=ALU.add).then_inc(na[p].y, 1)
                    norms_dve(nc, dve, na, i + 1, y, cent, mean_ps, var_ps, y)
                    for p in range(2):
                        dve.wait_ge(na[p].out, i + 1)
                        nc.vector.tensor_scalar(c.outer[:, 2 * i + p], y[p][:], 1.0, None, ALU.mult)
                        nc.vector.tensor_scalar(c.resid[:, 2 * i + p], y[p][:], 1.0, None, ALU.mult).then_inc(nb_[p].y, 1)
                    norms_dve(nc, dve, nb_, i + 1, y, cent, mean_ps, var_ps, cent)
                    for p in range(2):
                        dve.wait_ge(nb_[p].out, i + 1)
                        nc.vector.tensor_scalar(c.normed[:, 2 * i + p], cent[p][:], gain, shift, ALU.mult, ALU.add).then_inc(affine[p], 1)


HG = 4
TURNS = NB * 4
HR = 64
SLOT = 9
Q_PART = (0, 0, 1, 0, 2, 1)
K_PART = (0, 1, 0, 2, 0, 1)
W_Q, W_K, W_V = 0, 2 * P, 4 * P
W_COLS = 4 * P + 32


def first(u):
    return isinstance(u, int) and u == 0


def phase_relative_attention(c, d):
    nc = c.nc
    SCALE = 8.0 ** -0.5
    with ExitStack() as ctx:
        ph = Phase(c, ctx)
        cos_q = ph.sb("cos_q", [P, T])
        sin_q = ph.sb("sin_q", [P, T])
        angle_k = ph.sb("angle_k", [P, T])
        angle_hi, angle_lo = ph.sb("angle_hi", [P, T], F16), ph.sb("angle_lo", [P, T], F16)
        part_vec = ph.sb("part_vec", [P, 5])
        q_less_h, q_less_m, k_less_h, k_less_m, k_ones = (part_vec[:, n:n + 1] for n in range(5))
        pick_sum = ph.sb("pick_sum", [P, P])
        wp_raw = ph.sb("wp_raw", [P, 4, 4 * P])
        wp_h = ph.sb("wp_h", [P, 4, 4 * P], BF16)
        wp_parts = ph.sb("wp_parts", [P, 4, 4 * P], BF16)
        w = [ph.sb(f"w_group{p}", [P, W_COLS]) for p in range(2)]
        wp = [ph.sb(f"wp_group{p}", [P, 4 * P], BF16) for p in range(2)]
        wo = [ph.sb(f"wo_group{p}", [P, P]) for p in range(2)]
        xs = [ph.sb(f"x_staged{p}", [P, T]) for p in range(2)]
        h6 = ph.sb("split_h", [P, 2, T], BF16)
        rest = ph.sb("split_rest", [P, 2, T])
        m6 = ph.sb("split_m", [P, 2, T], BF16)
        qs = [ph.sb(f"q_parts{p}", [P, 2, T], BF16) for p in range(2)]
        ks = [ph.sb(f"k_parts{p}", [P, 2, T], BF16) for p in range(2)]
        v_rest = ph.sb("v_rest", [P, NT, HG, 8])
        v_m = ph.sb("v_m", [P, NT, HG, 8], BF16)
        v_h = ph.sb("v_h", [P, NT, HG, 8], BF16)
        vaug = [ph.sb(f"v_aug{p}", [P, NT, HG, 32], BF16) for p in range(2)]
        half = ph.sb("turned_halves", [P, 2, 2, T])
        rot = ph.sb("rot", [P, HG, T])
        rot_hi, rot_lo = ([ph.sb(f"rot_{n}{p}", [P, HG, T], F16) for p in range(2)] for n in ("hi", "lo"))
        mx = ph.sb("mx", [P, NT, HG])
        mx_rest = ph.sb("mx_rest", [P, NT, HG])
        mx_part = ph.sb("mx_part", [P, 2, NT, HG], BF16)
        max_wide = ph.sb("max_wide", [P, NT, 2, 2, HR])
        p32 = ph.sb("p32", [P, 4, T])
        p_hi = ph.sb("p_hi", [P, 2, NT, T], F16)
        p_lo = ph.sb("p_lo", [P, 2, NT, T], F16)
        av = ph.sb("av", [P, T])
        rden = ph.sb("rden", [P, T])
        avn = ph.sb("av_normed", [P, T])

        score_ps = c.bank[0:2]
        av_ps, a_ps, b_ps, misc_ps = c.bank[2], c.bank[3], c.bank[4], c.bank[5]
        rough_ps = c.bank[6:8]

        tables = ph.sem("p2_tables")
        set_up = ph.sem("p2_set_up")
        wp_split = ph.sem("p2_wp_split")
        w_here = [ph.sem(f"p2_w_here{p}") for p in range(2)]
        wo_here = [ph.sem(f"p2_wo_here{p}") for p in range(2)]
        qk_ready = ph.sem("p2_qk_ready")
        v_ready = ph.sem("p2_v")
        h_done, rest_done, m_done = ph.sem("p2_h_done"), ph.sem("p2_rest_done"), ph.sem("p2_m_done")
        parts_done = ph.sem("p2_parts_done")
        v_chain, v_done = ph.sem("p2_v_chain"), ph.sem("p2_v_done")
        turned = ph.sem("p2_turned")
        halves = ph.sem("p2_halves")
        rot_ready = ph.sem("p2_rot")
        rot_hi_ready = ph.sem("p2_rot_hi")
        rot_split = ph.sem("p2_rot_split")
        angle_split = ph.sem("p2_angle_split")
        rough = ph.sem("p2_rough")
        maxed = ph.sem("p2_maxed")
        mx_chain, mx_wide = ph.sem("p2_mx_chain"), ph.sem("p2_mx_wide")
        max_turned = ph.sem("p2_max_turned")
        q_final = ph.sem("p2_q_final")
        scored = ph.sem("p2_scored")
        exped = ph.sem("p2_exped")
        hi_done, lo_done = ph.sem("p2_hi_done"), ph.sem("p2_lo_done")
        av_ready, av_copied = ph.sem("p2_av"), ph.sem("p2_av_copied")
        den_ready, den_log, den_inv = ph.sem("p2_den"), ph.sem("p2_den_log"), ph.sem("p2_den_inv")
        avn_ready, o_ready = ph.sem("p2_avn"), ph.sem("p2_o")
        added = ph.sem("p2_added")
        N_TABLES = 8
        MX_STEPS = 4

        with nc.Block() as block:
            @block.sync
            def _(sp):
                sp.dma_start(cos_q[:], d["rel_cos"]).then_inc(tables, 16)
                sp.dma_start(sin_q[:], d["rel_sin"]).then_inc(tables, 16)
                sp.dma_start(angle_k[:], d["rel_angle"]).then_inc(tables, 16)
                sp.dma_start(part_vec[:], d["rel_part_vec"]).then_inc(tables, 16)
                sp.dma_start(pick_sum[:], d["rel_pick_sum"]).then_inc(tables, 16)
                sp.dma_start(wp_raw[:], d["rel_wp"]).then_inc(tables, 16)
                sp.dma_start(vaug[0][:], d["rel_v_aug"]).then_inc(tables, 16)
                sp.dma_start(vaug[1][:], d["rel_v_aug"]).then_inc(tables, 16)

                def load_w(u, p):
                    sp.dma_start(w[p][:], d["rel_w"][u % 4]).then_inc(w_here[p], 16)
                    sp.dma_start(xs[p][:], c.normed[:, (u // 4) % NB]).then_inc(w_here[p], 16)
                    sp.dma_start(wp[p][:], wp_parts[:, u % 4]).then_inc(w_here[p], 16)

                def load_wo(t, p):
                    sp.dma_start(wo[p][:], d["rel_wo"][t % 4]).then_inc(wo_here[p], 16)

                sp.wait_ge(wp_split, 4)
                for p in range(2):
                    load_w(p, p)
                    load_wo(p, p)
                with sp.Fori(0, TURNS // 2 - 1) as i:
                    for p in range(2):
                        t = 2 * i + p
                        sp.wait_ge(turned, HG * (t + 1))
                        load_w(t + 2, p)
                        sp.wait_ge(o_ready, t + 1)
                        load_wo(t + 2, p)

            @block.gpsimd
            def _(pool):
                nc.gpsimd.memset(max_wide[:], 0.0).then_inc(set_up, 1)
                pool.sem_inc(lo_done, 4)

                def turn(u, p, r):
                    pool.wait_ge(halves, HG * u + r + 1)
                    nc.gpsimd.tensor_tensor(rot[:, r], half[:, r % 2, 0], half[:, r % 2, 1], ALU.add).then_inc(rot_ready, 1)

                def turn_low(u, p, r):
                    pool.wait_ge(rot_hi_ready, HG * u + r + 1)
                    nc.gpsimd.tensor_tensor(rot_lo[p][:, r], rot[:, r], rot_hi[p][:, r], ALU.subtract).then_inc(rot_split, 1)

                def low_parts(t, r, tiles=range(NT)):
                    for j in tiles:
                        pool.wait_ge(hi_done, 16 * t + 4 * r + j + 1)
                        nc.gpsimd.tensor_tensor(p_lo[:, r % 2, j], p32[:, j], p_hi[:, r % 2, j], ALU.subtract).then_inc(lo_done, 1)

                def step(t, p):
                    u, n = t + 1, 1 - p
                    turn(u, n, 0)
                    low_parts(t, 1, (0, 1))
                    turn(u, n, 1)
                    low_parts(t, 1, (2, 3))
                    turn_low(u, n, 0)
                    turn_low(u, n, 1)
                    low_parts(t, 2, (0, 1))
                    turn(u, n, 2)
                    low_parts(t, 2, (2, 3))
                    turn(u, n, 3)
                    low_parts(t, 3)
                    turn_low(u, n, 2)
                    turn_low(u, n, 3)
                    low_parts(u, 0)

                pool.wait_ge(angle_split, 1)
                nc.gpsimd.tensor_tensor(angle_lo[:], angle_k[:], angle_hi[:], ALU.subtract).then_inc(set_up, 1)
                for r in range(HG):
                    turn(0, 0, r)
                for r in range(HG):
                    turn_low(0, 0, r)
                low_parts(0, 0)
                with pool.Fori(0, TURNS // 2 - 1) as i:
                    step(2 * i, 0)
                    step(2 * i + 1, 1)
                step(TURNS - 2, 0)
                for r in range(1, HG):
                    low_parts(TURNS - 1, r)

            @block.tensor
            def _(pe):
                pe.wait_ge(tables, 16 * N_TABLES)
                pe.wait_ge(set_up, 2)

                def rows_of(r):
                    return slice(HR * (r % 2), HR * (r % 2) + HR)

                def project_q(u, i, p):
                    pe.wait_ge(w_here[p], 48 * (i + 1))
                    if not first(u):
                        pe.wait_ge(halves, HG * u)
                    for tt, ps in enumerate((a_ps, b_ps)):
                        nc.tensor.matmul(ps, w[p][:, W_Q + P * tt:W_Q + P * tt + P], xs[p][:], start=True, stop=True).then_inc(qk_ready, 1)

                def project_kv(u, p):
                    pe.wait_ge(halves, HG * u + 2)
                    if not first(u):
                        pe.wait_ge(v_done, 2 * u)
                    for tt, ps in enumerate((a_ps, b_ps)):
                        nc.tensor.matmul(ps, w[p][:, W_K + P * tt:W_K + P * tt + P], xs[p][:], start=True, stop=True).then_inc(qk_ready, 1)
                    for j in range(NT):
                        last = nc.tensor.matmul(misc_ps[:, 32 * j:32 * j + 32], xs[p][:, P * j:P * j + P],
                                                w[p][:, W_V:W_V + 32], start=True, stop=True)
                    last.then_inc(v_ready, 1)

                def turn(u, p, r):
                    if r % 2 == 0:
                        pe.wait_ge(parts_done, 4 * u + 2 + r)
                    else:
                        pe.wait_ge(halves, HG * u + r)
                    for n, ps in enumerate((a_ps, b_ps)):
                        at = 2 * P * (r // 2) + P * n
                        last = nc.tensor.matmul(ps, wp[p][rows_of(r), at:at + P], qs[p][rows_of(r), r // 2], start=True, stop=True)
                    last.then_inc(turned, 1)

                def rough_scores(u, p, r, tiles=range(NT)):
                    pe.wait_ge(rot_hi_ready, HG * u + r + 1)
                    for k in tiles:
                        pe.wait_ge(maxed, 16 * u + 4 * r + k + 1)
                        q_tile = slice(P * k, P * k + P)
                        ps = rough_ps[k % 2]
                        nc.tensor.matmul(ps, rot_hi[p][:, r, q_tile], angle_hi[:], start=True, stop=False)
                        nc.tensor.matmul(ps, qs[p][rows_of(r), r // 2, q_tile], ks[p][rows_of(r), r // 2],
                                         start=False, stop=True).then_inc(rough, 1)

                def turn_maxima(u):
                    pe.wait_ge(mx_wide, u + 1)
                    for tt, ps in enumerate(rough_ps):
                        for k in range(NT):
                            last = nc.tensor.transpose(ps[:, P * k:P * k + P], max_wide[:, k, tt].rearrange("p a b -> p (a b)"), c.ident[:])
                    last.then_inc(max_turned, 1)

                def scores(t, p, r, tiles=range(NT)):
                    if r == 0:
                        pe.wait_ge(q_final, 2 * t + 2)
                        pe.wait_ge(rot_split, HG * (t + 1))
                    for j in tiles:
                        keys = slice(P * j, P * j + P)
                        pe.wait_ge(exped, 16 * t + 4 * r + j + 1)
                        ps = score_ps[j % 2]
                        nc.tensor.matmul(ps, angle_hi[:, keys], rot_hi[p][:, r], start=True, stop=False)
                        nc.tensor.matmul(ps, angle_hi[:, keys], rot_lo[p][:, r], start=False, stop=False)
                        nc.tensor.matmul(ps, angle_lo[:, keys], rot_hi[p][:, r], start=False, stop=False)
                        nc.tensor.matmul(ps, ks[p][rows_of(r), r // 2, keys], qs[p][rows_of(r), r // 2], start=False, stop=True).then_inc(scored, 1)

                def weigh_v(t, p, r):
                    if r == 0:
                        pe.wait_ge(added, t + 1)
                        pe.wait_ge(v_done, 2 * t + 2)
                    pe.wait_ge(lo_done, 16 * t + 4 * r + 4 + 4)
                    for j in range(NT):
                        for part in (p_hi, p_lo):
                            last = nc.tensor.matmul(av_ps[32 * r:32 * r + 32, :], vaug[p][:, j, r], part[:, r % 2, j],
                                                    start=(j == 0 and part is p_hi), stop=(j == NT - 1 and part is p_lo))
                    if r == HG - 1:
                        last.then_inc(av_ready, 1)

                def denominators(t):
                    pe.wait_ge(av_copied, t + 1)
                    nc.tensor.matmul(av_ps, pick_sum[:], av[:], start=True, stop=True).then_inc(den_ready, 1)

                def project_out(t, i, p):
                    pe.wait_ge(wo_here[p], 16 * (i + 1))
                    pe.wait_ge(avn_ready, t + 1)
                    nc.tensor.matmul(av_ps, wo[p][:], avn[:], start=True, stop=True).then_inc(o_ready, 1)

                def step(t, i, p, last=False):
                    u, n = t + 1, 1 - p
                    turn(u, n, 0)
                    scores(t, p, 1, (0, 1))
                    turn(u, n, 1)
                    scores(t, p, 1, (2, 3))
                    project_kv(u, n)
                    weigh_v(t, p, 0)
                    scores(t, p, 2, (0, 1))
                    turn(u, n, 2)
                    rough_scores(u, n, 0, (0, 1))
                    scores(t, p, 2, (2,))
                    rough_scores(u, n, 0, (2,))
                    scores(t, p, 2, (3,))
                    rough_scores(u, n, 0, (3,))
                    turn(u, n, 3)
                    weigh_v(t, p, 1)
                    rough_scores(u, n, 1, (0,))
                    scores(t, p, 3, (0,))
                    rough_scores(u, n, 1, (1, 2))
                    scores(t, p, 3, (1,))
                    rough_scores(u, n, 1, (3,))
                    rough_scores(u, n, 2, (0,))
                    scores(t, p, 3, (2,))
                    rough_scores(u, n, 2, (1, 2))
                    scores(t, p, 3, (3,))
                    rough_scores(u, n, 2, (3,))
                    rough_scores(u, n, 3, (0,))
                    weigh_v(t, p, 2)
                    rough_scores(u, n, 3, (1, 2, 3))
                    weigh_v(t, p, 3)
                    if not last:
                        project_q(t + 2, i + 1, p)
                    turn_maxima(u)
                    denominators(t)
                    scores(u, n, 0)
                    project_out(t, i, p)

                project_q(0, 0, 0)
                turn(0, 0, 0)
                turn(0, 0, 1)
                project_kv(0, 0)
                turn(0, 0, 2)
                rough_scores(0, 0, 0)
                turn(0, 0, 3)
                for r in range(1, HG):
                    rough_scores(0, 0, r)
                project_q(1, 0, 1)
                turn_maxima(0)
                scores(0, 0, 0)
                with pe.Fori(0, TURNS // 2 - 1) as i:
                    step(2 * i, i, 0)
                    step(2 * i + 1, i, 1)
                step(TURNS - 2, TURNS // 2 - 1, 0, last=True)
                t = TURNS - 1
                for r in range(1, HG):
                    scores(t, 1, r)
                    weigh_v(t, 1, r - 1)
                weigh_v(t, 1, HG - 1)
                denominators(t)
                project_out(t, TURNS // 2 - 1, 1)

            @block.scalar
            def _(act):
                act.wait_ge(tables, 16 * N_TABLES)
                nc.scalar.activation(angle_hi[:], angle_k[:], ACT.Copy).then_inc(angle_split, 1)
                nc.scalar.activation(wp_h[:], wp_raw[:], ACT.Copy).then_inc(wp_split, 1)
                act.wait_ge(wp_split, 2)
                nc.scalar.activation(wp_h[:], wp_raw[:], ACT.Copy).then_inc(wp_split, 1)
                act.sem_inc(exped, 2)

                def split_h(u, k):
                    for tt, ps in enumerate((a_ps, b_ps)):
                        act.wait_ge(qk_ready, 4 * u + 2 * k + tt + 1)
                        if k == 0:
                            nc.scalar.activation(h6[:, tt], ps, ACT.Copy).then_inc(h_done, 1)
                        else:
                            nc.scalar.activation(h6[:, tt], ps, ACT.Identity, bias=k_ones).then_inc(h_done, 1)

                def split_m(u, k):
                    for tt in range(2):
                        act.wait_ge(rest_done, 4 * u + 2 * k + tt + 1)
                        nc.scalar.activation(m6[:, tt], rest[:, tt], ACT.Copy).then_inc(m_done, 1)

                def narrow(u, p, r):
                    act.wait_ge(rot_ready, HG * u + r + 1)
                    nc.scalar.activation(rot_hi[p][:, r], rot[:, r], ACT.Copy).then_inc(rot_hi_ready, 1)

                def exps(t, r, tiles=range(NT)):
                    for j in tiles:
                        act.wait_ge(scored, 16 * t + 4 * r + j + 1)
                        act.wait_ge(lo_done, 16 * t + 4 * r + j + 1)
                        nc.scalar.activation(p32[:, j], score_ps[j % 2], ACT.Exp, scale=SCALE).then_inc(exped, 1)

                def copy_av(t):
                    act.wait_ge(av_ready, t + 1)
                    nc.scalar.activation(av[:], av_ps, ACT.Copy).then_inc(av_copied, 1)

                def invert_denominators(t):
                    act.wait_ge(den_ready, t + 1)
                    nc.scalar.activation(rden[:], av_ps, ACT.Ln).then_inc(den_log, 1)
                    act.wait_ge(den_log, t + 1)
                    nc.scalar.activation(rden[:], rden[:], ACT.Exp, scale=-1.0).then_inc(den_inv, 1)

                def step(t, p, last=False):
                    u, n = t + 1, 1 - p
                    exps(t, 1, (0, 1))
                    narrow(u, n, 0)
                    exps(t, 1, (2, 3))
                    split_h(u, 1)
                    narrow(u, n, 1)
                    split_m(u, 1)
                    exps(t, 2)
                    narrow(u, n, 2)
                    exps(t, 3, (0, 1))
                    narrow(u, n, 3)
                    exps(t, 3, (2, 3))
                    copy_av(t)
                    if not last:
                        split_h(t + 2, 0)
                    exps(u, 0, (0, 1))
                    invert_denominators(t)
                    if not last:
                        split_m(t + 2, 0)
                    exps(u, 0, (2, 3))

                split_h(0, 0)
                split_m(0, 0)
                narrow(0, 0, 0)
                narrow(0, 0, 1)
                split_h(0, 1)
                split_m(0, 1)
                narrow(0, 0, 2)
                narrow(0, 0, 3)
                split_h(1, 0)
                split_m(1, 0)
                exps(0, 0)
                with act.Fori(0, TURNS // 2 - 1) as i:
                    step(2 * i, 0)
                    step(2 * i + 1, 1)
                step(TURNS - 2, 0, last=True)
                for r in range(1, HG):
                    exps(TURNS - 1, r)
                copy_av(TURNS - 1)
                invert_denominators(TURNS - 1)

            @block.vector
            def _(dve):
                dve.wait_ge(tables, 16 * N_TABLES)
                dve.wait_ge(set_up, 2)
                dve.sem_inc(maxed, 2)
                dve.sem_inc(added, 1)
                dve.wait_ge(wp_split, 1)
                nc.vector.scalar_tensor_tensor(out=wp_raw[:], in0=wp_h[:], scalar=k_less_h, in1=wp_raw[:],
                                               op0=ALU.mult, op1=ALU.add).then_inc(wp_split, 1)
                dve.wait_ge(wp_split, 3)
                nc.vector.scalar_tensor_tensor(out=wp_parts[:], in0=wp_h[:], scalar=k_less_m, in1=wp_raw[:],
                                               op0=ALU.mult, op1=ALU.add).then_inc(wp_split, 1)

                def parts_less_h(u, k):
                    for tt, ps in enumerate((a_ps, b_ps)):
                        dve.wait_ge(h_done, 4 * u + 2 * k + tt + 1)
                        if k or not first(u):
                            dve.wait_ge(parts_done, 4 * u + 2 * k + tt - 1)
                        nc.vector.scalar_tensor_tensor(out=rest[:, tt], in0=h6[:, tt], scalar=(k_less_h if k else q_less_h), in1=ps,
                                                       op0=ALU.mult, op1=ALU.add).then_inc(rest_done, 1)

                def parts_less_m(u, p, k):
                    dst, less_m = (ks, k_less_m) if k else (qs, q_less_m)
                    for tt in range(2):
                        dve.wait_ge(m_done, 4 * u + 2 * k + tt + 1)
                        nc.vector.scalar_tensor_tensor(out=dst[p][:, tt], in0=m6[:, tt], scalar=less_m, in1=rest[:, tt],
                                                       op0=ALU.mult, op1=ALU.add).then_inc(parts_done, 1)

                def parts(u, p, k):
                    parts_less_h(u, k)
                    parts_less_m(u, p, k)

                def v_parts(u, p):
                    v_ps = misc_ps[:, 0:P].rearrange("p (j r e) -> p j r e", j=NT, r=HG)
                    dve.wait_ge(v_ready, u + 1)
                    if not first(u):
                        dve.wait_ge(v_done, 2 * u)
                    nc.vector.tensor_scalar(v_h[:], v_ps, 1.0, None, ALU.mult).then_inc(v_chain, 1)
                    dve.wait_ge(v_chain, 3 * u + 1)
                    nc.vector.tensor_scalar(vaug[p][:, :, :, 0:8], v_h[:], 1.0, None, ALU.mult)
                    nc.vector.tensor_tensor(v_rest[:], v_h[:], v_ps, ALU.subtract).then_inc(v_chain, 1)
                    dve.wait_ge(v_chain, 3 * u + 2)
                    nc.vector.tensor_scalar(v_m[:], v_rest[:], -1.0, None, ALU.mult).then_inc(v_chain, 1)
                    dve.wait_ge(v_chain, 3 * u + 3)
                    nc.vector.tensor_scalar(vaug[p][:, :, :, 9:17], v_m[:], 1.0, None, ALU.mult)
                    nc.vector.tensor_tensor(v_rest[:], v_rest[:], v_m[:], ALU.add).then_inc(v_done, 1)
                    dve.wait_ge(v_done, 2 * u + 1)
                    nc.vector.tensor_scalar(vaug[p][:, :, :, 18:26], v_rest[:], -1.0, None, ALU.mult).then_inc(v_done, 1)

                def turn(u, r):
                    dve.wait_ge(turned, HG * u + r + 1)
                    if r >= 2:
                        dve.wait_ge(rot_ready, HG * u + r - 1)
                    nc.vector.tensor_tensor(half[:, r % 2, 0], a_ps, cos_q[:], ALU.mult)
                    nc.vector.tensor_tensor(half[:, r % 2, 1], b_ps, sin_q[:], ALU.mult).then_inc(halves, 1)

                def maxima(u, r, tiles=range(NT)):
                    for k in tiles:
                        dve.wait_ge(rough, 16 * u + 4 * r + k + 1)
                        nc.vector.tensor_reduce(mx[:, k, r:r + 1], rough_ps[k % 2], AX_X, ALU.max).then_inc(maxed, 1)

                def spread_maxima(u):
                    def then(k, ins):
                        ins.then_inc(mx_chain, 1)
                        dve.wait_ge(mx_chain, MX_STEPS * u + k)

                    def wide(s):
                        return max_wide[:, :, :, :, SLOT * s + 8]

                    def heads(a):
                        return a.rearrange("p j (t r) -> p j t r", t=2)

                    dve.wait_ge(maxed, 16 * u + 18)
                    then(1, nc.vector.tensor_scalar(mx_part[:, 0], mx[:], 1.0, None, ALU.mult))
                    nc.vector.tensor_scalar(wide(0), heads(mx_part[:, 0]), 1.0, None, ALU.mult)
                    then(2, nc.vector.tensor_tensor(mx_rest[:], mx[:], mx_part[:, 0], ALU.subtract))
                    then(3, nc.vector.tensor_scalar(mx_part[:, 1], mx_rest[:], 1.0, None, ALU.mult))
                    nc.vector.tensor_scalar(wide(1), heads(mx_part[:, 1]), 1.0, None, ALU.mult)
                    then(4, nc.vector.tensor_tensor(mx_part[:, 0], mx_rest[:], mx_part[:, 1], ALU.subtract))
                    nc.vector.tensor_scalar(wide(2), heads(mx_part[:, 0]), 1.0, None, ALU.mult).then_inc(mx_wide, 1)

                def finish_q(u, p):
                    dve.wait_ge(max_turned, u + 1)
                    for tt, ps in enumerate(rough_ps):
                        nc.vector.tensor_tensor(qs[p][:, tt], qs[p][:, tt], ps, ALU.subtract).then_inc(q_final, 1)

                def high_parts(t, r, tiles=range(NT)):
                    for j in tiles:
                        dve.wait_ge(exped, 16 * t + 4 * r + j + 1 + 2)
                        nc.vector.tensor_scalar(p_hi[:, r % 2, j], p32[:, j], 1.0, None, ALU.mult).then_inc(hi_done, 1)

                def normalise(t):
                    dve.wait_ge(den_inv, t + 1)
                    nc.vector.tensor_tensor(avn[:], av[:], rden[:], ALU.mult).then_inc(avn_ready, 1)

                def add(t, b):
                    dve.wait_ge(o_ready, t + 1)
                    nc.vector.tensor_tensor(c.resid[:, b], c.resid[:, b], av_ps, ALU.add).then_inc(added, 1)

                def step(t, b, p, last=False):
                    u, n = t + 1, 1 - p
                    turn(u, 0)
                    high_parts(t, 1, (0, 1))
                    turn(u, 1)
                    v_parts(t, p)
                    high_parts(t, 1, (2, 3))
                    parts(u, n, 1)
                    high_parts(t, 2, (0, 1))
                    turn(u, 2)
                    maxima(u, 0, (0, 1))
                    high_parts(t, 2, (2,))
                    maxima(u, 0, (2,))
                    high_parts(t, 2, (3,))
                    maxima(u, 0, (3,))
                    turn(u, 3)
                    maxima(u, 1, (0,))
                    high_parts(t, 3, (0,))
                    maxima(u, 1, (1, 2))
                    high_parts(t, 3, (1,))
                    maxima(u, 1, (3,))
                    maxima(u, 2, (0,))
                    high_parts(t, 3, (2,))
                    maxima(u, 2, (1, 2))
                    high_parts(t, 3, (3,))
                    maxima(u, 2, (3,))
                    maxima(u, 3)
                    spread_maxima(u)
                    finish_q(u, n)
                    if not last:
                        parts_less_h(t + 2, 0)
                    high_parts(u, 0, (0, 1))
                    normalise(t)
                    if not last:
                        parts_less_m(t + 2, p, 0)
                    high_parts(u, 0, (2, 3))
                    add(t, b)

                parts(0, 0, 0)
                turn(0, 0)
                turn(0, 1)
                parts(0, 0, 1)
                turn(0, 2)
                maxima(0, 0)
                turn(0, 3)
                for r in range(1, HG):
                    maxima(0, r)
                spread_maxima(0)
                finish_q(0, 0)
                parts(1, 1, 0)
                high_parts(0, 0)
                with dve.Fori(0, TURNS // 2 - 1) as i:
                    step(2 * i, i // 2, 0)
                    step(2 * i + 1, i // 2, 1)
                step(TURNS - 2, NB - 1, 0, last=True)
                v_parts(TURNS - 1, 1)
                for r in range(1, HG):
                    high_parts(TURNS - 1, r)
                normalise(TURNS - 1)
                add(TURNS - 1, NB - 1)


def phase_norm(c, name):
    nc = c.nc
    with ExitStack() as ctx:
        ph = Phase(c, ctx)
        cent = [ph.sb(f"{name}_cent{p}", [P, T]) for p in range(2)]
        sq = [ph.sb(f"{name}_sq{p}", [P, T]) for p in range(2)]
        s = [NormSems(ph.sem, f"{name}{p}") for p in range(2)]

        with nc.Block() as block:
            @block.tensor
            def _(pe):
                with pe.Fori(0, NB // 2) as i:
                    for p in range(2):
                        pe.wait_ge(s[p].y, i + 1)
                        nc.tensor.matmul(c.bank[p][:], c.ones[:], c.resid[:, 2 * i + p], start=True, stop=True).then_inc(s[p].mean, 1)
                    for p in range(2):
                        pe.wait_ge(s[p].sq, i + 1)
                        nc.tensor.matmul(c.bank[2 + p][:], c.ones[:], sq[p][:], start=True, stop=True).then_inc(s[p].var, 1)

            @block.scalar
            def _(act):
                nc.scalar.preload_act_table_set(LN_EXP)
                with act.Fori(0, NB // 2) as i:
                    for p in range(2):
                        act.wait_ge(s[p].cent, i + 1)
                        nc.scalar.activation(sq[p][:], cent[p][:], ACT.Square).then_inc(s[p].sq, 1)
                    for p in range(2):
                        var = c.bank[2 + p]
                        act.wait_ge(s[p].var, i + 1)
                        nc.scalar.activation(var[:], var[:], ACT.Ln, bias=c.eps[:]).then_inc(s[p].log, 1)
                        act.wait_ge(s[p].log, i + 1)
                        nc.scalar.activation(var[:], var[:], ACT.Exp, scale=-0.5).then_inc(s[p].rstd, 1)

            @block.vector
            def _(dve):
                for p in range(2):
                    dve.sem_inc(s[p].y, 1)
                with dve.Fori(0, NB // 2) as i:
                    for p in range(2):
                        dve.wait_ge(s[p].mean, i + 1)
                        nc.vector.tensor_tensor(cent[p][:], c.resid[:, 2 * i + p], c.bank[p][:], ALU.subtract).then_inc(s[p].cent, 1)
                    for p in range(2):
                        dve.wait_ge(s[p].rstd, i + 1)
                        nc.vector.tensor_tensor(c.resid[:, 2 * i + p], cent[p][:], c.bank[2 + p][:], ALU.mult).then_inc(s[p].y, 1)


NE = 32
TOP = 4


def gates_of_batches(c, d, ph, gate_parts):
    nc = c.nc
    sel_w = ph.sb("sel_w", [P, NE])
    vec = ph.sb("ln2_vec", [P, 2])
    def pair(name, shape, dt=F32):
        return [ph.sb(f"gate_{name}{p}", shape, dt) for p in range(2)]

    y, cent, sq, x2 = (pair(n, [P, T]) for n in ("y", "cent", "sq", "x2"))
    e, e1, prob = (pair(n, [P, NT, NE]) for n in ("exp", "exp1", "prob"))
    top8 = pair("top8", [P, NT, 8])
    above = pair("above", [P, NT, NE])
    equal = pair("equal", [P, NT, NE])
    n_above = pair("n_above", [P, NT])
    nth = pair("nth", [P, NT, NE])
    fits = pair("fits", [P, NT, NE])
    tie, chosen, gate = (pair(n, [P, NT, NE]) for n in ("tie", "chosen", "value"))
    one = ph.sb("gate_one", [P, NE])
    pad = pair("pad", [P, 1])
    rest = pair("rest", [NE, T])
    mid, high = pair("mid", [NE, T], BF16), pair("high", [NE, T], BF16)
    loaded, set_up = ph.sem("p3_loaded"), ph.sem("p3_set_up")
    ln = [NormSems(ph.sem, f"p3n{p}") for p in range(2)]
    x2_ready, logits, exped, gate_ready, gate_turned = (
        [ph.sem(f"p3_{n}{p}") for p in range(2)] for n in ("x2", "logits", "exped", "gate", "gate_turned"))
    chain = [ph.sem(f"p3_dve_chain{p}") for p in range(2)]
    DVE_STEPS = 12
    mean_ps, var_ps, logit_ps, gate_ps = (c.bank[2 * i:2 * i + 2] for i in range(4))
    logit_v = [ps[:, 0:NT * NE].rearrange("p (j e) -> p j e", j=NT) for ps in logit_ps]

    with nc.Block() as block:
        @block.sync
        def _(sp):
            sp.dma_start(sel_w[:], d["sel_w"]).then_inc(loaded, 16)
            sp.dma_start(vec[:, 0:1], d["ln2_g"]).then_inc(loaded, 16)
            sp.dma_start(vec[:, 1:2], d["ln2_b"]).then_inc(loaded, 16)

        @block.gpsimd
        def _(pool):
            nc.gpsimd.memset(one[:], 1.0).then_inc(set_up, 1)

        @block.tensor
        def _(pe):
            pe.wait_ge(loaded, 48)
            with pe.Fori(0, NB // 2) as i:
                norms_pe(nc, pe, ln, i + 1, c.ones[:], y, sq, mean_ps, var_ps)
                for p in range(2):
                    pe.wait_ge(x2_ready[p], i + 1)
                    for j in range(NT):
                        last = nc.tensor.matmul(logit_v[p][:, j], x2[p][:, P * j:P * j + P], sel_w[:], start=True, stop=True)
                    last.then_inc(logits[p], 1)
                for p in range(2):
                    pe.wait_ge(gate_ready[p], i + 1)
                    for j in range(NT):
                        last = nc.tensor.transpose(gate_ps[p][0:NE, P * j:P * j + P], gate[p][:, j], c.ident[:])
                    last.then_inc(gate_turned[p], 1)

        @block.scalar
        def _(act):
            nc.scalar.preload_act_table_set(LN_EXP)
            with act.Fori(0, NB // 2) as i:
                norms_act(nc, act, ln, i + 1, cent, sq, var_ps, c.eps[:])
                for p in range(2):
                    act.wait_ge(logits[p], i + 1)
                    nc.scalar.activation(e[p][:], logit_v[p], ACT.Exp, scale=-1.0).then_inc(exped[p], 1)

        @block.vector
        def _(dve):
            dve.wait_ge(loaded, 48)
            dve.wait_ge(set_up, 1)
            with dve.Fori(0, NB // 2) as i:
                def after(p, k):
                    dve.wait_ge(chain[p], DVE_STEPS * i + k)

                for p in range(2):
                    nc.vector.tensor_scalar(y[p][:], c.resid[:, 2 * i + p], 1.0, None, ALU.mult).then_inc(ln[p].y, 1)
                for p in range(2):
                    b = 2 * i + p
                    dve.wait_ge(ln[p].y, i + 1)
                    nc.vector.tensor_tensor(c.resid[:, b], y[p][:], c.outer[:, b], ALU.add)
                norms_dve(nc, dve, ln, i + 1, y, cent, mean_ps, var_ps, y)
                for p in range(2):
                    dve.wait_ge(ln[p].out, i + 1)
                    nc.vector.tensor_scalar(x2[p][:], y[p][:], vec[:, 0:1], vec[:, 1:2], ALU.mult, ALU.add).then_inc(x2_ready[p], 1)
                for p in range(2):
                    dve.wait_ge(x2_ready[p], i + 1)
                    nc.vector.tensor_scalar(c.normed[:, 2 * i + p], x2[p][:], 1.0, None, ALU.mult)
                for p in range(2):
                    dve.wait_ge(exped[p], i + 1)
                    nc.vector.tensor_scalar(e1[p][:], e[p][:], 1.0, None, ALU.add).then_inc(chain[p], 1)
                for p in range(2):
                    after(p, 1)
                    nc.vector.reciprocal(prob[p][:], e1[p][:]).then_inc(chain[p], 1)
                for p in range(2):
                    after(p, 2)
                    nc.vector.memset(pad[p][:], 0.0)
                    for j in range(NT):
                        last = nc.vector.max(top8[p][:, j], prob[p][:, j])
                    last.then_inc(chain[p], 1)
                for p in range(2):
                    after(p, 3)
                    for j in range(NT):
                        fourth = top8[p][:, j, TOP - 1:TOP]
                        nc.vector.tensor_scalar(above[p][:, j], prob[p][:, j], fourth, None, ALU.is_gt)
                        last = nc.vector.tensor_scalar(equal[p][:, j], prob[p][:, j], fourth, None, ALU.is_equal)
                    last.then_inc(chain[p], 1)
                for p in range(2):
                    after(p, 4)
                    nc.vector.tensor_reduce(n_above[p][:], above[p][:], AX_X, ALU.add)
                    for j in range(NT):
                        last = nc.vector.tensor_tensor_scan(nth[p][:, j], one[:], equal[p][:, j], 0.0, ALU.mult, ALU.add)
                    last.then_inc(chain[p], 1)
                for p in range(2):
                    after(p, 5)
                    for j in range(NT):
                        last = nc.vector.tensor_scalar(fits[p][:, j], nth[p][:, j], n_above[p][:, j:j + 1], float(TOP), ALU.add, ALU.is_le)
                    last.then_inc(chain[p], 1)
                for p in range(2):
                    after(p, 6)
                    nc.vector.tensor_tensor(tie[p][:], equal[p][:], fits[p][:], ALU.mult).then_inc(chain[p], 1)
                for p in range(2):
                    after(p, 7)
                    nc.vector.tensor_tensor(chosen[p][:], tie[p][:], above[p][:], ALU.add).then_inc(chain[p], 1)
                for p in range(2):
                    after(p, 8)
                    nc.vector.tensor_tensor(gate[p][:], chosen[p][:], prob[p][:], ALU.mult).then_inc(gate_ready[p], 1)
                for p in range(2):
                    dve.wait_ge(gate_turned[p], i + 1)
                    nc.vector.tensor_copy(high[p][:], gate_ps[p][0:NE, :]).then_inc(chain[p], 1)
                for p in range(2):
                    after(p, 9)
                    nc.vector.tensor_tensor(rest[p][:], gate_ps[p][0:NE, :], high[p][:], ALU.subtract).then_inc(chain[p], 1)
                    nc.vector.tensor_scalar(gate_parts[0:NE, 2 * i + p], high[p][:], 1.0, None, ALU.mult)
                for p in range(2):
                    after(p, 10)
                    nc.vector.tensor_copy(mid[p][:], rest[p][:]).then_inc(chain[p], 1)
                for p in range(2):
                    after(p, 11)
                    nc.vector.tensor_scalar(gate_parts[NE:2 * NE, 2 * i + p], mid[p][:], 1.0, None, ALU.mult)
                    nc.vector.tensor_tensor(gate_parts[2 * NE:3 * NE, 2 * i + p], rest[p][:], mid[p][:],
                                            ALU.subtract).then_inc(chain[p], 1)
                for p in range(2):
                    after(p, 12)


def experts(c, d, ph, gate_parts):
    nc = c.nc
    keys = [ph.sb(f"keys{p}", [P, P]) for p in range(2)]
    values = [ph.sb(f"values{p}", [P, P]) for p in range(2)]
    pick = [ph.sb(f"pick_expert{p}", [3 * NE, P], BF16) for p in range(2)]
    h = [ph.sb(f"hidden{p}", [P, T]) for p in range(2)]
    hg = [ph.sb(f"hidden_gated{p}", [P, T]) for p in range(2)]
    here = [ph.sem(f"p3_expert_here{p}") for p in range(2)]
    h_ready, g_ready = ph.sem("p3_h"), ph.sem("p3_g")
    rectified, gated = ph.sem("p3_rectified"), ph.sem("p3_gated")
    valued = ph.sem("p3_valued")
    added = ph.sem("p3_added")
    h_ps, g_ps, v_ps = c.bank[0:2], c.bank[2:4], c.bank[4:6]

    with nc.Block() as block:
        @block.sync
        def _(sp):
            def load(x, p):
                sp.dma_start(keys[p][:], d["keys"][x]).then_inc(here[p], 16)
                sp.dma_start(values[p][:], d["values"][x]).then_inc(here[p], 16)
                sp.dma_start(pick[p][:], d["pick_expert"][x]).then_inc(here[p], 16)

            load(0, 0)
            load(1, 1)
            with sp.Fori(0, NE // 2 - 1) as i:
                for p in range(2):
                    sp.wait_ge(valued, NB * (2 * i + p + 1))
                    load(2 * i + p + 2, p)

        @block.tensor
        def _(pe):
            with pe.Fori(0, NE // 2) as i:
                def apply_values(k):
                    pe.wait_ge(gated, 2 * NB * i + k + 1)
                    pe.wait_ge(added, 2 * NB * i + k + 1)
                    nc.tensor.matmul(v_ps[k % 2][:], values[k // NB][:], hg[k % 2][:], start=True, stop=True).then_inc(valued, 1)

                for k in range(2 * NB):
                    p, b = divmod(k, NB)
                    if b == 0:
                        pe.wait_ge(here[p], 48 * (i + 1))
                    nc.tensor.matmul(h_ps[k % 2][:], keys[p][:], c.normed[:, b], start=True, stop=True).then_inc(h_ready, 1)
                    nc.tensor.matmul(g_ps[k % 2][:], pick[p][:], gate_parts[:, b], start=True, stop=True).then_inc(g_ready, 1)
                    if k:
                        apply_values(k - 1)
                apply_values(2 * NB - 1)

        @block.scalar
        def _(act):
            with act.Fori(0, NE // 2) as i:
                for k in range(2 * NB):
                    act.wait_ge(h_ready, 2 * NB * i + k + 1)
                    nc.scalar.activation(h[k % 2][:], h_ps[k % 2][:], ACT.Relu).then_inc(rectified, 1)

        @block.vector
        def _(dve):
            dve.sem_inc(added, 2)
            with dve.Fori(0, NE // 2) as i:
                def add(k):
                    dve.wait_ge(valued, 2 * NB * i + k + 1)
                    resid = c.resid[:, k % NB]
                    nc.vector.tensor_tensor(resid, resid, v_ps[k % 2][:], ALU.add).then_inc(added, 1)

                for k in range(2 * NB):
                    dve.wait_ge(rectified, 2 * NB * i + k + 1)
                    dve.wait_ge(g_ready, 2 * NB * i + k + 1)
                    nc.vector.tensor_tensor(hg[k % 2][:], h[k % 2][:], g_ps[k % 2][:], ALU.mult).then_inc(gated, 1)
                    if k:
                        add(k - 1)
                add(2 * NB - 1)


def phase_experts(c, d):
    with ExitStack() as ctx:
        ph = Phase(c, ctx)
        gate_parts = ph.sb("gate_parts", [3 * NE, NB, T], BF16)
        gates_of_batches(c, d, ph, gate_parts)
        experts(c, d, ph, gate_parts)
    phase_norm(c, "ffn0_norm")


NH = 4
DS = 64
NR = NB * NH
DI = NH * DS
TWO_PI_HI = 6.28125
TWO_PI_LO = 2.0 * np.pi - TWO_PI_HI
ROUND = 1.5 * 2.0 ** 23
PI_IN = 3.1415925
NEG = -1e30


def state_space_rows(c, d, ph, dt, ncs, cols):
    nc = c.nc
    w_rows = ph.sb("w_rows", [P, 3, NB, NR])
    bias = ph.sb("dt_bias", [NR, 1])
    absd, absa = ph.sb("ss_absd", [NR, T]), ph.sb("ss_absa", [NR, T])
    one = ph.sb("ss_one", [NR, T])
    m, sp, trap, w1, w2, decay, nadt, cc, n1 = (ph.sb(f"ss_{n}", [NR, T]) for n in (
        "max0", "softplus_a", "trap", "w1", "w2", "decay", "neg_adt", "c", "n1"))
    loaded, set_up = ph.sem("p4_loaded"), ph.sem("p4_set_up")
    rows_ready = ph.sem("p4_rows")
    act_chain, dve_chain = ph.sem("p4_act_chain"), ph.sem("p4_dve_chain")
    dt_log, a_log, trap_exp, decay_ready = ph.sem("p4_dt_log"), ph.sem("p4_a_log"), ph.sem("p4_trap_exp"), ph.sem("p4_decay")
    nadt_ready, cols_in, cols_turned = ph.sem("p4_nadt"), ph.sem("p4_cols_in"), ph.sem("p4_cols_turned")
    dt_ps, a_ps, trap_ps = (c.bank[i][0:NR, :] for i in range(3))

    with nc.Block() as block:
        @block.sync
        def _(sp_):
            sp_.dma_start(w_rows[:], d["ss_w_rows"]).then_inc(loaded, 16)
            sp_.dma_start(bias[:], d["ss_dt_bias"]).then_inc(loaded, 16)

        @block.gpsimd
        def _(pool):
            nc.gpsimd.memset(one[:], 1.0).then_inc(set_up, 1)

        @block.tensor
        def _(pe):
            pe.wait_ge(loaded, 32)
            for q, ps in enumerate((dt_ps, a_ps, trap_ps)):
                for b in range(NB):
                    last = nc.tensor.matmul(ps, w_rows[:, q, b], c.resid[:, b], start=(b == 0), stop=(b == NB - 1))
                last.then_inc(rows_ready, 1)
            pe.wait_ge(cols_in, 1)
            for q, rows in enumerate((cc, n1, w1)):
                for j in range(NT):
                    last = nc.tensor.transpose(c.bank[3 + q][:, NR * j:NR * j + NR], rows[:, P * j:P * j + P], c.ident[0:NR, 0:NR])
            last.then_inc(cols_turned, 1)

        @block.scalar
        def _(act):
            nc.scalar.preload_act_table_set(LN_EXP)
            steps = [0]

            def then(ins):
                steps[0] += 1
                ins.then_inc(act_chain, 1)
                act.wait_ge(act_chain, steps[0])

            act.wait_ge(loaded, 32)
            act.wait_ge(rows_ready, 2)
            then(nc.scalar.activation(absd[:], dt_ps, ACT.Abs, bias=bias[:]))
            then(nc.scalar.activation(absd[:], absd[:], ACT.Exp, scale=-1.0))
            nc.scalar.activation(absd[:], absd[:], ACT.Ln, bias=1.0).then_inc(dt_log, 1)
            then(nc.scalar.activation(absa[:], a_ps, ACT.Abs))
            then(nc.scalar.activation(absa[:], absa[:], ACT.Exp, scale=-1.0))
            nc.scalar.activation(absa[:], absa[:], ACT.Ln, bias=1.0).then_inc(a_log, 1)
            act.wait_ge(rows_ready, 3)
            nc.scalar.activation(trap[:], trap_ps, ACT.Exp, scale=-1.0).then_inc(trap_exp, 1)
            act.wait_ge(nadt_ready, 1)
            nc.scalar.activation(decay[:], nadt[:], ACT.Exp, scale=-1.0).then_inc(decay_ready, 1)

        @block.vector
        def _(dve):
            steps = [0]

            def then(ins):
                steps[0] += 1
                ins.then_inc(dve_chain, 1)
                dve.wait_ge(dve_chain, steps[0])

            dve.wait_ge(loaded, 32)
            dve.wait_ge(set_up, 1)
            dve.wait_ge(dt_log, 1)
            then(nc.vector.tensor_scalar(m[:], dt_ps, bias[:], 0.0, ALU.add, ALU.max))
            then(nc.vector.tensor_tensor(dt[:], m[:], absd[:], ALU.add))
            dve.wait_ge(a_log, 1)
            then(nc.vector.tensor_scalar(m[:], a_ps, 0.0, None, ALU.max))
            then(nc.vector.tensor_tensor(sp[:], m[:], absa[:], ALU.add))
            nc.vector.scalar_tensor_tensor(out=nadt[:], in0=sp[:], scalar=1e-4, in1=dt[:], op0=ALU.max, op1=ALU.mult).then_inc(nadt_ready, 1)
            dve.wait_ge(nadt_ready, 1)
            then(nc.vector.tensor_tensor_scan(ncs[:], one[:], nadt[:], 0.0, ALU.mult, ALU.add))
            dve.wait_ge(trap_exp, 1)
            then(nc.vector.tensor_scalar(m[:], trap[:], 1.0, None, ALU.add))
            then(nc.vector.reciprocal(sp[:], m[:]))
            then(nc.vector.tensor_tensor(w1[:], sp[:], dt[:], ALU.mult))
            then(nc.vector.tensor_tensor(w2[:], dt[:], w1[:], ALU.subtract))
            nc.vector.memset(cc[:, T - 1:T], 0.0)
            nc.vector.memset(n1[:, T - 1:T], 0.0)
            nc.vector.tensor_copy(n1[:, 0:T - 1], ncs[:, 1:T])
            dve.wait_ge(decay_ready, 1)
            then(nc.vector.tensor_tensor(m[:, 0:T - 1], decay[:, 1:T], w1[:, 0:T - 1], ALU.mult))
            nc.vector.tensor_tensor(cc[:, 0:T - 1], m[:, 0:T - 1], w2[:, 1:T], ALU.add).then_inc(cols_in, 1)
            dve.wait_ge(cols_turned, 1)
            for q in range(3):
                nc.vector.tensor_copy(cols[:, q], c.bank[3 + q][:, 0:NT * NR].rearrange("p (j r) -> p j r", j=NT))


def state_space_angles(c, d, ph, dt, cos, sin):
    nc = c.nc
    w_ang = ph.sb("w_angle", [P, P])
    sign = ph.sb("sin_sign", [P, 1])
    pick = [ph.sb(f"pick_mean{p}", [NR, P]) for p in range(2)]
    one = ph.sb("ang_one", [P, T])
    mean_dt, step_, phase, km, k, r1, r2, r, over, rc = ([ph.sb(f"ang_{n}{p}", [P, T]) for p in range(2)] for n in (
        "mean_dt", "step", "phase", "km", "k", "r1", "r2", "r", "over", "rc"))
    loaded, set_up = ph.sem("p4a_loaded"), ph.sem("p4a_set_up")
    here, projected, copied, chain, reduced, turned = ([ph.sem(f"p4a_{n}{p}") for p in range(2)] for n in (
        "here", "projected", "copied", "chain", "reduced", "sines"))
    STEPS = 9
    ang_ps, mean_ps = c.bank[0:2], c.bank[2:4]

    with nc.Block() as block:
        @block.sync
        def _(sp):
            sp.dma_start(w_ang[:], d["ss_w_angle"]).then_inc(loaded, 16)
            sp.dma_start(sign[:], d["ss_sign"]).then_inc(loaded, 16)
            for p in range(2):
                sp.dma_start(pick[p][:], d["ss_pick"][p, :, NH * P:]).then_inc(here[p], 16)
            with sp.Fori(0, NB // 2 - 1) as i:
                for p in range(2):
                    sp.wait_ge(projected[p], i + 1)
                    sp.dma_start(pick[p][:], d["ss_pick"][2 * i + p + 2, :, NH * P:]).then_inc(here[p], 16)

        @block.gpsimd
        def _(pool):
            nc.gpsimd.memset(one[:], 1.0).then_inc(set_up, 1)

        @block.tensor
        def _(pe):
            pe.wait_ge(loaded, 32)
            with pe.Fori(0, NB // 2) as i:
                for p in range(2):
                    pe.wait_ge(here[p], 16 * (i + 1))
                    pe.wait_ge(chain[p], STEPS * i + 1)
                    nc.tensor.matmul(ang_ps[p], w_ang[:], c.resid[:, 2 * i + p], start=True, stop=True)
                    nc.tensor.matmul(mean_ps[p], pick[p][:], dt[:], start=True, stop=True).then_inc(projected[p], 1)

        @block.scalar
        def _(act):
            act.wait_ge(loaded, 32)
            with act.Fori(0, NB // 2) as i:
                for p in range(2):
                    act.wait_ge(projected[p], i + 1)
                    nc.scalar.activation(mean_dt[p][:], mean_ps[p], ACT.Copy).then_inc(copied[p], 1)
                for p in range(2):
                    act.wait_ge(reduced[p], i + 1)
                    nc.scalar.activation(sin[:, 2 * i + p], r[p][:], ACT.Sin, scale=sign[:])
                    nc.scalar.activation(cos[:, 2 * i + p], rc[p][:], ACT.Sin).then_inc(turned[p], 1)

        @block.vector
        def _(dve):
            dve.wait_ge(set_up, 1)
            for p in range(2):
                dve.sem_inc(chain[p], 1)
                dve.sem_inc(turned[p], 1)
            with dve.Fori(0, NB // 2) as i:
                def after(p, n):
                    dve.wait_ge(chain[p], STEPS * i + n + 1)

                for p in range(2):
                    dve.wait_ge(copied[p], i + 1)
                    nc.vector.tensor_tensor(step_[p][:], ang_ps[p], mean_dt[p][:], ALU.mult).then_inc(chain[p], 1)
                for p in range(2):
                    after(p, 1)
                    nc.vector.tensor_tensor_scan(phase[p][:], one[:], step_[p][:], 0.0, ALU.mult, ALU.add).then_inc(chain[p], 1)
                for p in range(2):
                    after(p, 2)
                    nc.vector.tensor_scalar(km[p][:], phase[p][:], 0.5 / np.pi, ROUND, ALU.mult, ALU.add).then_inc(chain[p], 1)
                for p in range(2):
                    after(p, 3)
                    nc.vector.tensor_scalar(k[p][:], km[p][:], -ROUND, None, ALU.add).then_inc(chain[p], 1)
                for p in range(2):
                    after(p, 4)
                    nc.vector.scalar_tensor_tensor(out=r1[p][:], in0=k[p][:], scalar=-TWO_PI_HI, in1=phase[p][:],
                                                   op0=ALU.mult, op1=ALU.add).then_inc(chain[p], 1)
                for p in range(2):
                    after(p, 5)
                    nc.vector.scalar_tensor_tensor(out=r2[p][:], in0=k[p][:], scalar=-TWO_PI_LO, in1=r1[p][:],
                                                   op0=ALU.mult, op1=ALU.add).then_inc(chain[p], 1)
                for p in range(2):
                    after(p, 6)
                    dve.wait_ge(turned[p], i + 1)
                    nc.vector.tensor_scalar(r[p][:], r2[p][:], PI_IN, -PI_IN, ALU.min, ALU.max).then_inc(chain[p], 1)
                for p in range(2):
                    after(p, 7)
                    nc.vector.tensor_scalar(over[p][:], r[p][:], np.pi / 2, -2.0 * np.pi, ALU.is_gt, ALU.mult).then_inc(chain[p], 1)
                for p in range(2):
                    after(p, 8)
                    nc.vector.scalar_tensor_tensor(out=r1[p][:], in0=r[p][:], scalar=np.pi / 2, in1=over[p][:],
                                                   op0=ALU.add, op1=ALU.add).then_inc(chain[p], 1)
                for p in range(2):
                    after(p, 9)
                    nc.vector.tensor_scalar(rc[p][:], r1[p][:], PI_IN, -PI_IN, ALU.min, ALU.max).then_inc(reduced[p], 1)


def state_space_outputs(c, d, ph, ncs, cols, cos, sin):
    nc = c.nc
    w_bc = ph.sb("w_bc", [P, P])
    w_zx = ph.sb("w_zx", [P, 2 * DI])
    w_out = ph.sb("ss_w_out", [P, 2, P])
    vec = ph.sb("bc_vec", [P, 2])
    ones64 = ph.sb("ones64", [P, P])
    swap = ph.sb("swap_pairs", [P, P])
    later = ph.sb("later", [P, NT, P])
    d_rep = ph.sb("d_rep", [P, NT, NH])
    pick = ph.sb("pick_rows", [NR, NH * P])
    xs = ph.sb("ss_x", [P, T])
    bc, cent, sq, v0, v, t1, t2 = (ph.sb(f"bc_{n}", [P, T]) for n in ("raw", "cent", "sq", "v0", "v", "t1", "t2"))
    brot, crot = ph.sb("b_rot", [DS, T]), ph.sb("c_rot", [DS, T])
    ez, z = ph.sb("ez", [P, NT, DI]), ph.sb("ss_z", [P, NT, DI])
    zs, xt, xc = ([ph.sb(f"ss_{n}{p}", [P, NT, DI]) for p in range(2)] for n in ("zs", "xt", "xc"))
    cq = [ph.sb(f"cq{p}", [P, 3, NT, NH]) for p in range(2)]
    dcoef = [ph.sb(f"dcoef{p}", [P, NT, NH]) for p in range(2)]
    OFF = [0, 512, 896, 1152]
    WID = [512 - P * j for j in range(NT)]
    ALL = OFF[-1] + WID[-1]
    cbs = [ph.sb(f"cb_products{p}", [P, ALL]) for p in range(2)]
    cbw = ph.sb("cbw", [P, NT, P])
    cb = ph.sb("cb", [P, NT])
    y1 = ph.sb("y1", [P, NT, DI])
    ygt = ph.sb("ygt", [P, 2, T])
    diag = [ph.sb(f"diag{p}", [P, T]) for p in range(2)]
    e = [ph.sb(f"e_{p}", [P, ALL]) for p in range(2)]
    mm = [ph.sb(f"m_{p}", [P, ALL]) for p in range(2)]

    loaded = ph.sem("p4b_loaded")
    xs_here, pick_here = ph.sem("p4b_xs_here"), ph.sem("p4b_pick_here")
    done = ph.sem("p4b_done")
    zx_ready = ph.sem("p4b_zx")
    bc_ready = ph.sem("p4b_bc")
    ln = NormSems(ph.sem, "p4b_n")
    cq_ready, v_ready, swapped, turned, rotated = (ph.sem(f"p4b_{n}") for n in ("cq", "v", "swapped", "turned", "rotated"))
    zx_copied = ph.sem("p4b_zx_copied")
    z_clamped, z_log, z_sig, zs_ready = (ph.sem(f"p4b_{n}") for n in ("z_clamped", "z_log", "z_sig", "zs"))
    cb_ready, cb_copied, xc_ready = ph.sem("p4b_cb"), ph.sem("p4b_cb_copied"), ph.sem("p4b_xc")
    cbw_ready, cb_diag, dc_part, dc_ready = (ph.sem(f"p4b_{n}") for n in ("cbw", "cb_diag", "dc_part", "dc"))
    n_ready = ph.sem("p4b_n_row")
    diag_ready = ph.sem("p4b_diag")
    e_ready, m_ready, weighed = ph.sem("p4b_e"), ph.sem("p4b_m"), ph.sem("p4b_weighed")
    y_part, y_sum, yg_ready, ygt_ready, ygt_copied, o_ready = (ph.sem(f"p4b_{n}") for n in (
        "y_part", "y_sum", "yg", "ygt", "ygt_copied", "o"))
    N_LOADS = 12
    bank = c.bank
    n_ps = bank[0:2]
    y_ps = bank[2:4]
    bc_ps, var_ps = bank[4], bank[4]
    zx_ps = bank[5:7]
    mean_ps, swap_ps = bank[7], bank[7]
    cb_ps = bank[4:8]

    def over_batches(engine, front, cycle):
        front(0, 0)
        with engine.Fori(0, NB // 2 - 1) as i:
            cycle(2 * i, 0, True)
            cycle(2 * i + 1, 1, True)
        cycle(NB - 2, 0, True)
        cycle(NB - 1, 1, False)

    def by_head(a):
        return a.rearrange("p j (h e) -> p (j h) e", e=DS)

    with nc.Block() as block:
        @block.sync
        def _(sp):
            sp.dma_start(w_bc[:], d["ss_w_bc"]).then_inc(loaded, 16)
            sp.dma_start(w_zx[:], d["ss_w_zx"]).then_inc(loaded, 16)
            sp.dma_start(w_out[:], d["ss_w_out"]).then_inc(loaded, 16)
            sp.dma_start(vec[:, 0:1], d["ss_gain"]).then_inc(loaded, 16)
            sp.dma_start(vec[:, 1:2], d["ss_shift"]).then_inc(loaded, 16)
            sp.dma_start(ones64[:], d["ones64"]).then_inc(loaded, 16)
            sp.dma_start(swap[:], d["ss_swap"]).then_inc(loaded, 16)
            for j in range(NT):
                sp.dma_start(later[:, j], d["ss_later"]).then_inc(loaded, 16)
            sp.dma_start(d_rep[:], d["ss_d"]).then_inc(loaded, 16)
            sp.dma_start(xs[:], c.resid[:, 0]).then_inc(xs_here, 16)
            sp.dma_start(pick[:], d["ss_pick"][0, :, 0:NH * P]).then_inc(pick_here, 16)
            with sp.Fori(0, NB - 1) as b:
                sp.wait_ge(zx_ready, NT * b + NT)
                sp.dma_start(xs[:], c.resid[:, b + 1]).then_inc(xs_here, 16)
                sp.wait_ge(n_ready, NH * b + NH)
                sp.dma_start(pick[:], d["ss_pick"][b + 1, :, 0:NH * P]).then_inc(pick_here, 16)

        @block.gpsimd
        def _(pool):
            pool.sem_inc(m_ready, 2)

            def masked(b, p, h):
                pool.wait_ge(e_ready, NH * b + h + 1 + 2)
                pool.wait_ge(weighed, NH * b + h + 1)
                if h == 0:
                    pool.wait_ge(cb_copied, b + 1)
                nc.gpsimd.tensor_tensor(mm[h % 2][:], e[h % 2][:], cbs[p][:], ALU.mult).then_inc(m_ready, 1)

            def gate(u, p):
                pool.wait_ge(z_sig, u + 1)
                nc.gpsimd.tensor_tensor(zs[p][:], ez[:], z[:], ALU.mult).then_inc(zs_ready, 1)

            def front(u, p):
                gate(u, p)
                masked(u, p, 0)

            def cycle(b, p, more):
                for h in range(1, NH):
                    masked(b, p, h)
                if more:
                    front(b + 1, 1 - p)

            over_batches(pool, front, cycle)

        @block.tensor
        def _(pe):
            pe.wait_ge(loaded, 16 * N_LOADS)
            pe.sem_inc(weighed, 2)

            def project_bc(u):
                pe.wait_ge(xs_here, 16 * (u + 1))
                if not first(u):
                    pe.wait_ge(cb_copied, u)
                nc.tensor.matmul(bc_ps, w_bc[:], xs[:], start=True, stop=True).then_inc(bc_ready, 1)

            def project_zx(u, j):
                if j >= 2:
                    pe.wait_ge(zx_copied, NT * u + j - 1)
                nc.tensor.matmul(zx_ps[j % 2], xs[:, P * j:P * j + P], w_zx[:], start=True, stop=True).then_inc(zx_ready, 1)

            def mean(u):
                pe.wait_ge(ln.y, u + 1)
                nc.tensor.matmul(mean_ps, ones64[:], bc[:], start=True, stop=True).then_inc(ln.mean, 1)

            def variance(u):
                pe.wait_ge(ln.sq, u + 1)
                nc.tensor.matmul(var_ps, ones64[:], sq[:], start=True, stop=True).then_inc(ln.var, 1)

            def swap_pairs(u):
                pe.wait_ge(v_ready, u + 1)
                nc.tensor.matmul(swap_ps, swap[:], v[:], start=True, stop=True).then_inc(swapped, 1)

            def row_of(b, h):
                if h == 0:
                    pe.wait_ge(pick_here, 16 * (b + 1))
                pe.wait_ge(e_ready, NH * b + h + 1)
                nc.tensor.matmul(n_ps[h % 2], pick[:, P * h:P * h + P], ncs[:], start=True, stop=True).then_inc(n_ready, 1)

            def c_times_b(u):
                pe.wait_ge(rotated, u + 1)
                pe.wait_ge(zx_copied, NT * u + NT)
                for j in range(NT):
                    nc.tensor.matmul(cb_ps[j][:, 0:WID[j]], brot[:, P * j:P * j + P], crot[:, P * j:],
                                     start=True, stop=True).then_inc(cb_ready, 1)

            def head(b, p, h):
                if h == 0:
                    pe.wait_ge(xc_ready, b + 1)
                    pe.wait_ge(done, b + 1)
                pe.wait_ge(m_ready, NH * b + h + 1 + 2)
                for tt in range(NT):
                    for j in range(tt + 1):
                        at = OFF[j] + P * (tt - j)
                        last = nc.tensor.matmul(y_ps[tt // 2][:, DI * (tt % 2) + DS * h:DI * (tt % 2) + DS * h + DS],
                                                mm[h % 2][:, at:at + P], xc[p][:, j, DS * h:DS * h + DS],
                                                start=(j == 0), stop=(j == tt))
                last.then_inc(weighed, 1)

            def turn_y(b):
                pe.wait_ge(yg_ready, b + 1)
                for f in range(2):
                    for tt in range(NT):
                        last = nc.tensor.transpose(y_ps[f][:, P * tt:P * tt + P], y1[:, tt, P * f:P * f + P], c.ident[:])
                last.then_inc(ygt_ready, 1)

            def project_out(b):
                pe.wait_ge(ygt_copied, b + 1)
                for f in range(2):
                    last = nc.tensor.matmul(y_ps[0], w_out[:, f], ygt[:, f], start=(f == 0), stop=(f == 1))
                last.then_inc(o_ready, 1)

            def front(u, p):
                project_bc(u)
                for j in range(NT):
                    project_zx(u, j)
                mean(u)
                variance(u)
                swap_pairs(u)
                row_of(u, 0)
                row_of(u, 1)
                c_times_b(u)

            def cycle(b, p, more):
                u = b + 1
                if more:
                    project_bc(u)
                head(b, p, 0)
                if more:
                    project_zx(u, 0)
                    project_zx(u, 1)
                    mean(u)
                row_of(b, 2)
                head(b, p, 1)
                if more:
                    project_zx(u, 2)
                    project_zx(u, 3)
                    variance(u)
                row_of(b, 3)
                head(b, p, 2)
                if more:
                    swap_pairs(u)
                head(b, p, 3)
                if more:
                    row_of(u, 0)
                    row_of(u, 1)
                    c_times_b(u)
                turn_y(b)
                project_out(b)

            over_batches(pe, front, cycle)

        @block.scalar
        def _(act):
            nc.scalar.preload_act_table_set(LN_EXP)
            act.wait_ge(loaded, 16 * N_LOADS)

            def copy_bc(u):
                act.wait_ge(bc_ready, u + 1)
                nc.scalar.activation(bc[:], bc_ps, ACT.Copy).then_inc(ln.y, 1)

            def copy_zx(u, p, j):
                act.wait_ge(zx_ready, NT * u + j + 1)
                if j == 0 and not first(u):
                    act.wait_ge(zs_ready, u)
                ps = zx_ps[j % 2]
                nc.scalar.activation(ez[:, j], ps[:, 0:DI], ACT.Exp, scale=-1.0)
                nc.scalar.activation(z[:, j], ps[:, 0:DI], ACT.Copy)
                nc.scalar.activation(xt[p][:, j], ps[:, DI:], ACT.Copy).then_inc(zx_copied, 1)

            def square(u):
                act.wait_ge(ln.cent, u + 1)
                nc.scalar.activation(sq[:], cent[:], ACT.Square).then_inc(ln.sq, 1)

            def inverse_deviation(u):
                act.wait_ge(ln.var, u + 1)
                nc.scalar.activation(var_ps, var_ps, ACT.Ln, bias=c.eps[:]).then_inc(ln.log, 1)
                act.wait_ge(ln.log, u + 1)
                nc.scalar.activation(var_ps, var_ps, ACT.Exp, scale=-0.5).then_inc(ln.rstd, 1)

            def sigmoid(u):
                act.wait_ge(z_clamped, u + 1)
                nc.scalar.activation(ez[:], ez[:], ACT.Ln).then_inc(z_log, 1)
                act.wait_ge(z_log, u + 1)
                nc.scalar.activation(ez[:], ez[:], ACT.Exp, scale=-1.0).then_inc(z_sig, 1)

            def decays(b, p, h):
                act.wait_ge(diag_ready, NH * b + h + 1)
                act.wait_ge(m_ready, NH * b + h + 1)
                for j in range(NT):
                    n1 = cq[p][:, 1, j, h:h + 1]
                    last = nc.scalar.activation(e[h % 2][:, OFF[j]:OFF[j] + P], diag[h % 2][:, P * j:P * j + P], ACT.Exp, bias=n1)
                    if j < NT - 1:
                        last = nc.scalar.activation(e[h % 2][:, OFF[j] + P:OFF[j] + WID[j]], n_ps[h % 2][:, P * (j + 1):],
                                                    ACT.Exp, scale=-1.0, bias=n1)
                last.then_inc(e_ready, 1)

            def copy_cb(u, p):
                for j in range(NT):
                    act.wait_ge(cb_ready, NT * u + j + 1)
                    last = nc.scalar.activation(cbs[p][:, OFF[j]:OFF[j] + WID[j]], cb_ps[j][:, 0:WID[j]], ACT.Copy)
                last.then_inc(cb_copied, 1)

            def copy_y(b):
                act.wait_ge(ygt_ready, b + 1)
                for f in range(2):
                    last = nc.scalar.activation(ygt[:, f], y_ps[f], ACT.Copy)
                last.then_inc(ygt_copied, 1)

            def front(u, p):
                copy_bc(u)
                for j in range(NT):
                    copy_zx(u, p, j)
                square(u)
                inverse_deviation(u)
                sigmoid(u)
                decays(u, p, 0)
                copy_cb(u, p)
                decays(u, p, 1)

            def cycle(b, p, more):
                u, n = b + 1, 1 - p
                if more:
                    copy_bc(u)
                    copy_zx(u, n, 0)
                    copy_zx(u, n, 1)
                decays(b, p, 2)
                if more:
                    square(u)
                    copy_zx(u, n, 2)
                    copy_zx(u, n, 3)
                    inverse_deviation(u)
                decays(b, p, 3)
                if more:
                    sigmoid(u)
                    decays(u, n, 0)
                    copy_cb(u, n)
                copy_y(b)
                if more:
                    decays(u, n, 1)

            over_batches(act, front, cycle)

        @block.vector
        def _(dve):
            dve.wait_ge(loaded, 16 * N_LOADS)
            dve.sem_inc(done, 1)
            dve.sem_inc(e_ready, 2)

            def coefficients(u, p):
                nc.vector.tensor_scalar(cq[p][:], cols[:, :, :, bass.ds(NH * u, NH)], 1.0, None, ALU.mult).then_inc(cq_ready, 1)

            def centre(u):
                dve.wait_ge(ln.mean, u + 1)
                nc.vector.tensor_tensor(cent[:], bc[:], mean_ps, ALU.subtract).then_inc(ln.cent, 1)

            def clamp(u):
                dve.wait_ge(zx_copied, NT * u + NT)
                nc.vector.tensor_scalar(ez[:], ez[:], 1e18, 1.0, ALU.min, ALU.add).then_inc(z_clamped, 1)

            def scale_bc(u):
                dve.wait_ge(ln.rstd, u + 1)
                nc.vector.tensor_tensor(v0[:], cent[:], var_ps, ALU.mult).then_inc(ln.out, 1)
                dve.wait_ge(ln.out, u + 1)
                nc.vector.tensor_scalar(v[:], v0[:], vec[:, 0:1], vec[:, 1:2], ALU.mult, ALU.add).then_inc(v_ready, 1)
                dve.wait_ge(v_ready, u + 1)
                nc.vector.tensor_tensor(t1[:], v[:], cos[:, u], ALU.mult)

            def rotate(u):
                dve.wait_ge(swapped, u + 1)
                nc.vector.tensor_tensor(t2[:], sin[:, u], swap_ps, ALU.mult).then_inc(turned, 1)
                dve.wait_ge(turned, u + 1)
                nc.vector.tensor_tensor(brot[:], t1[0:DS], t2[0:DS], ALU.add)
                nc.vector.tensor_tensor(crot[:], t1[DS:P], t2[DS:P], ALU.add).then_inc(rotated, 1)

            def weigh_x(u, p):
                dve.wait_ge(cq_ready, u + 1)
                scale = cq[p][:, 0].rearrange("p j h -> p (j h)").unsqueeze(2).to_broadcast([P, NT * NH, DS])
                nc.vector.tensor_tensor(by_head(xc[p][:]), by_head(xt[p][:]), scale, ALU.mult).then_inc(xc_ready, 1)

            def diagonals(b, h):
                dve.wait_ge(n_ready, NH * b + h + 1)
                dve.wait_ge(e_ready, NH * b + h + 1)
                nc.vector.scalar_tensor_tensor(out=diag[h % 2][:], in0=n_ps[h % 2], scalar=-1.0,
                                               in1=later[:].rearrange("p j t -> p (j t)"),
                                               op0=ALU.mult, op1=ALU.add).then_inc(diag_ready, 1)

            def own_token(u, p):
                dve.wait_ge(cb_copied, u + 1)
                for j in range(NT):
                    last = nc.vector.tensor_tensor(cbw[:, j], c.ident[:], cbs[p][:, OFF[j]:OFF[j] + P], ALU.mult)
                last.then_inc(cbw_ready, 1)
                dve.wait_ge(cbw_ready, u + 1)
                nc.vector.tensor_reduce(cb[:], cbw[:], AX_X, ALU.add).then_inc(cb_diag, 1)
                dve.wait_ge(cb_diag, u + 1)
                nc.vector.tensor_tensor(dcoef[p][:], cq[p][:, 2], cb[:].unsqueeze(2).to_broadcast([P, NT, NH]), ALU.mult).then_inc(dc_part, 1)
                dve.wait_ge(dc_part, u + 1)
                nc.vector.tensor_tensor(dcoef[p][:], dcoef[p][:], d_rep[:], ALU.add).then_inc(dc_ready, 1)

            def gated_y(b, p):
                dve.wait_ge(dc_ready, b + 1)
                nc.vector.tensor_tensor(by_head(y1[:]), by_head(xt[p][:]),
                                        dcoef[p][:].rearrange("p j h -> p (j h)").unsqueeze(2).to_broadcast([P, NT * NH, DS]),
                                        ALU.mult).then_inc(y_part, 1)
                dve.wait_ge(y_part, b + 1)
                dve.wait_ge(weighed, NH * b + NH + 2)
                for f in range(2):
                    last = nc.vector.tensor_tensor(y1[:, 2 * f:2 * f + 2], y1[:, 2 * f:2 * f + 2],
                                                   y_ps[f].rearrange("p (j e) -> p j e", j=2), ALU.add)
                last.then_inc(y_sum, 1)
                dve.wait_ge(y_sum, b + 1)
                dve.wait_ge(zs_ready, b + 1)
                nc.vector.tensor_tensor(y1[:], y1[:], zs[p][:], ALU.mult).then_inc(yg_ready, 1)

            def add(b):
                dve.wait_ge(o_ready, b + 1)
                nc.vector.tensor_tensor(c.resid[:, b], c.resid[:, b], y_ps[0], ALU.add).then_inc(done, 1)

            def front(u, p):
                coefficients(u, p)
                centre(u)
                clamp(u)
                scale_bc(u)
                rotate(u)
                weigh_x(u, p)
                diagonals(u, 0)
                diagonals(u, 1)
                own_token(u, p)

            def cycle(b, p, more):
                u, n = b + 1, 1 - p
                if more:
                    coefficients(u, n)
                    centre(u)
                diagonals(b, 2)
                if more:
                    clamp(u)
                diagonals(b, 3)
                if more:
                    scale_bc(u)
                    rotate(u)
                    weigh_x(u, n)
                    diagonals(u, 0)
                gated_y(b, p)
                if more:
                    diagonals(u, 1)
                    own_token(u, n)
                add(b)

            over_batches(dve, front, cycle)


def phase_state_space(c, d):
    with ExitStack() as ctx:
        ph = Phase(c, ctx)
        dt, ncs = ph.sb("ss_dt", [NR, T]), ph.sb("ss_ncs", [NR, T])
        cols = ph.sb("ss_cols", [P, 3, NT, NR])
        cos, sin = ph.sb("ss_cos", [P, NB, T]), ph.sb("ss_sin", [P, NB, T])
        with ExitStack() as inner:
            state_space_rows(c, d, Phase(c, inner), dt, ncs, cols)
        with ExitStack() as inner:
            state_space_angles(c, d, Phase(c, inner), dt, cos, sin)
        with ExitStack() as inner:
            state_space_outputs(c, d, Phase(c, inner), ncs, cols, cos, sin)
    phase_norm(c, "ss_norm")


DEPTH = 2
LH = 8
LD = 64
INNER = LH * LD
HID = 341
HC = [(0, 128), (128, 128), (256, HID - 256)]
UNITS = 2 * NT
KW = LD + P
NORM_SCALE = 2.0 ** 20


def head_of(half, slot):
    return 4 * half + 2 * (slot % 2) + slot // 2


class LocalWeights:
    def __init__(self, ph):
        self.qk = ph.sb("l_wqk", [P, 2, INNER])
        self.qk_half = ph.sb("l_wqk_half", [P, 2, INNER])
        self.v = ph.sb("l_wv", [P, INNER])
        self.o = ph.sb("l_wo", [P, NT, P])
        self.w1 = ph.sb("l_w1", [P, 2 * HID])
        self.w2 = ph.sb("l_w2", [P, 3, P])
        self.vec = ph.sb("l_vec", [P, 13])


def local_attention(c, d, ph, w, l, tab, tables, masks, identb, kf, qf):
    nc = c.nc
    s = ph.s
    bank = c.bank
    hx, sq, rinv, th, tsum, v, vh, p, ptb, pta, maxraw, negmax, psum, prec, o, ot, ssm, ssq, rq8, rq = (ph.b[n] for n in (
        "hx", "sq", "rinv", "th", "tsum", "v", "vh", "p", "ptb", "pta", "maxraw", "negmax", "psum", "prec", "o", "ot",
        "ssm", "ssq", "rq8", "rq"))
    score = [bank[0:2], bank[2:4]]
    v_bank = [bank[4], bank[7]]
    k_ss_bank = bank[5]
    q_ss_bank = bank[6][0:LH, :]
    rq_bank = bank[6][:, 0:NT * LH]
    N_LOADS = 7
    ones_blk, ones_row = ph.b["ones_blk"], ph.b["ones_row"]

    def n_of(b):
        return l * NB + b + 1

    def over_batches(engine, front, attention):
        front(n_of(0))
        with engine.Fori(0, NB - 1) as b:
            attention(n_of(b), b, True)
        attention(n_of(NB - 1), NB - 1, False)

    with nc.Block() as block:
        @block.sync
        def _(sp):
            for dst, name in ((w.qk, "l_wqk"), (w.qk_half, "l_wqk_half"), (w.v, "l_wv"), (w.o, "l_wo"),
                              (w.w1, "l_w1"), (w.w2, "l_w2"), (w.vec, "l_vec")):
                sp.dma_start(dst[:], d[name][l]).then_inc(s["w_here"], 16)
            with sp.Fori(0, NB) as b:
                sp.wait_ge(s["hx_used"], n_of(b))
                sp.dma_start(hx[0:LD, :], c.resid[0:LD, b]).then_inc(s["hx_here"], 16)
                sp.dma_start(hx[LD:P, 1:T], c.resid[LD:P, b, 0:T - 1]).then_inc(s["hx_here"], 16)

        @block.gpsimd
        def _(pool):
            with pool.Fori(0, NB) as b:
                for m in range(8):
                    g = (n_of(b) - 1) * 8 + m
                    pool.wait_ge(s["halves"], g + 1 + 2)
                    if m % 2 == 0:
                        nc.gpsimd.tensor_tensor(qf[:, m // 2], th[0][:, 0], th[0][:, 1], ALU.add).then_inc(s["qk_done"], 1)
                    else:
                        gk = (n_of(b) - 1) * 4 + m // 2
                        nc.gpsimd.tensor_tensor(tsum[m // 2 % 2][:], th[1][:, 0], th[1][:, 1], ALU.add).then_inc(s["k_summed"], 1)
                        pool.wait_ge(s["rinv"], gk + 1)
                        pool.wait_ge(s["k_summed"], gk + 1)
                        nc.gpsimd.tensor_tensor(kf[:, m // 2], tsum[m // 2 % 2][:], rinv[m // 2 % 2][:], ALU.mult).then_inc(s["qk_done"], 1)

        @block.tensor
        def _(pe):
            def project(n, m):
                q, mm = m % 2, m // 2
                pe.wait_ge(s["halves"], 8 * (n - 1) + m - 1 + 2)
                cols = slice(P * mm, P * mm + P)
                nc.tensor.matmul(bank[2 * q], w.qk[:, q, cols], hx[:], start=True, stop=True)
                nc.tensor.matmul(bank[2 * q + 1], w.qk_half[:, q, cols], hx[:], start=True, stop=True).then_inc(s["projected"], 1)

            def norms(n, m):
                pe.wait_ge(s["squared"], 8 * (n - 1) + m + 1)
                if m % 2:
                    pe.wait_ge(s["k_ss_read"], 4 * (n - 1) + m // 2 + 1)
                    nc.tensor.matmul(k_ss_bank, ones_blk[:], sq[m % 3][:], start=True, stop=True).then_inc(s["k_ss"], 1)
                else:
                    nc.tensor.matmul(q_ss_bank, ones_row[:, m // 2], sq[m % 3][:], start=(m == 0), stop=(m == 6)).then_inc(s["q_ss"], 1)

            def turn_q_norms(n):
                for j in range(NT):
                    last = nc.tensor.transpose(rq_bank[:, LH * j:LH * j + LH], rq8[:, P * j:P * j + P], c.ident[0:LH, 0:LH])
                last.then_inc(s["rq_turned"], 1)

            def values(n, j, after_batch):
                if j == 1 and after_batch:
                    pe.wait_ge(s["added"], n - 1)
                if j >= 2:
                    pe.wait_ge(s["v_copied"], NT * (n - 1) + j - 1)
                nc.tensor.matmul(v_bank[j % 2], hx[:, P * j:P * j + P], w.v[:], start=True, stop=True).then_inc(s["v_ready"], 1)

            def front_end(n, after_batch):
                for m in range(4, 8):
                    project(n, m)
                    norms(n, m - 1)
                norms(n, 7)
                values(n, 0, after_batch)
                values(n, 1, after_batch)
                pe.wait_ge(s["rq_rows"], n)
                values(n, 2, after_batch)
                turn_q_norms(n)
                values(n, 3, after_batch)

            def front(n):
                pe.wait_ge(s["w_here"], 16 * N_LOADS * (l + 1))
                pe.wait_ge(s["hx_here"], 32 * n)
                for m in range(4):
                    project(n, m)
                    if m:
                        norms(n, m - 1)
                front_end(n, False)

            def attention(n, b, more):
                def scores(u):
                    j, hg = divmod(u, 2)
                    lo = LD if j == 0 else 0
                    if u < 2:
                        pe.wait_ge(s["qk_done"], 8 * (n - 1) + 4 + 4 * u)
                    for e in range(2):
                        for k in range(2):
                            nc.tensor.matmul(score[u % 2][k][:, 256 * e + lo:256 * e + KW], identb[:], masks[:, lo:KW],
                                             start=True, stop=False)
                        for k in range(2):
                            h = head_of(hg, 2 * k + e)
                            rows = slice(LD * (h % 2), LD * (h % 2) + LD)
                            last = nc.tensor.matmul(score[u % 2][k][:, 256 * e + lo:256 * e + KW],
                                                    qf[rows, h // 2, P * j:P * j + P],
                                                    kf[rows, h // 2, P * j - LD + lo:P * j + P], start=False, stop=True)
                    last.then_inc(s["scored"], 1)

                def turn(u):
                    j = u // 2
                    pe.wait_ge(s["exped"], UNITS * (n - 1) + u + 1)
                    for hh in range(4):
                        last = nc.tensor.transpose(bank[4][:, P * hh:P * hh + P], p[u % 2][:, hh, LD:KW], c.ident[:])
                    if j:
                        for hh in range(4):
                            last = nc.tensor.transpose(bank[5][0:LD, P * hh:P * hh + P], p[u % 2][:, hh, 0:LD], c.ident[:])
                    last.then_inc(s["p_turned"], 1)

                def weigh(u):
                    j, hg = divmod(u, 2)
                    pe.wait_ge(s["ptb_copied"], UNITS * (n - 1) + u + 1)
                    pe.wait_ge(s["pta_copied"], UNITS * (n - 1) + u + 1)
                    for hh in range(4):
                        at = slice(LD * head_of(hg, hh), LD * head_of(hg, hh) + LD)
                        if j:
                            nc.tensor.matmul(bank[6][:, at], pta[u % 2][:, P * hh:P * hh + P], vh[:, j, at], start=True, stop=False)
                        last = nc.tensor.matmul(bank[6][:, at], ptb[u % 2][:, P * hh:P * hh + P], v[:, j, at], start=(j == 0), stop=True)
                    last.then_inc(s["weighed"], 1)

                def turn_out(j):
                    pe.wait_ge(s["o_normed"], NT * (n - 1) + j + 1)
                    if j:
                        pe.wait_ge(s["ot_copied"], NT * (n - 1) + j)
                    for m in range(NT):
                        last = nc.tensor.transpose(bank[7][:, P * m:P * m + P], o[:, P * m:P * m + P], c.ident[:])
                    last.then_inc(s["o_turned"], 1)

                def project_out():
                    pe.wait_ge(s["ot_copied"], NT * n)
                    for m in range(NT):
                        last = nc.tensor.matmul(bank[7], w.o[:, m], ot[:, m], start=(m == 0), stop=(m == NT - 1))
                    last.then_inc(s["o_ready"], 1)

                scores(0)
                scores(1)
                pe.wait_ge(s["v_copied"], NT * n)
                pe.sem_inc(s["hx_used"], 1)
                for u in range(UNITS - 1):
                    turn(u)
                    if u + 2 < UNITS:
                        scores(u + 2)
                    if u % 2 == 0 and u:
                        turn_out(u // 2 - 1)
                    weigh(u)
                if more:
                    pe.wait_ge(s["hx_here"], 32 * n + 32)
                    project(n + 1, 0)
                turn(UNITS - 1)
                if more:
                    project(n + 1, 1)
                weigh(UNITS - 1)
                if more:
                    project(n + 1, 2)
                    norms(n + 1, 1)
                turn_out(NT - 1)
                if more:
                    norms(n + 1, 0)
                    project(n + 1, 3)
                    norms(n + 1, 2)
                project_out()
                if more:
                    front_end(n + 1, True)

            over_batches(pe, front, attention)

        @block.scalar
        def _(act):
            nc.scalar.preload_act_table_set(LN_EXP)

            def square(n, m):
                act.wait_ge(s["projected"], 8 * (n - 1) + m + 1)
                if m >= 3:
                    act.wait_ge(s["q_ss" if m % 2 else "k_ss"], 4 * (n - 1) + (m - 3) // 2 + 1)
                nc.scalar.activation(sq[m % 3][:], bank[2 * (m % 2)], ACT.Square).then_inc(s["squared"], 1)

            def k_inverse_norm(n, mm):
                g = 4 * (n - 1) + mm
                act.wait_ge(s["k_ss_read"], g + 1 + 1)
                if mm >= 2:
                    act.wait_ge(s["qk_done"], 8 * (n - 1) + 2 * mm - 2)
                nc.scalar.activation(rinv[mm % 2][:], ssm[mm % 2][:], ACT.Ln, scale=NORM_SCALE).then_inc(s["ss_log"], 1)
                act.wait_ge(s["ss_log"], g + 1)
                nc.scalar.activation(rinv[mm % 2][:], rinv[mm % 2][:], ACT.Exp, scale=-0.5).then_inc(s["rinv"], 1)

            def q_inverse_norms(n):
                act.wait_ge(s["q_ss_read"], n)
                nc.scalar.activation(rq8[:], ssq[:], ACT.Ln, scale=NORM_SCALE).then_inc(s["q_ss_log"], 1)
                act.wait_ge(s["q_ss_log"], n)
                nc.scalar.activation(rq8[:], rq8[:], ACT.Exp, scale=-0.5).then_inc(s["rq_rows"], 1)

            def copy_v(n, j):
                act.wait_ge(s["v_ready"], NT * (n - 1) + j + 1)
                last = nc.scalar.activation(v[:, j], v_bank[j % 2], ACT.Copy)
                if j + 1 < NT:
                    last = nc.scalar.activation(vh[:, j + 1], v_bank[j % 2][LD:P, :], ACT.Copy)
                last.then_inc(s["v_copied"], 1)

            def front_end(n):
                for m in range(4, 8):
                    square(n, m)
                    if m % 2 == 0:
                        k_inverse_norm(n, m // 2 - 1)
                q_inverse_norms(n)
                copy_v(n, 0)
                k_inverse_norm(n, 3)
                for j in range(1, NT):
                    copy_v(n, j)

            def front(n):
                for m in range(3):
                    square(n, m)
                k_inverse_norm(n, 0)
                square(n, 3)
                front_end(n)

            def attention(n, b, more):
                def exps(u):
                    j = u // 2
                    lo = LD if j == 0 else 0
                    act.wait_ge(s["negmax"], UNITS * (n - 1) + u + 1)
                    for hh in range(4):
                        ps = score[u % 2][hh // 2][:, 256 * (hh % 2) + lo:256 * (hh % 2) + KW]
                        at = 4 * (u % 2) + hh
                        last = nc.scalar.activation(p[u % 2][:, hh, lo:KW], ps, ACT.Exp, bias=negmax[u % 2][:, hh:hh + 1],
                                                    scale=rq[:, j, at:at + 1],
                                                    accum_out=psum[:, j % 2, head_of(u % 2, hh):head_of(u % 2, hh) + 1])
                    last.then_inc(s["exped"], 1)

                def copy_a(u):
                    act.wait_ge(s["p_turned"], UNITS * (n - 1) + u + 1)
                    if u >= 2:
                        nc.scalar.activation(pta[u % 2][:], bank[5][0:LD, :], ACT.Copy).then_inc(s["pta_copied"], 1)
                    else:
                        act.sem_inc(s["pta_copied"], 1)

                exps(0)
                for u in range(UNITS - 1):
                    exps(u + 1)
                    copy_a(u)
                if more:
                    square(n + 1, 0)
                copy_a(UNITS - 1)
                if more:
                    square(n + 1, 1)
                    square(n + 1, 2)
                    k_inverse_norm(n + 1, 0)
                    square(n + 1, 3)
                    front_end(n + 1)

            over_batches(act, front, attention)

        @block.vector
        def _(dve):
            dve.wait_ge(s["w_here"], 16 * N_LOADS * (l + 1))
            for k in range(4):
                nc.vector.tensor_scalar(tab[:, k], tables[:, k], w.vec[:, k:k + 1], (8.0 if k < 2 else 1.0) * NORM_SCALE ** 0.5,
                                        ALU.mult, ALU.mult).then_inc(s["tables_done"], 1)
            dve.wait_ge(s["tables_done"], 4 * (l + 1))

            def halves(n, m):
                q = m % 2
                g = 8 * (n - 1) + m
                dve.wait_ge(s["squared"], g + 1)
                if m >= 2:
                    if q:
                        dve.wait_ge(s["k_summed"], 4 * (n - 1) + m // 2)
                    else:
                        dve.wait_ge(s["qk_done"], g - 1)
                nc.vector.tensor_tensor(th[q][:, 0], bank[2 * q], tab[:, 2 * q], ALU.mult)
                nc.vector.tensor_tensor(th[q][:, 1], bank[2 * q + 1], tab[:, 2 * q + 1], ALU.mult).then_inc(s["halves"], 1)

            def read_k_norm(n, mm):
                dve.wait_ge(s["k_ss"], 4 * (n - 1) + mm + 1)
                if mm >= 2:
                    dve.wait_ge(s["ss_log"], 4 * (n - 1) + mm - 1)
                nc.vector.tensor_scalar(ssm[mm % 2][:], k_ss_bank, 1e-24, None, ALU.max).then_inc(s["k_ss_read"], 1)

            def front_end(n):
                for m in range(4, 8):
                    halves(n, m)
                    if m % 2 == 0:
                        read_k_norm(n, m // 2 - 1)
                dve.wait_ge(s["q_ss"], 4 * n)
                nc.vector.tensor_scalar(ssq[:], q_ss_bank, 1e-24, None, ALU.max).then_inc(s["q_ss_read"], 1)
                read_k_norm(n, 3)
                dve.wait_ge(s["rq_turned"], n)
                nc.vector.tensor_scalar(rq[:], rq_bank.rearrange("p (j h) -> p j h", j=NT), 1.0, None, ALU.mult).then_inc(s["rq"], 1)

            def front(n):
                for m in range(3):
                    halves(n, m)
                read_k_norm(n, 0)
                halves(n, 3)
                front_end(n)

            def attention(n, b, more):
                def maxima(u):
                    j, hg = divmod(u, 2)
                    lo = LD if u < 2 else 0
                    if u == 0:
                        dve.wait_ge(s["rq"], n)
                    dve.wait_ge(s["scored"], UNITS * (n - 1) + u + 1)
                    for k in range(2):
                        ps = score[u % 2][k].rearrange("p (e t) -> p e t", e=2)[:, :, lo:KW]
                        last = nc.vector.tensor_reduce(maxraw[u % 2][:, 2 * k:2 * k + 2], ps, AX_X, ALU.max, negate=True)
                    last.then_inc(s["maxraw"], 1)
                    dve.wait_ge(s["maxraw"], UNITS * (n - 1) + u + 1)
                    nc.vector.tensor_tensor(negmax[u % 2][:], maxraw[u % 2][:], rq[:, j, 4 * hg:4 * hg + 4], ALU.mult).then_inc(s["negmax"], 1)

                def copy_b(u):
                    dve.wait_ge(s["p_turned"], UNITS * (n - 1) + u + 1)
                    nc.vector.tensor_scalar(ptb[u % 2][:], bank[4], 1.0, None, ALU.mult).then_inc(s["ptb_copied"], 1)

                def normalise(j):
                    dve.wait_ge(s["exped"], UNITS * (n - 1) + 2 * j + 2)
                    nc.vector.reciprocal(prec[:], psum[:, j % 2]).then_inc(s["prec"], 1)
                    dve.wait_ge(s["prec"], NT * (n - 1) + j + 1)
                    dve.wait_ge(s["weighed"], UNITS * (n - 1) + 2 * j + 2)
                    nc.vector.tensor_tensor(o[:].rearrange("p (h e) -> p h e", e=LD), bank[6].rearrange("p (h e) -> p h e", e=LD),
                                            prec[:].unsqueeze(2).to_broadcast([P, LH, LD]), ALU.mult).then_inc(s["o_normed"], 1)

                def copy_ot(j):
                    dve.wait_ge(s["o_turned"], NT * (n - 1) + j + 1)
                    nc.vector.tensor_scalar(ot[:, :, P * j:P * j + P], bank[7].rearrange("p (m t) -> p m t", m=NT),
                                            1.0, None, ALU.mult).then_inc(s["ot_copied"], 1)

                def add():
                    dve.wait_ge(s["o_ready"], n)
                    nc.vector.tensor_tensor(c.resid[:, b], c.resid[:, b], bank[7], ALU.add).then_inc(s["added"], 1)

                maxima(0)
                maxima(1)
                for u in range(UNITS - 1):
                    copy_b(u)
                    if u + 2 < UNITS:
                        maxima(u + 2)
                    if u % 2 == 0 and u:
                        copy_ot(u // 2 - 1)
                    if u % 2:
                        normalise(u // 2)
                if more:
                    halves(n + 1, 0)
                copy_b(UNITS - 1)
                if more:
                    halves(n + 1, 1)
                normalise(NT - 1)
                if more:
                    halves(n + 1, 2)
                    read_k_norm(n + 1, 0)
                copy_ot(NT - 1)
                if more:
                    halves(n + 1, 3)
                add()
                if more:
                    front_end(n + 1)

            over_batches(dve, front, attention)


def local_norm(c, ph, w, l):
    nc = c.nc
    s = ph.s
    y, cent, sq = ph.b["ny"], ph.b["th"], ph.b["sq"]
    norms = ph.norms
    with nc.Block() as block:
        @block.sync
        def _(sp):
            with sp.Fori(0, NB // 2) as i:
                for p in range(2):
                    n = l * (NB // 2) + i
                    b = 2 * i + p
                    sp.wait_ge(norms[p].cent, n + 1)
                    sp.dma_start(y[p][0:LD, :], c.resid[0:LD, b]).then_inc(norms[p].y, 16)
                    sp.dma_start(y[p][LD:P, 1:T], c.resid[LD:P, b, 0:T - 1]).then_inc(norms[p].y, 16)

        @block.tensor
        def _(pe):
            with pe.Fori(0, NB // 2) as i:
                n = l * (NB // 2) + i + 1
                for p in range(2):
                    pe.wait_ge(norms[p].y, 32 * n)
                    nc.tensor.matmul(c.bank[p][:], c.ones[:], y[p][:], start=True, stop=True).then_inc(norms[p].mean, 1)
                for p in range(2):
                    pe.wait_ge(norms[p].sq, n)
                    pe.wait_ge(norms[p].out, n)
                    nc.tensor.matmul(c.bank[2 + p][:], c.ones[:], sq[p][:], start=True, stop=True).then_inc(norms[p].var, 1)

        @block.scalar
        def _(act):
            nc.scalar.preload_act_table_set(LN_EXP)
            with act.Fori(0, NB // 2) as i:
                n = l * (NB // 2) + i + 1
                for p in range(2):
                    act.wait_ge(norms[p].cent, n + 1)
                    nc.scalar.activation(sq[p][:], cent[p][:, 0], ACT.Square).then_inc(norms[p].sq, 1)
                for p in range(2):
                    var = c.bank[2 + p]
                    act.wait_ge(norms[p].var, n)
                    nc.scalar.activation(var[:], var[:], ACT.Ln, bias=c.eps[:]).then_inc(norms[p].log, 1)
                    act.wait_ge(norms[p].log, n)
                    nc.scalar.activation(var[:], var[:], ACT.Exp, scale=-0.5).then_inc(norms[p].rstd, 1)

        @block.vector
        def _(dve):
            with dve.Fori(0, NB // 2) as i:
                n = l * (NB // 2) + i + 1
                for p in range(2):
                    dve.wait_ge(norms[p].mean, n)
                    nc.vector.tensor_tensor(cent[p][:, 0], y[p][:], c.bank[p][:], ALU.subtract).then_inc(norms[p].cent, 1)
                for p in range(2):
                    dve.wait_ge(norms[p].rstd, n)
                    nc.vector.tensor_tensor(cent[p][:, 1], cent[p][:, 0], c.bank[2 + p][:], ALU.mult).then_inc(norms[p].out, 1)
                for p in range(2):
                    dve.wait_ge(norms[p].out, n + 1)
                    nc.vector.tensor_scalar(c.normed[:, 2 * i + p], cent[p][:, 1], w.vec[:, 4:5], w.vec[:, 5:6], ALU.mult, ALU.add)


def local_feed_forward(c, ph, w, l):
    nc = c.nc
    s = ph.s
    gel, hid = ph.b["gel"], ph.b["hid"]
    a_ps, g_ps, o_ps = (c.bank[0], c.bank[1]), (c.bank[2], c.bank[3]), (c.bank[4], c.bank[5])
    STEPS = 6

    with nc.Block() as block:
        @block.tensor
        def _(pe):
            with pe.Fori(0, NB // 2) as i:
                pair = l * (NB // 2) + i

                def up(k):
                    bb, ch = divmod(k, 3)
                    at, rows = HC[ch]
                    x = c.normed[:, 2 * i + bb]
                    pe.wait_ge(s["gated"], STEPS * pair + k - 1 + 2)
                    nc.tensor.matmul(a_ps[k % 2][0:rows, :], w.w1[:, at:at + rows], x, start=True, stop=True)
                    nc.tensor.matmul(g_ps[k % 2][0:rows, :], w.w1[:, HID + at:HID + at + rows], x, start=True, stop=True).then_inc(s["up"], 1)

                def down(k):
                    bb, ch = divmod(k, 3)
                    rows = HC[ch][1]
                    pe.wait_ge(s["gated"], STEPS * pair + k + 1 + 2)
                    if ch == 0:
                        pe.wait_ge(s["f_added"], 2 * pair + bb + 1)
                    last = nc.tensor.matmul(o_ps[bb][:], w.w2[0:rows, ch], hid[k % 3][0:rows, :], start=(ch == 0), stop=(ch == 2))
                    if ch == 2:
                        last.then_inc(s["down"], 1)

                for k in range(STEPS):
                    up(k)
                    if k:
                        down(k - 1)
                down(STEPS - 1)

        @block.scalar
        def _(act):
            with act.Fori(0, NB // 2) as i:
                for k in range(STEPS):
                    ch = k % 3
                    rows = HC[ch][1]
                    act.wait_ge(s["up"], STEPS * (l * (NB // 2) + i) + k + 1)
                    nc.scalar.activation(gel[k % 2][0:rows, :], g_ps[k % 2][0:rows, :], ACT.Gelu,
                                         bias=w.vec[0:rows, 9 + ch:10 + ch]).then_inc(s["gelu"], 1)

        @block.vector
        def _(dve):
            with dve.Fori(0, NB // 2) as i:
                pair = l * (NB // 2) + i

                def add(bb):
                    dve.wait_ge(s["down"], 2 * pair + bb + 1)
                    x = c.resid[:, 2 * i + bb]
                    nc.vector.scalar_tensor_tensor(out=x, in0=o_ps[bb][:], scalar=w.vec[:, 12:13], in1=x,
                                                   op0=ALU.add, op1=ALU.add).then_inc(s["f_added"], 1)

                for k in range(STEPS):
                    ch = k % 3
                    rows = HC[ch][1]
                    dve.wait_ge(s["gelu"], STEPS * pair + k + 1)
                    nc.vector.scalar_tensor_tensor(out=hid[k % 3][0:rows, :], in0=a_ps[k % 2][0:rows, :],
                                                   scalar=w.vec[0:rows, 6 + ch:7 + ch], in1=gel[k % 2][0:rows, :],
                                                   op0=ALU.add, op1=ALU.mult).then_inc(s["gated"], 1)
                    if k == 3:
                        add(0)
                add(1)


def phase_local(c, d):
    nc = c.nc
    with ExitStack() as ctx:
        ph = Phase(c, ctx)
        w = LocalWeights(ph)
        tables = ph.sb("l_tables", [P, 4, T])
        tab = ph.sb("l_tab", [P, 4, T])
        masks = ph.sb("l_masks", [P, KW], BF16)
        identb = ph.sb("l_identb", [P, P], BF16)
        qf, kf = ph.sb("l_q", [P, NT, T]), ph.sb("l_k", [P, NT, T])
        ph.b = dict(
            hx=ph.sb("l_hx", [P, T]), ones_blk=ph.sb("l_ones_blk", [P, P]), ones_row=ph.sb("l_ones_row", [P, NT, LH]),
            ssq=ph.sb("l_ssq", [LH, T]), rq8=ph.sb("l_rq8", [LH, T]), rq=ph.sb("l_rq", [P, NT, LH]), maxraw=[ph.sb(f"l_maxraw{k}", [P, 4]) for k in range(2)],
            sq=[ph.sb(f"l_sq{k}", [P, T]) for k in range(3)], rinv=[ph.sb(f"l_rinv{k}", [P, T]) for k in range(2)],
            ssm=[ph.sb(f"l_ssm{k}", [P, T]) for k in range(2)],
            th=[ph.sb(f"l_th{k}", [P, 2, T]) for k in range(2)], tsum=[ph.sb(f"l_tsum{k}", [P, T]) for k in range(2)],
            v=ph.sb("l_v", [P, NT, INNER]), vh=ph.sb("l_vh", [LD, NT, INNER]),
            p=[ph.sb(f"l_p{k}", [P, 4, KW]) for k in range(2)], ptb=[ph.sb(f"l_ptb{k}", [P, 4 * P]) for k in range(2)],
            pta=[ph.sb(f"l_pta{k}", [LD, 4 * P]) for k in range(2)], negmax=[ph.sb(f"l_negmax{k}", [P, 4]) for k in range(2)],
            psum=ph.sb("l_psum", [P, 2, LH]), prec=ph.sb("l_prec", [P, LH]), o=ph.sb("l_o", [P, INNER]),
            ot=ph.sb("l_ot", [P, NT, T]), ny=[ph.sb(f"l_ny{k}", [P, T]) for k in range(2)],
            gel=[ph.sb(f"l_gel{k}", [P, T]) for k in range(2)], hid=[ph.sb(f"l_hid{k}", [P, T]) for k in range(3)])
        ph.s = {n: ph.sem(f"p5_{n}") for n in (
            "loaded", "w_here", "hx_here", "hx_used", "tables_done", "v_ready", "v_copied", "projected", "squared",
            "k_ss", "k_ss_read", "q_ss", "q_ss_read", "ss_log", "rinv", "q_ss_log", "rq_rows", "rq_turned", "rq", "halves", "k_summed", "qk_done",
            "scored", "maxraw", "negmax", "exped", "p_turned", "ptb_copied",
            "pta_copied", "weighed", "prec", "o_normed", "o_turned", "ot_copied", "o_ready", "added",
            "up", "gelu", "gated", "down", "f_added")}
        ph.norms = [NormSems(ph.sem, f"p5n{p}") for p in range(2)]
        s = ph.s
        with nc.Block() as block:
            @block.sync
            def _(sp):
                for dst, name in ((tables, "l_tables"), (masks, "l_masks"), (identb, "l_identb"), (ph.b["ones_blk"], "l_ones_blk"),
                                  (ph.b["ones_row"], "l_ones_row")):
                    sp.dma_start(dst[:], d[name]).then_inc(s["loaded"], 16)
                sp.wait_ge(s["loaded"], 80)

            @block.gpsimd
            def _(pool):
                nc.gpsimd.memset(ph.b["hx"][:], 0.0)
                nc.gpsimd.memset(ph.b["ny"][0][:], 0.0)
                nc.gpsimd.memset(ph.b["ny"][1][:], 0.0)

            @block.vector
            def _(dve):
                dve.sem_inc(s["hx_used"], 1)
                dve.sem_inc(s["halves"], 2)
                dve.sem_inc(s["k_ss_read"], 1)
                dve.sem_inc(s["gated"], 2)
                dve.sem_inc(s["f_added"], 2)
                for p in range(2):
                    dve.sem_inc(ph.norms[p].cent, 1)
                    dve.sem_inc(ph.norms[p].out, 1)

        with nc.Fori(0, DEPTH) as l:
            local_attention(c, d, ph, w, l, tab, tables, masks, identb, kf, qf)
            local_norm(c, ph, w, l)
            local_feed_forward(c, ph, w, l)


def phase_local_attention(c, d):
    nc = c.nc
    with ExitStack() as ctx:
        with nc.Block() as block:
            @block.gpsimd
            def _(pool):
                nc.gpsimd.tensor_copy(c.outer[:], c.resid[:])
        phase_local(c, d)
        with nc.Block() as block:
            @block.vector
            def _(dve):
                for b in range(NB):
                    nc.vector.tensor_tensor(c.resid[:, b], c.resid[:, b], c.outer[:, b], ALU.add)
    phase_norm(c, "last_norm")


def in_slots(w):
    heads = w.reshape(P, 4, 2, 2, 8).transpose(1, 2, 0, 3, 4)
    out = np.zeros((4, 2, P, 2, HR), w.dtype)
    for s in range(len(Q_PART)):
        out[..., SLOT * s:SLOT * s + 8] = heads
    return out.reshape(4, 2, P, P)


def lay_out(i):
    d = {}
    d["x"] = i["L0_attn_x"].transpose(0, 2, 1)
    w_in = i["L0_attn_w_in"].reshape(16, 3, 8, P)
    b_in = i["L0_attn_b_in"].reshape(16, 3, 8)
    d["wv0"] = w_in[:, 2].reshape(P, P).T
    d["bv0"] = b_in[:, 2].reshape(P, 1)
    d["wo0"] = i["L0_attn_w_out"].T
    d["bo0"] = i["L0_attn_b_out"].reshape(P, 1)
    d["ln1_g"] = i["L0_ffn_ln1_g"].reshape(P, 1)
    d["ln1_b"] = i["L0_ffn_ln1_b"].reshape(P, 1)
    d["ident"] = np.eye(P, dtype=np.float32)
    wp = i["L0_ffn_wp"]
    swapped = np.concatenate([wp[64:], wp[:64]], axis=0)
    flat = lambda a: a.transpose(0, 2, 1, 3).reshape(4, P, 2 * P)
    wv = i["L0_ffn_wv"].reshape(P, 4, 32).transpose(1, 0, 2)
    d["rel_w"] = np.concatenate([flat(in_slots(i["L0_ffn_wq"])), flat(in_slots(i["L0_ffn_wk"])), wv], axis=2)
    ab = np.stack([in_slots(wp), in_slots(swapped)], axis=2)
    d["rel_wp"] = ab.transpose(4, 0, 1, 2, 3).reshape(P, 4, 4 * P)
    wo = np.zeros((4, 4, 32, P), np.float32)
    for part in range(3):
        wo[:, :, SLOT * part:SLOT * part + 8] = i["L0_ffn_wo"].reshape(4, 4, 8, P)
    d["rel_wo"] = wo.reshape(4, P, P)
    freq = (1.0 / 10000.0 ** (np.arange(0, P, 2, dtype=np.float32) / np.float32(P))).astype(np.float32)
    angle = freq.astype(np.float64)[:, None] * np.arange(T)[None, :]
    sin, cos = np.sin(angle).astype(np.float32), np.cos(angle).astype(np.float32)
    d["rel_cos"] = np.concatenate([cos, cos])
    d["rel_sin"] = np.concatenate([sin, -sin])
    d["rel_angle"] = np.concatenate([sin, cos])
    part_vec = np.zeros((2, HR, 5), np.float32)
    for s, (qp, kp) in enumerate(zip(Q_PART, K_PART)):
        rows = slice(SLOT * s, SLOT * s + 8)
        part_vec[:, rows, 0] = -float(qp > 0)
        part_vec[:, rows, 1] = -float(qp > 1)
        part_vec[:, rows, 2] = -float(kp > 0)
        part_vec[:, rows, 3] = -float(kp > 1)
        if s < 3:
            part_vec[:, SLOT * s + 8, 2] = 1.0
            part_vec[:, SLOT * s + 8, 4] = 1.0
    d["rel_part_vec"] = part_vec.reshape(P, 5)
    pick = np.zeros((4, 32, 4, 32), np.float32)
    for r in range(4):
        pick[r, 8, r, :] = 1.0
    d["rel_pick_sum"] = pick.reshape(P, P)
    v_aug = np.zeros((P, NT, 4, 32), mybir.dt.np(BF16))
    v_aug[..., 8] = 1.0
    d["rel_v_aug"] = v_aug
    d["ln2_g"] = i["L0_ffn_ln2_g"].reshape(P, 1)
    d["ln2_b"] = i["L0_ffn_ln2_b"].reshape(P, 1)
    d["sel_w"] = i["L0_ffn_sel_w"]
    d["keys"] = i["L0_ffn_keys"]
    d["values"] = i["L0_ffn_values"]
    pick_expert = np.zeros((NE, 3, NE, P), mybir.dt.np(BF16))
    for e in range(NE):
        pick_expert[e, :, e] = 1.0
    d["pick_expert"] = pick_expert.reshape(NE, 3 * NE, P)
    w = i["L1_attn_W_in"]
    at = np.cumsum([0, DI, DI, DS, DS, NH, NH, NH, DS // 2])
    z, x, bp, cp, dd_dt, dd_a, trap, ang = (w[:, at[n]:at[n + 1]] for n in range(8))
    w_rows = np.zeros((P, 3, NB, NB, NH), np.float32)
    for q, part in enumerate((dd_dt, dd_a, trap)):
        for b in range(NB):
            w_rows[:, q, b, b] = part
    d["ss_w_rows"] = w_rows.reshape(P, 3, NB, NR)
    d["ss_dt_bias"] = np.tile(i["L1_attn_dt_bias"], NB).reshape(NR, 1)
    d["ss_w_angle"] = np.tile(ang, (1, 4))
    pairs = lambda a: np.concatenate([a[..., 0::2], a[..., 1::2]], axis=-1)
    d["ss_w_bc"] = np.concatenate([pairs(bp), pairs(cp)], axis=1)
    d["ss_gain"] = np.concatenate([pairs(i["L1_attn_Bn_g"]), pairs(i["L1_attn_Cn_g"])]).reshape(P, 1)
    d["ss_shift"] = np.concatenate([pairs(i["L1_attn_Bn_b"]), pairs(i["L1_attn_Cn_b"])]).reshape(P, 1)
    d["ss_w_zx"] = np.concatenate([z, x], axis=1)
    d["ss_w_out"] = i["L1_attn_W_out"].reshape(2, P, P).transpose(1, 0, 2)
    d["ss_d"] = np.broadcast_to(i["L1_attn_D_param"], (P, NT, NH))
    sign = np.ones((4, 32), np.float32)
    sign[0::2] = -1.0
    d["ss_sign"] = sign.reshape(P, 1)
    pick = np.zeros((NB, NB, NH, NH + 1, P), np.float32)
    for b in range(NB):
        for h in range(NH):
            pick[b, b, h, h] = 1.0
        pick[b, b, :, NH] = 1.0 / NH
    d["ss_pick"] = pick.reshape(NB, NR, (NH + 1) * P)
    d["ones64"] = np.kron(np.eye(2, dtype=np.float32), np.full((DS, DS), 1.0 / DS, np.float32))
    swap = np.zeros((P, P), np.float32)
    swap[np.arange(P) ^ 32, np.arange(P)] = 1.0
    d["ss_swap"] = swap
    d["ss_later"] = np.where(np.arange(P)[None, :] > np.arange(P)[:, None], 0.0, NEG).astype(np.float32)
    w = i["L1_ffn_wqkv"]
    halves = lambda a: a.reshape(DEPTH, -1, LH, 2, LD // 2)[:, :, :, ::-1].reshape(DEPTH, -1, INNER)
    d["l_wqk"] = w[:, :, 0:2 * INNER].reshape(DEPTH, P, 2, INNER)
    d["l_wqk_half"] = np.stack([halves(w[:, :, 0:INNER]), halves(w[:, :, INNER:2 * INNER])], axis=2)
    d["l_wv"] = w[:, :, 2 * INNER:]
    d["l_wo"] = i["L1_ffn_wo"].reshape(DEPTH, NT, P, P).transpose(0, 2, 1, 3)
    d["l_w1"] = i["L1_ffn_w1"]
    w2 = np.zeros((DEPTH, 3 * P, P), np.float32)
    w2[:, 0:HID] = i["L1_ffn_w2"]
    d["l_w2"] = w2.reshape(DEPTH, 3, P, P).transpose(0, 2, 1, 3)
    vec = np.zeros((DEPTH, P, 13), np.float32)
    for k, g in enumerate((i["L1_ffn_q_scale"], i["L1_ffn_k_scale"])):
        vec[:, :, 2 * k] = np.tile(g, (1, 2))
        vec[:, :, 2 * k + 1] = np.tile(np.roll(g, LD // 2, axis=1), (1, 2))
    vec[:, :, 4] = i["L1_ffn_ln_g"]
    vec[:, :, 5] = i["L1_ffn_ln_b"]
    for ch, (at, rows) in enumerate(HC):
        vec[:, 0:rows, 6 + ch] = i["L1_ffn_b1"][:, at:at + rows]
        vec[:, 0:rows, 9 + ch] = i["L1_ffn_b1"][:, HID + at:HID + at + rows]
    vec[:, :, 12] = i["L1_ffn_b2"]
    d["l_vec"] = vec
    half = np.arange(0, LD, 2, dtype=np.float32)
    freq = (1.0 / 10000.0 ** (half / np.float32(LD))).astype(np.float32).astype(np.float64)
    t = np.arange(T, dtype=np.float64)
    base = (half.astype(np.float64) + 0.4 * LD) / (1.4 * LD)
    scale = base[:, None] ** ((t[None, :] - T // 2) / (LD // 2))
    cos, sin = np.cos(freq[:, None] * t), np.sin(freq[:, None] * t)
    tables = np.zeros((P, 4, T), np.float32)
    for k, f in enumerate((scale, 1.0 / scale)):
        tables[:, 2 * k] = np.tile(cos * f, (4, 1))
        tables[:, 2 * k + 1] = np.concatenate([-sin * f, sin * f, -sin * f, sin * f])
    d["l_tables"] = tables
    col, row = np.arange(KW)[None, :], np.arange(P)[:, None]
    d["l_masks"] = np.where((col >= row) & (col <= row + LD), 0.0, NEG).astype(mybir.dt.np(BF16))
    d["l_identb"] = np.eye(P).astype(mybir.dt.np(BF16))
    d["l_ones_blk"] = np.kron(np.eye(2, dtype=np.float32), np.ones((LD, LD), np.float32))
    row = np.zeros((P, NT, LH), np.float32)
    for g in range(2):
        for slot in range(4):
            h = head_of(g, slot)
            row[LD * (h % 2):LD * (h % 2) + LD, h // 2, 4 * g + slot] = 1.0
    d["l_ones_row"] = row
    return d



def build(nc, d, out):
    with ExitStack() as ctx:
        c = Core(nc, ctx)
        phase_first_attention(c, d)
        phase_relative_attention(c, d)
        phase_experts(c, d)
        phase_state_space(c, d)
        phase_local_attention(c, d)
        store(c, out)


def store(c, out):
    nc = c.nc
    with ExitStack() as ctx:
        stored = Phase(c, ctx).sem("stored")
        with nc.Block() as block:
            @block.sync
            def _(sp):
                sp.dma_start(out.rearrange("b p t -> p b t"), c.resid[:]).then_inc(stored, 16)
                sp.wait_ge(stored, 16)


def kernel(**inputs):
    import numpy as _np
    import concourse.bacc as _bacc
    from concourse import mybir as _mybir
    from concourse.bass_utils import run_bass_kernel_spmd as _run

    arrays = lay_out({k: _np.asarray(v) for k, v in inputs.items()})
    nc = _bacc.Bacc("TRN2", target_bir_lowering=False, num_devices=1)
    feeds, d = {}, {}
    for name, a in arrays.items():
        a = _np.ascontiguousarray(a)
        feeds[f"in_{name}"] = a
        d[name] = nc.dram_tensor(f"in_{name}", a.shape, _mybir.dt.from_np(a.dtype), kind="ExternalInput").ap()
    out = nc.dram_tensor("out_0", (NB, P, T), F32, kind="ExternalOutput").ap()
    build(nc, d, out)
    r = _run(nc, [feeds], core_ids=[0])
    return _np.ascontiguousarray(r.results[0]["out_0"].transpose(0, 2, 1))
```
